# Optimizing a Trainium2 kernel written in Bass

```python
import numpy as np
import jax
import jax.numpy as jnp

def _softmax(x, axis=-1):
    return jax.nn.softmax(x, axis=axis)

def _gelu(x):
    return jax.nn.gelu(x, approximate=True)

def _silu(x):
    return jax.nn.silu(x)

def _sigmoid(x):
    return jax.nn.sigmoid(x)

def _layernorm(x, axis=-1, eps=1e-05):
    m = jnp.mean(x, axis=axis, keepdims=True)
    v = jnp.var(x, axis=axis, keepdims=True)
    return (x - m) / jnp.sqrt(v + eps)

def _scatter_add(tgt, idx, src, axis=0):
    return tgt.at[idx].add(src)

def _segment_sum(src, seg, n):
    return jax.ops.segment_sum(src, seg, n)
kernel_name = 'mk_perceiver_d2_seqx_r4_ca456f'

def setup_inputs(seed: int=0):
    np.random.seed(seed)
    _w = jnp.asarray

    def _rec_inputs():
        import jax
        import jax.numpy as jnp
        _rk = jax.random.key(seed)
        x = 0.0002279 + 0.9999 * jax.random.normal(jax.random.fold_in(_rk, 1), (2, 64, 256), jnp.float32)
        _lenS = 64 - jax.random.randint(jax.random.fold_in(_rk, 7), (2,), 0, max(1, 64 // 4) + 1, jnp.int32)
        _lenS2 = 1024 - jax.random.randint(jax.random.fold_in(_rk, 8), (2,), 0, max(1, 1024 // 4) + 1, jnp.int32)
        _ctx_1024P = jax.random.normal(jax.random.fold_in(_rk, 11), (2, 16, 256), jnp.float32)
        _ctx_1024c = jax.random.dirichlet(jax.random.fold_in(_rk, 511), 0.3 * jnp.ones((16,), jnp.float32), (2, 1024))
        _ctx_1024t = jnp.einsum('bsk,bkd->bsd', _ctx_1024c, _ctx_1024P)
        _ctx_1024t = _ctx_1024t * jax.lax.rsqrt(jnp.mean(jnp.square(_ctx_1024t)) + 1e-12) * 0.953939
        ctx_1024 = 7.22013e-05 + 1.00017 * (_ctx_1024t + 0.3 * jax.random.normal(jax.random.fold_in(_rk, 611), (2, 1024, 256), jnp.float32))
        return (x, ctx_1024)
    x, ctx_1024 = _rec_inputs()

    def _L0_xattn_setup():
        import jax, jax.numpy as jnp
        import numpy as np
        HIDDEN = 256
        H = 16
        HK = 4
        G = H // HK
        D = 64
        EPS = 1e-06

        def rmsnorm(x, w):
            var = jnp.mean(jnp.square(x), axis=-1, keepdims=True)
            return x * jax.lax.rsqrt(var + EPS) * w
        key = jax.random.key(seed)
        ks = jax.random.split(key, 8)
        B, S_KV, S_Q = (2, 1024, 128)
        inputs = jax.random.normal(ks[0], (B, S_KV, HIDDEN), dtype=jnp.float32)
        latent = jax.random.normal(ks[1], (B, S_Q, HIDDEN), dtype=jnp.float32)

        def xavier(k, shape, gain=1.0):
            fan_out, fan_in = shape
            limit = gain * np.sqrt(6.0 / (fan_in + fan_out))
            return jax.random.uniform(k, shape, jnp.float32, -limit, limit)
        wq = xavier(ks[2], (H * D, HIDDEN))
        wk = xavier(ks[3], (HK * D, HIDDEN))
        wv = xavier(ks[4], (HK * D, HIDDEN))
        wo = xavier(ks[5], (HIDDEN, H * D), gain=1.0 / np.sqrt(2.0))
        q_norm_w = jnp.ones((D,), jnp.float32)
        k_norm_w = jnp.ones((D,), jnp.float32)
        return {'inputs': inputs, 'latent': latent, 'wq': wq, 'wk': wk, 'wv': wv, 'wo': wo, 'q_norm_w': q_norm_w, 'k_norm_w': k_norm_w}
    _L0_xattn_all = _L0_xattn_setup()
    _L0_xattn_in = {k: v for k, v in _L0_xattn_all.items() if k in ('wq', 'wk', 'wv', 'wo', 'q_norm_w', 'k_norm_w')}
    del _L0_xattn_all

    def _L0_attn_setup():
        import jax, jax.numpy as jnp
        import numpy as np
        EPS = 1e-06

        def _rmsnorm(z, w):
            zf = z.astype(jnp.float32)
            zn = zf * jax.lax.rsqrt(jnp.mean(zf * zf, axis=-1, keepdims=True) + EPS)
            return zn.astype(z.dtype) * w
        key = jax.random.key(seed)
        ks = jax.random.split(key, 6)
        B, T, D, H = (4, 1024, 256, 512)
        x = jax.random.normal(ks[0], (B, T, D), dtype=jnp.float32)
        input_norm_w = jnp.ones((D,), dtype=jnp.float32)
        a_log = jax.random.normal(ks[1], (D,), dtype=jnp.float32) * 0.5
        c_out = jax.random.normal(ks[2], (D,), dtype=jnp.float32)
        d_skip = jax.random.normal(ks[3], (D,), dtype=jnp.float32)
        ff_norm_w = jnp.ones((D,), dtype=jnp.float32)
        ff_fc_w = jax.random.normal(ks[4], (H, D), dtype=jnp.float32) * 0.02
        ff_proj_w = jax.random.normal(ks[5], (D, H), dtype=jnp.float32) * 0.02
        return {'x': x, 'input_norm_w': input_norm_w, 'a_log': a_log, 'c_out': c_out, 'd_skip': d_skip, 'ff_norm_w': ff_norm_w, 'ff_fc_w': ff_fc_w, 'ff_proj_w': ff_proj_w}
    _L0_attn_all = _L0_attn_setup()
    _L0_attn_in = {k: v for k, v in _L0_attn_all.items() if k in ('input_norm_w', 'a_log', 'c_out', 'd_skip', 'ff_norm_w', 'ff_fc_w', 'ff_proj_w')}
    del _L0_attn_all

    def _L0_ffn_setup():
        import jax, jax.numpy as jnp
        import numpy as np
        D_MODEL = 256
        D_FF = 1024
        N_EXPERTS = 8
        TOP_K = 2
        D_FF_PER = D_FF // N_EXPERTS
        B, T = (4, 512)
        key = jax.random.key(seed)
        ks = jax.random.split(key, 7)
        b1_bound = 1.0 / np.sqrt(D_MODEL)
        b2_bound = 1.0 / np.sqrt(D_FF_PER)
        return {'x': jax.random.normal(ks[0], (B, T, D_MODEL), dtype=jnp.float32), 'router_w': jax.random.uniform(ks[1], (D_MODEL, N_EXPERTS), minval=-b1_bound, maxval=b1_bound, dtype=jnp.float32), 'router_b': jax.random.uniform(ks[2], (N_EXPERTS,), minval=-b1_bound, maxval=b1_bound, dtype=jnp.float32), 'W1': jax.random.uniform(ks[3], (N_EXPERTS, D_MODEL, D_FF_PER), minval=-b1_bound, maxval=b1_bound, dtype=jnp.float32), 'b1': jax.random.uniform(ks[4], (N_EXPERTS, D_FF_PER), minval=-b1_bound, maxval=b1_bound, dtype=jnp.float32), 'W2': jax.random.uniform(ks[5], (N_EXPERTS, D_FF_PER, D_MODEL), minval=-b2_bound, maxval=b2_bound, dtype=jnp.float32), 'b2': jax.random.uniform(ks[6], (N_EXPERTS, D_MODEL), minval=-b2_bound, maxval=b2_bound, dtype=jnp.float32)}
    _L0_ffn_all = _L0_ffn_setup()
    _L0_ffn_in = {k: v for k, v in _L0_ffn_all.items() if k in ('router_w', 'router_b', 'W1', 'b1', 'W2', 'b2')}
    del _L0_ffn_all

    def _L1_xattn_setup():
        import jax, jax.numpy as jnp
        import numpy as np
        D_MODEL = 256
        N_HEADS = 16
        D_K = D_MODEL // N_HEADS
        B, S = (2, 512)
        key = jax.random.key(seed)
        ks = jax.random.split(key, 11)
        s = 1.0 / np.sqrt(D_MODEL)
        return {'q': jax.random.normal(ks[0], (B, S, D_MODEL), jnp.float32), 'k': jax.random.normal(ks[1], (B, S, D_MODEL), jnp.float32), 'v': jax.random.normal(ks[2], (B, S, D_MODEL), jnp.float32), 'Wq': jax.random.normal(ks[3], (D_MODEL, D_MODEL), jnp.float32) * s, 'bq': jnp.zeros((D_MODEL,), jnp.float32), 'Wk': jax.random.normal(ks[4], (D_MODEL, D_MODEL), jnp.float32) * s, 'bk': jnp.zeros((D_MODEL,), jnp.float32), 'Wv': jax.random.normal(ks[5], (D_MODEL, D_MODEL), jnp.float32) * s, 'bv': jnp.zeros((D_MODEL,), jnp.float32), 'Wo': jax.random.normal(ks[6], (D_MODEL, D_MODEL), jnp.float32) * s, 'bo': jnp.zeros((D_MODEL,), jnp.float32)}
    _L1_xattn_all = _L1_xattn_setup()
    _L1_xattn_in = {k: v for k, v in _L1_xattn_all.items() if k in ('Wq', 'bq', 'Wk', 'bk', 'Wv', 'bv', 'Wo', 'bo')}
    del _L1_xattn_all

    def _L1_attn_setup():
        import jax, jax.numpy as jnp
        import numpy as np
        BASE_THETA = 0.5
        K_DOP = 0.2
        K_NOR = 0.15
        K_SERO = 0.1
        DIM = 256
        key = jax.random.key(seed)
        ks = jax.random.split(key, 9)
        scale = 1.0 / np.sqrt(DIM)
        x = jax.random.normal(ks[0], (2, 512, DIM), dtype=jnp.float32)
        Wq = jax.random.normal(ks[1], (DIM, DIM), dtype=jnp.float32) * scale
        bq = jnp.zeros((DIM,), dtype=jnp.float32)
        Wk = jax.random.normal(ks[2], (DIM, DIM), dtype=jnp.float32) * scale
        bk = jnp.zeros((DIM,), dtype=jnp.float32)
        Wv = jax.random.normal(ks[3], (DIM, DIM), dtype=jnp.float32) * scale
        bv = jnp.zeros((DIM,), dtype=jnp.float32)
        Wo = jax.random.normal(ks[4], (DIM, DIM), dtype=jnp.float32) * scale
        bo = jnp.zeros((DIM,), dtype=jnp.float32)
        return {'x': x, 'Wq': Wq, 'bq': bq, 'Wk': Wk, 'bk': bk, 'Wv': Wv, 'bv': bv, 'Wo': Wo, 'bo': bo}
    _L1_attn_all = _L1_attn_setup()
    _L1_attn_in = {k: v for k, v in _L1_attn_all.items() if k in ('Wq', 'bq', 'Wk', 'bk', 'Wv', 'bv', 'Wo', 'bo')}
    del _L1_attn_all

    def _L1_ffn_setup():
        import jax, jax.numpy as jnp
        import numpy as np
        B, S, D = (2, 512, 256)
        I = 128
        E = 16
        TOP_K = 2

        def _mlp(x, wg, wu, wd):
            return jnp.einsum('bsi,id->bsd', jax.nn.silu(x @ wg) * (x @ wu), wd)
        key = jax.random.key(seed)
        ks = jax.random.split(key, 10)
        sc_d = 1.0 / np.sqrt(D)
        sc_i = 1.0 / np.sqrt(I)
        return {'x': jax.random.normal(ks[0], (B, S, D), dtype=jnp.float32), 'gate_w': jax.random.normal(ks[1], (D, E), dtype=jnp.float32) * sc_d, 'gate_b': jnp.zeros((E,), dtype=jnp.float32), 'shared_wg': jax.random.normal(ks[2], (D, I), dtype=jnp.float32) * sc_d, 'shared_wu': jax.random.normal(ks[3], (D, I), dtype=jnp.float32) * sc_d, 'shared_wd': jax.random.normal(ks[4], (I, D), dtype=jnp.float32) * sc_i, 'experts_wg': jax.random.normal(ks[5], (E, D, I), dtype=jnp.float32) * sc_d, 'experts_wu': jax.random.normal(ks[6], (E, D, I), dtype=jnp.float32) * sc_d, 'experts_wd': jax.random.normal(ks[7], (E, I, D), dtype=jnp.float32) * sc_i}
    _L1_ffn_all = _L1_ffn_setup()
    _L1_ffn_in = {k: v for k, v in _L1_ffn_all.items() if k in ('gate_w', 'gate_b', 'shared_wg', 'shared_wu', 'shared_wd', 'experts_wg', 'experts_wu', 'experts_wd')}
    del _L1_ffn_all
    return {'x': x, 'ctx_1024': ctx_1024, 'L0_xattn_wq': _L0_xattn_in['wq'], 'L0_xattn_wk': _L0_xattn_in['wk'], 'L0_xattn_wv': _L0_xattn_in['wv'], 'L0_xattn_wo': _L0_xattn_in['wo'], 'L0_xattn_q_norm_w': _L0_xattn_in['q_norm_w'], 'L0_xattn_k_norm_w': _L0_xattn_in['k_norm_w'], 'L0_attn_input_norm_w': _L0_attn_in['input_norm_w'], 'L0_attn_a_log': _L0_attn_in['a_log'], 'L0_attn_c_out': _L0_attn_in['c_out'], 'L0_attn_d_skip': _L0_attn_in['d_skip'], 'L0_attn_ff_norm_w': _L0_attn_in['ff_norm_w'], 'L0_attn_ff_fc_w': _L0_attn_in['ff_fc_w'], 'L0_attn_ff_proj_w': _L0_attn_in['ff_proj_w'], 'L0_ffn_router_w': _L0_ffn_in['router_w'], 'L0_ffn_router_b': _L0_ffn_in['router_b'], 'L0_ffn_W1': _L0_ffn_in['W1'], 'L0_ffn_b1': _L0_ffn_in['b1'], 'L0_ffn_W2': _L0_ffn_in['W2'], 'L0_ffn_b2': _L0_ffn_in['b2'], 'L1_xattn_Wq': _L1_xattn_in['Wq'], 'L1_xattn_bq': _L1_xattn_in['bq'], 'L1_xattn_Wk': _L1_xattn_in['Wk'], 'L1_xattn_bk': _L1_xattn_in['bk'], 'L1_xattn_Wv': _L1_xattn_in['Wv'], 'L1_xattn_bv': _L1_xattn_in['bv'], 'L1_xattn_Wo': _L1_xattn_in['Wo'], 'L1_xattn_bo': _L1_xattn_in['bo'], 'L1_attn_Wq': _L1_attn_in['Wq'], 'L1_attn_bq': _L1_attn_in['bq'], 'L1_attn_Wk': _L1_attn_in['Wk'], 'L1_attn_bk': _L1_attn_in['bk'], 'L1_attn_Wv': _L1_attn_in['Wv'], 'L1_attn_bv': _L1_attn_in['bv'], 'L1_attn_Wo': _L1_attn_in['Wo'], 'L1_attn_bo': _L1_attn_in['bo'], 'L1_ffn_gate_w': _L1_ffn_in['gate_w'], 'L1_ffn_gate_b': _L1_ffn_in['gate_b'], 'L1_ffn_shared_wg': _L1_ffn_in['shared_wg'], 'L1_ffn_shared_wu': _L1_ffn_in['shared_wu'], 'L1_ffn_shared_wd': _L1_ffn_in['shared_wd'], 'L1_ffn_experts_wg': _L1_ffn_in['experts_wg'], 'L1_ffn_experts_wu': _L1_ffn_in['experts_wu'], 'L1_ffn_experts_wd': _L1_ffn_in['experts_wd']}

def reference(x, ctx_1024, L0_xattn_wq, L0_xattn_wk, L0_xattn_wv, L0_xattn_wo, L0_xattn_q_norm_w, L0_xattn_k_norm_w, L0_attn_input_norm_w, L0_attn_a_log, L0_attn_c_out, L0_attn_d_skip, L0_attn_ff_norm_w, L0_attn_ff_fc_w, L0_attn_ff_proj_w, L0_ffn_router_w, L0_ffn_router_b, L0_ffn_W1, L0_ffn_b1, L0_ffn_W2, L0_ffn_b2, L1_xattn_Wq, L1_xattn_bq, L1_xattn_Wk, L1_xattn_bk, L1_xattn_Wv, L1_xattn_bv, L1_xattn_Wo, L1_xattn_bo, L1_attn_Wq, L1_attn_bq, L1_attn_Wk, L1_attn_bk, L1_attn_Wv, L1_attn_bv, L1_attn_Wo, L1_attn_bo, L1_ffn_gate_w, L1_ffn_gate_b, L1_ffn_shared_wg, L1_ffn_shared_wu, L1_ffn_shared_wd, L1_ffn_experts_wg, L1_ffn_experts_wu, L1_ffn_experts_wd):
    import jax
    import jax.numpy as jnp

    def _L0_xattn_ref(inputs, latent, wq, wk, wv, wo, q_norm_w, k_norm_w):
        import jax, jax.numpy as jnp
        import numpy as np
        HIDDEN = 256
        H = 16
        HK = 4
        G = H // HK
        D = 64
        EPS = 1e-06

        def rmsnorm(x, w):
            var = jnp.mean(jnp.square(x), axis=-1, keepdims=True)
            return x * jax.lax.rsqrt(var + EPS) * w
        B, S_q, _ = latent.shape
        S_kv = inputs.shape[1]
        q = (latent @ wq.T).reshape(B, S_q, H, D)
        k = (inputs @ wk.T).reshape(B, S_kv, HK, D)
        v = (inputs @ wv.T).reshape(B, S_kv, HK, D)
        q = rmsnorm(q, q_norm_w)
        k = rmsnorm(k, k_norm_w)
        q = q.transpose(0, 2, 1, 3).reshape(B, HK, G, S_q, D)
        k = k.transpose(0, 2, 1, 3)
        v = v.transpose(0, 2, 1, 3)
        scores = jnp.einsum('bkgqd,bksd->bkgqs', q, k)
        attn = jax.nn.softmax(scores.astype(jnp.float32), axis=-1).astype(q.dtype)
        out = jnp.einsum('bkgqs,bksd->bkgqd', attn, v)
        out = out.reshape(B, H, S_q, D).transpose(0, 2, 1, 3).reshape(B, S_q, H * D)
        return out @ wo.T

    def _L0_attn_ref(x, input_norm_w, a_log, c_out, d_skip, ff_norm_w, ff_fc_w, ff_proj_w):
        import jax, jax.numpy as jnp
        import numpy as np
        EPS = 1e-06

        def _rmsnorm(z, w):
            zf = z.astype(jnp.float32)
            zn = zf * jax.lax.rsqrt(jnp.mean(zf * zf, axis=-1, keepdims=True) + EPS)
            return zn.astype(z.dtype) * w
        normed = _rmsnorm(x, input_norm_w)
        a = jnp.exp(-jnp.exp(a_log))
        A = jnp.broadcast_to(a, normed.shape)

        def combine(e1, e2):
            a1, b1 = e1
            a2, b2 = e2
            return (a1 * a2, a2 * b1 + b2)
        _, h = jax.lax.associative_scan(combine, (A, normed), axis=1)
        scan_out = h * c_out + normed * d_skip
        x1 = x + scan_out
        n2 = _rmsnorm(x1, ff_norm_w)
        hidden = jax.nn.silu(jnp.einsum('btd,hd->bth', n2, ff_fc_w))
        ff_out = jnp.einsum('bth,dh->btd', hidden, ff_proj_w)
        return x1 + ff_out

    def _L0_ffn_ref(x, router_w, router_b, W1, b1, W2, b2):
        import jax, jax.numpy as jnp
        import numpy as np
        D_MODEL = 256
        D_FF = 1024
        N_EXPERTS = 8
        TOP_K = 2
        D_FF_PER = D_FF // N_EXPERTS
        B, T = (4, 512)
        router_logits = x @ router_w + router_b
        routing_weights = jax.nn.softmax(router_logits, axis=-1)
        top_k_weights, top_k_indices = jax.lax.top_k(routing_weights, TOP_K)
        top_k_weights = top_k_weights / jnp.sum(top_k_weights, axis=-1, keepdims=True)
        routing_mask = jnp.zeros_like(routing_weights)
        routing_mask = jnp.take_along_axis(routing_mask, top_k_indices, axis=-1)
        b_idx = jnp.arange(x.shape[0])[:, None, None]
        t_idx = jnp.arange(x.shape[1])[None, :, None]
        routing_mask = jnp.zeros_like(routing_weights).at[b_idx, t_idx, top_k_indices].set(top_k_weights)
        h1 = jnp.einsum('btd,nde->btne', x, W1) + b1
        h1 = jax.nn.gelu(h1, approximate=False)
        out_per_expert = jnp.einsum('btne,nef->btnf', h1, W2) + b2
        output = jnp.sum(out_per_expert * routing_mask[..., None], axis=-2)
        return output

    def _L1_xattn_ref(q, k, v, Wq, bq, Wk, bk, Wv, bv, Wo, bo):
        import jax, jax.numpy as jnp
        import numpy as np
        D_MODEL = 256
        N_HEADS = 16
        D_K = D_MODEL // N_HEADS
        B, S = (2, 512)
        b = q.shape[0]

        def proj(x, W, bias):
            y = jnp.einsum('bsd,ed->bse', x, W) + bias
            return y.reshape(b, -1, N_HEADS, D_K).transpose(0, 2, 1, 3)
        qh, kh, vh = (proj(q, Wq, bq), proj(k, Wk, bk), proj(v, Wv, bv))
        scores = jnp.einsum('bhqd,bhkd->bhqk', qh, kh) / np.sqrt(D_K)
        attn = jax.nn.softmax(scores, axis=-1)
        x = jnp.einsum('bhqk,bhkd->bhqd', attn, vh)
        x = x.transpose(0, 2, 1, 3).reshape(b, -1, D_MODEL)
        return jnp.einsum('bsd,ed->bse', x, Wo) + bo

    def _L1_attn_ref(x, Wq, bq, Wk, bk, Wv, bv, Wo, bo):
        import jax, jax.numpy as jnp
        import numpy as np
        BASE_THETA = 0.5
        K_DOP = 0.2
        K_NOR = 0.15
        K_SERO = 0.1
        DIM = 256
        q = jnp.einsum('bsd,ed->bse', x, Wq) + bq
        k = jnp.einsum('bsd,ed->bse', x, Wk) + bk
        v = jnp.einsum('bsd,ed->bse', x, Wv) + bv
        qk = jnp.einsum('bsd,btd->bst', q, k)
        theta = BASE_THETA + K_DOP * jax.nn.sigmoid(qk) + K_NOR * jnp.tanh(qk) + K_SERO * jax.nn.relu(qk)
        attn = jax.nn.softmax(theta, axis=-1)
        out = jnp.einsum('bst,btd->bsd', attn, v)
        return jnp.einsum('bsd,ed->bse', out, Wo) + bo

    def _L1_ffn_ref(x, gate_w, gate_b, shared_wg, shared_wu, shared_wd, experts_wg, experts_wu, experts_wd):
        import jax, jax.numpy as jnp
        import numpy as np
        B, S, D = (2, 512, 256)
        I = 128
        E = 16
        TOP_K = 2

        def _mlp(x, wg, wu, wd):
            return jnp.einsum('bsi,id->bsd', jax.nn.silu(x @ wg) * (x @ wu), wd)
        router_logits = jax.nn.sigmoid(x @ gate_w + gate_b)
        expert_values, expert_indices = jax.lax.top_k(router_logits, k=TOP_K)
        expert_values = expert_values / jnp.sum(expert_values, axis=-1, keepdims=True)
        hg = jnp.einsum('bsd,edi->bsei', x, experts_wg)
        hu = jnp.einsum('bsd,edi->bsei', x, experts_wu)
        all_outputs = jnp.einsum('bsei,eid->bsed', jax.nn.silu(hg) * hu, experts_wd)
        selected = jnp.take_along_axis(all_outputs, expert_indices[..., None], axis=2)
        expert_weighted = jnp.sum(expert_values[..., None] * selected, axis=2)
        return x + _mlp(x, shared_wg, shared_wu, shared_wd) + expert_weighted
    x = x + _L0_xattn_ref(ctx_1024, _layernorm(x, axis=-1), L0_xattn_wq, L0_xattn_wk, L0_xattn_wv, L0_xattn_wo, L0_xattn_q_norm_w, L0_xattn_k_norm_w)
    x = x + _L0_attn_ref(_layernorm(x, axis=-1), L0_attn_input_norm_w, L0_attn_a_log, L0_attn_c_out, L0_attn_d_skip, L0_attn_ff_norm_w, L0_attn_ff_fc_w, L0_attn_ff_proj_w)
    x = x + _L0_ffn_ref(_layernorm(x, axis=-1), L0_ffn_router_w, L0_ffn_router_b, L0_ffn_W1, L0_ffn_b1, L0_ffn_W2, L0_ffn_b2)
    x = x + _L1_xattn_ref(_layernorm(x, axis=-1), ctx_1024, ctx_1024, L1_xattn_Wq, L1_xattn_bq, L1_xattn_Wk, L1_xattn_bk, L1_xattn_Wv, L1_xattn_bv, L1_xattn_Wo, L1_xattn_bo)
    x = x + _L1_attn_ref(_layernorm(x, axis=-1), L1_attn_Wq, L1_attn_bq, L1_attn_Wk, L1_attn_bk, L1_attn_Wv, L1_attn_bv, L1_attn_Wo, L1_attn_bo)
    x = x + _L1_ffn_ref(_layernorm(x, axis=-1), L1_ffn_gate_w, L1_ffn_gate_b, L1_ffn_shared_wg, L1_ffn_shared_wu, L1_ffn_shared_wd, L1_ffn_experts_wg, L1_ffn_experts_wu, L1_ffn_experts_wd)
    return x

_drawn_inputs = setup_inputs


def setup_inputs(seed=0):
    import zlib

    import numpy as np

    out = dict(_drawn_inputs(seed))
    spreads = {'L0_xattn_q_norm_w': (1.0, 0.2),
     'L0_xattn_k_norm_w': (1.0, 0.2),
     'L0_attn_input_norm_w': (1.0, 0.2),
     'L0_attn_ff_norm_w': (1.0, 0.6),
     'L1_xattn_bq': (0.0, 0.8),
     'L1_xattn_bk': (0.0, 2.0),
     'L1_xattn_bv': (0.0, 0.1),
     'L1_xattn_bo': (0.0, 0.1),
     'L1_attn_bq': (0.0, 0.67),
     'L1_attn_bk': (0.0, 2.0),
     'L1_attn_bv': (0.0, 0.1),
     'L1_attn_bo': (0.0, 0.1),
     'L1_ffn_gate_b': (0.0, 0.1)}
    factors = {'L0_ffn_router_b': 5.961, 'L0_ffn_b1': 8.0, 'L0_ffn_b2': 3.19}
    for name, (base, spread) in spreads.items():
        noise = np.random.default_rng([zlib.crc32(name.encode()), seed]).standard_normal(out[name].shape)
        drawn = base * np.exp(spread * noise) if base else spread * noise
        out[name] = jnp.asarray(drawn.astype(out[name].dtype))
    for name, factor in factors.items():
        out[name] = (out[name] * factor).astype(out[name].dtype)
    return out
```

```python
from contextlib import ExitStack

import numpy as np

import concourse.bass as bass
from concourse import mybir

ALU = mybir.AluOpType
ACT = mybir.ActivationFunctionType
AX = mybir.AxisListType
F32 = mybir.dt.float32
F32R = mybir.dt.float32r
U32 = mybir.dt.uint32

P = 128
B, T, D = 2, 64, 256
KT = D // P
S = 1024
NKEY = S // P
NCTX = B * NKEY
CHUNK = 512
H0, HK0, D0 = 16, 4, 64
G0 = H0 // HK0
H1, D1 = 16, 16
GRP1 = P // (2 * D1)
TILES = B * H0 // 2
FF = 512
E0, F0 = 8, 128
E1, F1 = 16, 128
LN_EPS, RMS_EPS = 1e-5, 1e-6
FAR = -1e30

ROWS = [("qn", D0), ("kn", D0), ("inw", D), ("ffw", D), ("rb", E0), ("kv1b", 2 * D), ("bq1", D),
        ("bo1", D), ("abv", D), ("abo", D), ("gb", E1)]
COLS = [("alog", KT), ("cout", KT), ("dskip", KT), ("b1", E0), ("abq", KT), ("abk", KT)]
CONSTS = [("ident", P), ("headmask", GRP1), ("pairmask", 2), ("theta0", P), ("iota", E1)]


ROOTS = ["lnA", "q0", "lnB", "rmB", "rmC", "lnC", "lnD", "lnE", "lnF"]
KEPT = ["lnA", "n2", "lnC", "lnD", "lnE", "lnF"]
TURNS = ["lnA", "normed", "scan_out", "n2", "lnC", "lnD", "lnE", "lnF"]


def nth(order, name):
    return order.index(name) + 1


def offsets(fields):
    at, out = 0, {}
    for name, n in fields:
        out[name] = (at, n)
        at += n
    return out, at


ROW_AT, NROW = offsets(ROWS)
COL_AT, NCOL = offsets(COLS)
CONST_AT, NCONST = offsets(CONSTS)


def build(nc, t):
    with ExitStack() as ctx:
        known = {}

        def sem(name):
            if name not in known:
                known[name] = nc.alloc_semaphore(name=name)
            return known[name]

        base = -(-nc.sbuf_base // 64) * 64
        top = [base]

        def region(nbytes):
            at = top[0]
            top[0] += -(-nbytes // 32) * 32
            return at

        def place(name, shape, dt, at):
            return nc.alloc_sbuf_tensor_at(name, shape, dt, offset=at)

        def new(name, shape, dt=F32):
            return place(name, shape, dt, region(4 * int(np.prod(shape[1:]))))

        r_ctx = region(4 * 2 * KT * B * S + 4 * 4 * KT * 512)
        ctx_hi = place("ctx_hi", [P, KT, B * S], F32R, r_ctx)
        ctx_lo = place("ctx_lo", [P, KT, B * S], F32R, r_ctx + 4 * KT * B * S)
        r_w = r_ctx + 8 * KT * B * S
        wkv_hi = [place(f"wkv_hi{l}", [P, KT, 512], F32R, r_w + l * 8 * KT * 512) for l in range(2)]
        wkv_lo = [place(f"wkv_lo{l}", [P, KT, 512], F32R, r_w + (2 * l + 1) * 4 * KT * 512) for l in range(2)]
        wgu = place("wgu", [P, E1 + 1, KT, 2 * F1], F32, r_ctx)
        watt = place("watt", [P, 4, KT, D], F32, r_ctx + 4 * (E1 + 1) * KT * 2 * F1)
        assert ((E1 + 1) * KT * 2 * F1 + 4 * KT * D) * 4 <= 8 * KT * B * S + 16 * KT * 512

        wo0 = new("wo0", [P, 8, D])
        r_k = region(4 * 4 * B * S)
        kstack = place("kstack", [P, 4, B * S], F32R, r_k)
        wdn = place("wdn", [P, E1 + 1, D], F32, r_k)
        vals = new("vals", [P, NCTX, D])
        r_pt = region(4 * 4 * NKEY * 256)
        pt = place("pt", [P, 4, NKEY, 256], F32, r_pt)
        ctx_raw = place("ctx_raw", [P, 4, KT, CHUNK], F32, r_pt)
        wkv_raw = [place(f"wkv_raw{l}", [P, KT, 512], F32, r_pt + 4 * 4 * KT * CHUNK + l * 4 * KT * 512)
                   for l in range(2)]
        w1 = place("w1", [P, KT, E0 * F0], F32, r_pt)
        w2 = place("w2", [P, E0, D], F32, r_pt + 4 * KT * E0 * F0)
        fc = place("fc", [P, KT, FF], F32, r_pt + 4 * (KT * E0 * F0 + E0 * D))
        proj = place("proj", [P, FF // P, D], F32, r_pt + 4 * (KT * E0 * F0 + E0 * D + KT * FF))
        r_p = region(4 * 3 * S)
        prob = place("prob", [P, 3, S], F32, r_p)
        wq0 = place("wq0", [P, KT, H0 * D0], F32, r_p)
        qstack = [new(f"qstack_{x}", [P, B, H0, T], F32R) for x in ("hi", "lo")]
        rw0 = new("rw0", [P, KT, E0])
        b2 = new("b2", [P, D])
        wq1 = new("wq1", [P, KT, D])
        wo1 = new("wo1", [P, KT, D])
        gw1 = new("gw1", [P, KT, E1])
        rows = new("rows", [P, NROW])
        cols = new("cols", [P, NCOL])
        consts = new("consts", [P, NCONST])
        ksp = new("ksp", [P, 2, 4, 2, 64], F32R)
        kn = new("kn", [P, 2, D])
        ksq = new("ksq", [P, 2, D])
        kss = new("kss", [P, 2, 4])
        kvar = new("kvar", [P, 2, 4])
        krs = new("krs", [P, 2, 4])
        mx = new("mx", [P, 2, TILES])
        nmx = new("nmx", [P, 2, TILES])
        sums = new("sums", [P, 2, TILES])
        rsum = new("rsum", [P, 2, TILES])
        xs = new("xs", [P, D])
        zn = new("zn", [P, D])
        zT = new("zT", [P, KT, P])
        wide = new("wide", [P, 1024])
        q_sb = place("q_sb", [P, H0, D0], F32, r_p + 4 * KT * H0 * D0)
        qdup0 = [place("qdup0_hi", [P, H0, 2, D0], F32R, r_p),
                 place("qdup0_lo", [P, H0, 2, D0], F32R, r_pt + 4 * 4 * KT * CHUNK + 2 * 4 * KT * 512)]
        qdup1 = [place(f"qdup1_{x}", [P, 4, 2, GRP1 * D1], F32R, r_p + n * 4 * 512)
                 for n, x in enumerate(("hi", "lo"))]
        oT = new("oT", [P, 8, B, T])
        acc = new("acc", [P, D])
        x1 = new("x1", [P, D])
        normed_t = new("normed_sb", [P, D])
        normed = normed_t[:]
        scratch = new("scratch", [P, D])
        routeT = new("routeT_sb", [P, P])
        scan = place("scan_sb", [P, 2, KT, B, T + T // 2], F32, r_p)
        skip = place("skip_sb", [P, KT, B, T], F32, r_p + 4 * 2 * KT * B * 96)
        scan_out_t = place("scan_out_sb", [P, D], F32, r_p + 4 * (2 * KT * B * 96 + D))
        scan_out = scan_out_t[:]
        att = place("att", [P, 6, P], F32, r_p + 4 * 4 * P)
        att_parts, att_theta, att_e, att_p = att[:, 0:3], att[:, 3], att[:, 4], att[:, 5]
        att_pT_t = place("att_pT_sb", [P, P], F32, r_p + 4 * 10 * P)
        att_pT = att_pT_t[:]
        att_v_t = place("att_v_sb", [P, D], F32, r_p + 4 * 11 * P)
        att_v = att_v_t[:]
        sm = new("sm", [P, 400])
        half = new("half", [P, 16])
        hid = place("hid", [P, 2, 2, P], F32, r_p)
        assert top[0] <= nc.sbuf_usable_end, (top[0], nc.sbuf_usable_end)

        banks = [ctx.enter_context(nc.psum_tensor(f"bank{i}", [P, 512], F32)) for i in range(4)]
        wide_ps = [ctx.enter_context(nc.psum_tensor(f"wide{i}", [P, 1024], F32)) for i in range(2)]
        kv_ps, tr_ps = banks[0:2], banks[2:4]
        pv_ps = banks[0:2]
        W0, W1_ = wide_ps[0], wide_ps[1]
        bank_a, bank_b, bank_c, bank_d = W0[:, 0:512], W0[:, 512:1024], W1_[:, 0:512], W1_[:, 512:1024]

        def row(name):
            at, n = ROW_AT[name]
            return rows[:, at:at + n]

        def col(name, i):
            at = COL_AT[name][0] + i
            return cols[:, at:at + 1]

        def const(name):
            at, n = CONST_AT[name]
            return consts[:, at:at + n]

        ident = const("ident")
        small = {}

        def s_(name, n=1):
            if name not in small:
                small[name] = (sum(k for _, k in small.values()), n)
                assert sum(k for _, k in small.values()) <= 400
            at, n = small[name]
            return sm[:, at:at + n]

        def then(eng, ins, name, n=1):
            ins.then_inc(sem(name), 1)
            eng.wait_ge(sem(name), n)

        block = ctx.enter_context(nc.Block())

        def loaded(eng, name):
            eng.wait_ge(sem("dma_" + name), 16)

        @block.sync
        def _(sp):
            def load(name, dst, src):
                sp.dma_start(dst, src).then_inc(sem("dma_" + name), 16)

            load("x", xs[:], t["x"])
            load("consts", consts[:], t["consts"])
            load("wkv0", wkv_raw[0][:], t["wkv0"])
            load("ctx0", ctx_raw[:, 0], t["ctxT"][0])
            load("wq0", wq0[:], t["wq0"])
            load("rows", rows[:], t["rows"].partition_broadcast(P))
            for c in range(1, 4):
                load(f"ctx{c}", ctx_raw[:, c], t["ctxT"][c])
            load("wkv1", wkv_raw[1][:], t["wkv1"])
            load("cols", cols[:], t["cols"])
            load("wo0", wo0[:], t["wo0"])
            load("rw0", rw0[:], t["rw0"])
            load("b2", b2[0:E0, :], t["b2"])
            load("wq1", wq1[:], t["wq1"])
            load("wo1", wo1[:], t["wo1"])
            load("gw1", gw1[:], t["gw1"])
            sp.wait_ge(sem("pv0"), 4)
            load("fc", fc[:], t["fc"])
            load("proj", proj[:], t["proj"])
            load("w1", w1[:], t["w1"])
            load("w2", w2[:], t["w2"])
            sp.wait_ge(sem("kv_mm1"), NCTX)
            load("watt", watt[:], t["watt"])
            load("wgu0", wgu[:, 0:8], t["wgu"][:, 0:8])
            load("wgu1", wgu[:, 8:17], t["wgu"][:, 8:17])
            sp.wait_ge(sem("score1"), TILES)
            load("wdn", wdn[:], t["wdn"])
            sp.wait_ge(sem("x_final"), 1)
            sp.dma_start(t["out"], xs[:]).then_inc(sem("stored"), 16)
            sp.wait_ge(sem("stored"), 16)

        @block.gpsimd
        def _(pool):
            then(pool, pool.memset(half[:], -0.5), "half_set")

            def rsqrt(name, n=1):
                pool.wait_ge(sem("var"), nth(ROOTS, name))
                pool.tensor_tensor(s_(name + "_rs", n), s_(name + "_ve", n), half[:, 0:n],
                                   ALU.pow).then_inc(sem("root"), 1)

            def key_rsqrt(i):
                pool.wait_ge(sem("kvar"), i + 1)
                if i >= 2:
                    pool.wait_ge(sem("kn0"), i - 1)
                pool.tensor_tensor(krs[:, i % 2], kvar[:, i % 2], half[:, 0:4],
                                   ALU.pow).then_inc(sem("krs"), 1)

            rsqrt("lnA")
            key_rsqrt(0)
            key_rsqrt(1)
            key_rsqrt(2)
            rsqrt("q0", 16)
            for i in range(3, NCTX):
                key_rsqrt(i)
            for name in ("lnB", "rmB", "rmC", "lnC", "lnD", "lnE", "lnF"):
                rsqrt(name)

        @block.tensor
        def _(pe):
            def kv_mm(l, i):
                c = i // 4
                if i % 4 == 0 and l == 0:
                    pe.wait_ge(sem("ctx_split"), 2 * (c + 1))
                if i == 0:
                    pe.wait_ge(sem(f"wkv_split{l}"), 2)
                if i >= 2:
                    pe.wait_ge(sem(f"kn{l}"), i - 1)
                    pe.wait_ge(sem(f"v{l}"), i - 1)
                elif l == 1:
                    pe.wait_ge(sem("pv_read0"), 4)
                sl = slice(i * P, (i + 1) * P)
                parts = [(ctx_hi, wkv_hi[l]), (ctx_lo, wkv_hi[l]), (ctx_hi, wkv_lo[l])]
                for n, (a, w) in enumerate(parts):
                    for k in range(KT):
                        mm = pe.matmul(kv_ps[i % 2][:], a[:, k, sl], w[:, k, :],
                                       start=(n == 0 and k == 0), stop=(n == 2 and k == KT - 1))
                mm.then_inc(sem(f"kv_mm{l}"), 1)

            def k_turn(l, i):
                pe.wait_ge(sem(f"ksplit{l}"), i + 1)
                if i >= 2:
                    pe.wait_ge(sem(f"kstack{l}"), i - 1)
                elif l == 1:
                    pe.wait_ge(sem("pt_odd0"), TILES)
                    pe.wait_ge(sem("pt_even0"), TILES)
                for h in range(4):
                    mm = pe.transpose(tr_ps[i % 2][:, h * P:(h + 1) * P],
                                      ksp[:, i % 2, h].bitcast(F32), ident)
                mm.then_inc(sem(f"k_turn{l}"), 1)

            def turn(name, src, dst_ps):
                pe.wait_ge(sem("turn_in"), nth(TURNS, name))
                for k in range(KT):
                    mm = pe.transpose(dst_ps[:, k * P:(k + 1) * P], src[:, k * P:(k + 1) * P], ident)
                mm.then_inc(sem("turned"), 1)

            def q_turn(l, part, n):
                slot = 4 * part + n if l == 0 else part
                pe.wait_ge(sem(f"q_split{l}"), part + 1)
                if slot >= 2:
                    pe.wait_ge(sem(f"q_stacked{l}"), slot - 1)
                dst = W0[:, (slot % 2) * 512:(slot % 2) * 512 + 512]
                for j in range(4):
                    src = qdup0[part][:, 4 * n + j] if l == 0 else qdup1[part][:, j]
                    mm = pe.transpose(dst[:, j * P:(j + 1) * P],
                                      src.bitcast(F32).rearrange("p x d -> p (x d)"), ident)
                mm.then_inc(sem(f"q_turn{l}"), 1)

            def score(l, i):
                b, r = divmod(i, TILES // B)
                if i % 8 == 0:
                    pe.wait_ge(sem(f"kstack{l}"), NKEY * (b + 1))
                if i == 0:
                    pe.wait_ge(sem(f"q_stacked{l}"), (8, 2)[l])
                if i >= 2:
                    pe.wait_ge(sem(f"exp{l}"), i - 1)
                h = 2 * r
                grp = h // 4
                for part in range(2):
                    for c in range(S // 512):
                        mm = pe.matmul(wide_ps[i % 2][:, c * 512:(c + 1) * 512],
                                       qstack[part][:, b, h:h + 2, :],
                                       kstack[:, grp, b * S + c * 512:b * S + (c + 1) * 512],
                                       start=(part == 0), stop=(part == 1))
                mm.then_inc(sem(f"score{l}"), 1)

            def p_turn(l, i):
                pe.wait_ge(sem(f"norm{l}"), i + 1)
                for hf in range(2):
                    if i >= 1:
                        pe.wait_ge(sem(f"pt_{('even', 'odd')[hf]}{l}"), i)
                    elif l == 0:
                        pe.wait_ge(sem("kstack0"), NCTX)
                    else:
                        pe.wait_ge(sem("kstack1"), NCTX)
                    for j in range(4):
                        kt = 4 * hf + j
                        mm = pe.transpose(tr_ps[hf][:, j * P:(j + 1) * P],
                                          prob[:, i % 3, kt * P:(kt + 1) * P], ident)
                    mm.then_inc(sem(f"p_turn{l}"), 1)

            def pv(l, g):
                pe.wait_ge(sem(f"pt_even{l}"), 4 * g + 4)
                pe.wait_ge(sem(f"pt_odd{l}"), 4 * g + 4)
                if g >= 2:
                    pe.wait_ge(sem(f"pv_read{l}"), g - 1)
                elif g == 0:
                    pe.wait_ge(sem(f"v{l}"), NCTX)
                    pe.wait_ge(sem(f"kn{l}"), NCTX)
                b, hf = divmod(g, 2)
                for kt in range(NKEY):
                    v = vals[:, b * NKEY + kt, :]
                    if l == 0:
                        for j in range(2):
                            mm = pe.matmul(pv_ps[g % 2][64 * j:64 * j + 64, 0:256],
                                           v[:, (2 * hf + j) * D0:(2 * hf + j + 1) * D0],
                                           pt[:, (2 * g + j) % 4, kt, :],
                                           start=(kt == 0), stop=(kt == NKEY - 1))
                    else:
                        for j in range(4):
                            f = P * hf + 32 * j
                            mm = pe.matmul(pv_ps[g % 2][32 * j:32 * j + 32, 0:P], v[:, f:f + 32],
                                           pt[:, (2 * g + j // 2) % 4, kt, (j % 2) * P:(j % 2 + 1) * P],
                                           start=(kt == 0), stop=(kt == NKEY - 1))
                mm.then_inc(sem(f"pv{l}"), 1)

            def attention(l):
                for i in range(TILES + 3):
                    if i < TILES:
                        score(l, i)
                    if 2 <= i < TILES + 2:
                        p_turn(l, i - 2)
                    if i >= 6 and i % 4 == 2:
                        pv(l, (i - 6) // 4)

            def linear(out, lhs, rhs, n):
                for k in range(n):
                    mm = pe.matmul(out, lhs(k), rhs(k), start=(k == 0), stop=(k == n - 1))
                return mm

            loaded(pe, "consts")
            turn("lnA", zn, bank_a)
            for i in range(2):
                kv_mm(0, i)
            pe.wait_ge(sem("kept"), nth(KEPT, "lnA"))
            loaded(pe, "wq0")
            for n in range(2):
                mm = linear(W1_[:, n * 512:(n + 1) * 512], lambda k: zT[:, k, :],
                            lambda k: wq0[:, k, n * 512:(n + 1) * 512], KT)
            mm.then_inc(sem("q0_mm"), 1)
            for i in range(2, NCTX):
                kv_mm(0, i)
                k_turn(0, i - 2)
                if i >= 8:
                    q_turn(0, (i - 8) // 4, (i - 8) % 4)
            k_turn(0, NCTX - 2)
            k_turn(0, NCTX - 1)

            attention(0)

            def step1(i):
                kv_mm(1, i)
                if i >= 1:
                    k_turn(1, i - 1)

            pe.wait_ge(sem("pv_read0"), 4)
            loaded(pe, "wo0")
            linear(bank_a[:, 0:D], lambda k: oT[:, k].rearrange("p b t -> p (b t)"),
                   lambda k: wo0[:, k, :], 8).then_inc(sem("out0_mm"), 1)
            step1(0)
            turn("normed", normed, bank_c)
            step1(1)
            turn("scan_out", scan_out, bank_a)
            step1(2)
            turn("n2", normed, bank_c)
            step1(3)
            pe.wait_ge(sem("kept"), nth(KEPT, "n2"))
            loaded(pe, "fc")
            for j in range(FF // P):
                mm = linear(bank_b[:, j * P:(j + 1) * P], lambda k: fc[:, k, j * P:(j + 1) * P],
                            lambda k: zT[:, k, :], KT)
            mm.then_inc(sem("ff_h"), 1)
            step1(4)
            pe.wait_ge(sem("ff_act"), 1)
            loaded(pe, "proj")
            linear(bank_d[:, 0:D], lambda k: wide[:, k * P:(k + 1) * P], lambda k: proj[:, k, :],
                   FF // P).then_inc(sem("ff_out"), 1)
            step1(5)
            turn("lnC", zn, bank_a)
            step1(6)
            pe.wait_ge(sem("kept"), nth(KEPT, "lnC"))
            loaded(pe, "rw0")
            linear(bank_b[:, 0:E0], lambda k: zT[:, k, :], lambda k: rw0[:, k, :],
                   KT).then_inc(sem("router_mm"), 1)
            loaded(pe, "w1")
            for e in range(E0):
                mm = linear((bank_c, bank_d)[e // 4][:, (e % 4) * P:(e % 4 + 1) * P],
                            lambda k: w1[:, k, e * F0:(e + 1) * F0], lambda k: zT[:, k, :], KT)
                if e % 4 == 3:
                    mm.then_inc(sem("moe_h"), 1)
            step1(7)
            step1(8)
            pe.wait_ge(sem("route0"), 1)
            pe.transpose(bank_a[0:E0, 0:P], s_("route0", E0), ident).then_inc(sem("route_turn"), 1)
            step1(9)
            pe.wait_ge(sem("routeT"), 1)
            loaded(pe, "b2")
            pe.matmul(bank_b[:, 0:D], routeT[0:E0, :], b2[0:E0, :], start=True,
                      stop=True).then_inc(sem("moe_b2"), 1)
            loaded(pe, "w2")
            for n in range(E0 // 2):
                if n == 1:
                    pe.wait_ge(sem("moe_acc"), 1)
                pe.wait_ge(sem("moe_act"), E0 if n >= 2 else 2 * n + 2)
                for j in range(2):
                    e = 2 * n + j
                    mm = pe.matmul((bank_a, bank_b, bank_c, bank_d)[n][:, j * D:(j + 1) * D],
                                   wide[:, e * P:(e + 1) * P], w2[:, e, :], start=True, stop=True)
                mm.then_inc(sem("moe_out"), 1)
                step1(10 + n)
            turn("lnD", zn, bank_a)
            step1(14)
            pe.wait_ge(sem("kept"), nth(KEPT, "lnD"))
            loaded(pe, "wq1")
            linear(bank_b[:, 0:D], lambda k: zT[:, k, :], lambda k: wq1[:, k, :],
                   KT).then_inc(sem("q1_mm"), 1)
            step1(15)
            q_turn(1, 0, 0)
            q_turn(1, 1, 0)
            k_turn(1, 15)

            attention(1)

            pe.wait_ge(sem("pv_read1"), 4)
            loaded(pe, "wo1")
            linear(bank_a[:, 0:D], lambda k: oT[:, k].rearrange("p b t -> p (b t)"),
                   lambda k: wo1[:, k, :], KT).then_inc(sem("out1_mm"), 1)

            turn("lnE", zn, bank_c)
            pe.wait_ge(sem("kept"), nth(KEPT, "lnE"))
            loaded(pe, "watt")
            for j in range(2 * KT):
                mm = linear(bank_b[:, j * P:(j + 1) * P],
                            lambda k: watt[:, j // KT, k, (j % KT) * P:(j % KT + 1) * P],
                            lambda k: zT[:, k, :], KT)
            mm.then_inc(sem("att_qk"), 1)
            linear(bank_d[:, 0:D], lambda k: zT[:, k, :], lambda k: watt[:, 2, k, :],
                   KT).then_inc(sem("att_v"), 1)
            pe.wait_ge(sem("att_qk_sb"), 4)
            linear(bank_a[:, 0:P], lambda k: wide[:, k * P:(k + 1) * P],
                   lambda k: wide[:, (2 + k) * P:(3 + k) * P], KT).then_inc(sem("att_s"), 1)
            pe.wait_ge(sem("att_p"), 1)
            pe.transpose(bank_c[:, 0:P], att_p, ident).then_inc(sem("att_p_turn"), 1)
            pe.wait_ge(sem("att_pT"), 1)
            for m in range(KT):
                mm = pe.matmul(bank_b[:, m * P:(m + 1) * P], att_v[:, m * P:(m + 1) * P],
                               att_pT, start=True, stop=True)
            mm.then_inc(sem("att_o"), 1)
            pe.wait_ge(sem("att_oT"), 1)
            linear(bank_d[:, 0:D], lambda k: zT[:, k, :], lambda k: watt[:, 3, k, :],
                   KT).then_inc(sem("att_out"), 1)

            turn("lnF", zn, bank_a)
            pe.wait_ge(sem("kept"), nth(KEPT, "lnF"))
            loaded(pe, "gw1")
            linear(bank_b[:, 0:E1], lambda k: zT[:, k, :], lambda k: gw1[:, k, :],
                   KT).then_inc(sem("gate_mm"), 1)
            for n in range(E1 + 3):
                if n <= E1:
                    loaded(pe, "wgu0" if n < 8 else "wgu1")
                    if n >= 2:
                        pe.wait_ge(sem("exp_h"), n - 1)
                    for gu in range(2):
                        mm = linear(banks[n % 2][:, gu * P:(gu + 1) * P],
                                    lambda k: wgu[:, n, k, gu * F1:(gu + 1) * F1],
                                    lambda k: zT[:, k, :], KT)
                    mm.then_inc(sem("exp_gu"), 1)
                if n >= 2:
                    m = n - 2
                    if m == 0:
                        loaded(pe, "wdn")
                    pe.wait_ge(sem("exp_h"), m + 1)
                    if m >= 2:
                        pe.wait_ge(sem("exp_sum"), m - 1)
                    pe.matmul(banks[2 + m % 2][:, 0:D], hid[:, m % 2, 1, :], wdn[:, m, :],
                              start=True, stop=True).then_inc(sem("exp_dn"), 1)

        @block.scalar
        def _(act):
            def v_copy(i):
                act.wait_ge(sem("kv_mm0"), i + 1)
                if i >= 2:
                    act.wait_ge(sem("kss"), i - 1)
                act.activation(ksq[:, i % 2], kv_ps[i % 2][:, 0:D], ACT.Square).then_inc(sem("ksq"), 1)
                act.activation(vals[:, i], kv_ps[i % 2][:, D:2 * D], ACT.Copy).then_inc(sem("v0"), 1)

            def k_stack(l, i):
                act.wait_ge(sem(f"k_turn{l}"), i + 1)
                if l == 1 and i == 0:
                    act.wait_ge(sem("score0"), TILES)
                act.activation(kstack[:, :, i * P:(i + 1) * P],
                               tr_ps[i % 2][:].rearrange("p (h k) -> p h k", h=4),
                               ACT.Copy).then_inc(sem(f"kstack{l}"), 1)

            def q_stack(slot):
                part, n = divmod(slot, 4)
                act.wait_ge(sem("q_turn0"), slot + 1)
                for b in range(B):
                    src = W0[:, (slot % 2) * 512:(slot % 2) * 512 + 512].rearrange(
                        "p (h b t) -> p b h t", h=4, b=B)
                    ins = act.activation(qstack[part][:, b, 4 * n:4 * n + 4, :], src[:, b], ACT.Copy)
                ins.then_inc(sem("q_stacked0"), 1)

            def exp(l, i):
                act.wait_ge(sem(f"nmx{l}"), i + 1)
                if i >= 3:
                    act.wait_ge(sem(f"p_turn{l}"), 2 * (i - 2))
                act.activation(prob[:, i % 3], wide_ps[i % 2][:], ACT.Exp, bias=nmx[:, l, i:i + 1],
                               scale=SCALE[l], accum_out=sums[:, l, i:i + 1]).then_inc(sem(f"exp{l}"), 1)

            def pt_even(l, i):
                act.wait_ge(sem(f"p_turn{l}"), 2 * i + 1)
                if i >= 8 and i % 4 == 0:
                    act.wait_ge(sem(f"pv{l}"), i // 4 - 1)
                act.activation(pt[:, (i // 2) % 4, 0:4, (i % 2) * P:(i % 2 + 1) * P],
                               tr_ps[0][:].rearrange("p (k q) -> p k q", k=4),
                               ACT.Copy).then_inc(sem(f"pt_even{l}"), 1)

            def attention(l):
                for i in range(TILES + 2):
                    if i < TILES:
                        exp(l, i)
                    if i >= 2:
                        pt_even(l, i - 2)

            loaded(act, "cols")
            then(act, act.activation(s_("ea", KT), cols[:, 0:KT], ACT.Exp), "decay")
            act.activation(s_("pow", 12)[:, 0:KT], s_("ea", KT), ACT.Exp, scale=-1.0).then_inc(sem("decay"), 1)
            for i in range(2):
                v_copy(i)
            act.wait_ge(sem("q0_mm"), 1)
            act.activation(wide[:], W1_[:], ACT.Square).then_inc(sem("q_sq"), 1)
            for i in range(2, NCTX):
                v_copy(i)
                k_stack(0, i - 2)
                if i >= 8:
                    q_stack(i - 8)
            k_stack(0, NCTX - 2)
            k_stack(0, NCTX - 1)

            attention(0)

            k_stack(1, 0)
            k_stack(1, 1)
            act.wait_ge(sem("ff_h"), 1)
            act.activation(wide[:, 0:FF], bank_b, ACT.Tanh, scale=0.5).then_inc(sem("ff_tanh"), 1)
            for i in range(2, 6):
                k_stack(1, i)
            act.wait_ge(sem("r_nmax"), 1)
            act.activation(s_("r_exp", E0), s_("r_logit", E0), ACT.Exp, bias=s_("r_nmax"),
                           accum_out=s_("r_sum")).then_inc(sem("r_exp"), 1)
            for e in range(E0):
                act.wait_ge(sem("moe_h"), e // 4 + 1)
                act.activation(wide[:, e * P:(e + 1) * P], (bank_c, bank_d)[e // 4][:, (e % 4) * P:(e % 4 + 1) * P],
                               ACT.Gelu, bias=col("b1", e)).then_inc(sem("moe_act"), 1)
            for i in range(6, NCTX):
                k_stack(1, i)

            attention(1)

            act.wait_ge(sem("att_s"), 1)
            for n, (func, scale) in enumerate(((ACT.Tanh, 0.5), (ACT.Tanh, 1.0), (ACT.Relu, 1.0))):
                act.activation(att_parts[:, n, :], bank_a[:, 0:P], func,
                               scale=scale).then_inc(sem("att_parts"), 1)
            act.wait_ge(sem("att_nmax"), 1)
            act.activation(att_e, att_theta, ACT.Exp, bias=s_("att_nmax"),
                           accum_out=s_("att_sum")).then_inc(sem("att_exp"), 1)
            act.wait_ge(sem("g_logit"), 1)
            act.activation(s_("g_tanh", E1), s_("g_logit", E1), ACT.Tanh, scale=0.5).then_inc(sem("g_tanh"), 1)
            for n in range(E1 + 1):
                act.wait_ge(sem("exp_gu"), n + 1)
                if n >= 2:
                    act.wait_ge(sem("exp_h"), n - 1)
                act.activation(hid[:, n % 2, 0, :], banks[n % 2][:, 0:P], ACT.Tanh,
                               scale=0.5).then_inc(sem("exp_tanh"), 1)

        @block.vector
        def _(dve):
            count = [0]

            def link(ins):
                count[0] += 1
                ins.then_inc(sem("dve_link"), 1)
                dve.wait_ge(sem("dve_link"), count[0])

            def layer_norm(name, src):
                link(dve.bn_stats(s_("bn", 6), src))
                link(dve.bn_aggr(s_(name + "_mv", 2), s_("bn", 6)))
                dve.tensor_scalar(s_(name + "_ve"), s_(name + "_mv", 2)[:, 1:2], LN_EPS, None,
                                  ALU.add).then_inc(sem("var"), 1)
                dve.wait_ge(sem("root"), nth(ROOTS, name))
                ins = dve.tensor_scalar(zn[:], src, s_(name + "_mv", 2)[:, 0:1], s_(name + "_rs"),
                                        ALU.subtract, ALU.mult)
                if name == "lnB":
                    link(ins)
                else:
                    then(dve, ins, "turn_in", nth(TURNS, name))

            def rms(name, src, out, weight):
                link(dve.tensor_tensor_reduce(scratch[:], src, src, 1.0, 0.0, ALU.mult, ALU.add,
                                              s_(name + "_ss")))
                dve.tensor_scalar(s_(name + "_ve"), s_(name + "_ss"), 1.0 / D, RMS_EPS, ALU.mult,
                                  ALU.add).then_inc(sem("var"), 1)
                dve.wait_ge(sem("root"), nth(ROOTS, name))
                return dve.scalar_tensor_tensor(out, src, s_(name + "_rs"), weight, ALU.mult, ALU.mult)

            def keep_turned(name, ps):
                dve.wait_ge(sem("turned"), nth(TURNS, name))
                dve.tensor_copy(zT[:].rearrange("p k n -> p (k n)"), ps[:, 0:2 * P]
                                ).then_inc(sem("kept"), 1)

            def split(hi, lo, src, name):
                then(dve, dve.tensor_copy(hi, src), name, split_at[name])
                split_at[name] += 1
                then(dve, dve.tensor_tensor(lo, src, hi.bitcast(F32), ALU.subtract), name, split_at[name])
                split_at[name] += 1

            split_at = {}

            def split_ctx(c):
                split_at.setdefault("ctx_split", 1)
                loaded(dve, f"ctx{c}")
                sl = slice(c * CHUNK, (c + 1) * CHUNK)
                split(ctx_hi[:, :, sl], ctx_lo[:, :, sl], ctx_raw[:, c], "ctx_split")

            def split_wkv(l):
                split_at[f"wkv_split{l}"] = 1
                loaded(dve, f"wkv{l}")
                split(wkv_hi[l][:], wkv_lo[l][:], wkv_raw[l][:], f"wkv_split{l}")

            def key_var(i):
                dve.wait_ge(sem("ksq"), i + 1)
                then(dve, dve.tensor_reduce(kss[:, i % 2], ksq[:, i % 2].rearrange("p (h d) -> p h d", h=4),
                                            AX.X, ALU.add), "kss", i + 1)
                if i >= 2:
                    dve.wait_ge(sem("krs"), i - 1)
                dve.tensor_scalar(kvar[:, i % 2], kss[:, i % 2], 1.0 / D0, RMS_EPS, ALU.mult,
                                  ALU.add).then_inc(sem("kvar"), 1)

            def key_split(l, i):
                if i >= 2:
                    dve.wait_ge(sem(f"k_turn{l}"), i - 1)
                if l == 0:
                    dve.wait_ge(sem("krs"), i + 1)
                    dve.wait_ge(sem("v0"), i + 1)
                    then(dve, dve.tensor_tensor(
                        kn[:, i % 2].rearrange("p (h d) -> p h d", h=4),
                        kv_ps[i % 2][:, 0:D].rearrange("p (h d) -> p h d", h=4),
                        krs[:, i % 2].unsqueeze(2).to_broadcast([P, 4, D0]), ALU.mult), "kn0", i + 1)
                else:
                    dve.wait_ge(sem("kv_mm1"), i + 1)
                    if i == 0:
                        loaded(dve, "rows")
                    then(dve, dve.tensor_tensor(kn[:, i % 2], kv_ps[i % 2][:, 0:D], row("kv1b")[:, 0:D],
                                                ALU.add), "kn1", i + 1)
                    if i == 0:
                        dve.wait_ge(sem("pv0"), 4)
                    dve.tensor_tensor(vals[:, i], kv_ps[i % 2][:, D:2 * D], row("kv1b")[:, D:2 * D],
                                      ALU.add).then_inc(sem("v1"), 1)
                src = kn[:, i % 2].rearrange("p (h d) -> p h d", h=4)
                link(dve.tensor_copy(ksp[:, i % 2, :, 0, :], src))
                dve.tensor_tensor(ksp[:, i % 2, :, 1, :], src, ksp[:, i % 2, :, 0, :].bitcast(F32),
                                  ALU.subtract).then_inc(sem(f"ksplit{l}"), 1)

            def row_max(l, i):
                dve.wait_ge(sem(f"score{l}"), i + 1)
                link(dve.tensor_reduce(mx[:, l, i:i + 1], wide_ps[i % 2][:], AX.X, ALU.max))
                dve.tensor_scalar(nmx[:, l, i:i + 1], mx[:, l, i:i + 1], -SCALE[l], None,
                                  ALU.mult).then_inc(sem(f"nmx{l}"), 1)

            def norm(l, i):
                dve.wait_ge(sem(f"exp{l}"), i + 1)
                link(dve.reciprocal(rsum[:, l, i:i + 1], sums[:, l, i:i + 1]))
                dve.tensor_scalar(prob[:, i % 3], prob[:, i % 3], rsum[:, l, i:i + 1], None,
                                  ALU.mult).then_inc(sem(f"norm{l}"), 1)

            def pt_odd(l, i):
                dve.wait_ge(sem(f"p_turn{l}"), 2 * i + 2)
                if i >= 8 and i % 4 == 0:
                    dve.wait_ge(sem(f"pv{l}"), i // 4 - 1)
                dve.tensor_copy(pt[:, (i // 2) % 4, 4:8, (i % 2) * P:(i % 2 + 1) * P],
                                tr_ps[1][:].rearrange("p (k q) -> p k q", k=4)
                                ).then_inc(sem(f"pt_odd{l}"), 1)

            def pv_read(l, g):
                dve.wait_ge(sem(f"pv{l}"), g + 1)
                b, hf = divmod(g, 2)
                if l == 0:
                    dve.tensor_copy(oT[:, 4 * hf:4 * hf + 4, b, :],
                                    pv_ps[g % 2][:, 0:256].rearrange("p (g t) -> p g t", g=4)
                                    ).then_inc(sem("pv_read0"), 1)
                else:
                    link(dve.tensor_scalar(scratch[:, 0:T], pv_ps[g % 2][:, 0:T],
                                           const("pairmask")[:, 0:1], None, ALU.mult))
                    dve.scalar_tensor_tensor(oT[:, hf, b, :], pv_ps[g % 2][:, T:2 * T],
                                             const("pairmask")[:, 1:2], scratch[:, 0:T], ALU.mult,
                                             ALU.add).then_inc(sem("pv_read1"), 1)
                    dve.wait_ge(sem("pv_read1"), g + 1)

            def attention(l):
                for i in range(TILES + 5):
                    if i < TILES:
                        row_max(l, i)
                    if 1 <= i <= TILES:
                        norm(l, i - 1)
                    if 2 <= i < TILES + 2:
                        pt_odd(l, i - 2)
                    if i >= 8 and i % 4 == 0:
                        pv_read(l, (i - 8) // 4)

            def residual(ps, name, bias=None):
                dve.wait_ge(sem(name), 1)
                if bias is not None:
                    link(dve.tensor_tensor(acc[:], ps, bias, ALU.add))
                    link(dve.tensor_tensor(xs[:], xs[:], acc[:], ALU.add))
                else:
                    link(dve.tensor_tensor(xs[:], xs[:], ps, ALU.add))

            def route(name, values, n, factor):
                top, idx, w = s_(name + "_top", 8), s_(name + "_idx", 8), s_(name + "_w", 2)
                link(dve.max(top, values))
                link(dve.max_index(idx.bitcast(U32), top, values))
                link(dve.tensor_copy(s_(name + "_at", 2), idx[:, 0:2].bitcast(U32)))
                link(dve.tensor_tensor(s_(name + "_s"), top[:, 0:1], top[:, 1:2], ALU.add))
                link(dve.reciprocal(s_(name + "_r"), s_(name + "_s")))
                link(dve.tensor_scalar(w, top[:, 0:2], s_(name + "_r"), factor, ALU.mult, ALU.mult))
                at = s_(name + "_at", 2)
                link(dve.tensor_scalar(s_(name + "_a", n), const("iota")[:, 0:n], at[:, 0:1], w[:, 0:1],
                                       ALU.is_equal, ALU.mult))
                link(dve.tensor_scalar(s_(name + "_b", n), const("iota")[:, 0:n], at[:, 1:2], w[:, 1:2],
                                       ALU.is_equal, ALU.mult))
                then(dve, dve.tensor_tensor(s_(name, n), s_(name + "_a", n), s_(name + "_b", n), ALU.add), name)

            loaded(dve, "x")
            layer_norm("lnA", xs[:])
            split_wkv(0)
            split_ctx(0)
            keep_turned("lnA", bank_a)
            key_var(0)
            key_var(1)
            key_split(0, 0)
            loaded(dve, "rows")
            link(dve.tensor_tensor(scratch[:, 0:D0], row("qn"), row("kn"), ALU.mult))
            split_ctx(1)
            key_var(2)
            key_split(0, 1)
            dve.wait_ge(sem("q_sq"), 1)
            link(dve.tensor_reduce(s_("q0_ss", 16), wide[:].rearrange("p (h d) -> p h d", h=H0), AX.X, ALU.add))
            dve.tensor_scalar(s_("q0_ve", 16), s_("q0_ss", 16), 1.0 / D0, RMS_EPS, ALU.mult,
                              ALU.add).then_inc(sem("var"), 1)
            key_var(3)
            key_split(0, 2)
            split_ctx(2)
            dve.wait_ge(sem("root"), nth(ROOTS, "q0"))
            link(dve.tensor_tensor(q_sb[:], W1_[:].rearrange("p (h d) -> p h d", h=H0),
                                   s_("q0_rs", 16).unsqueeze(2).to_broadcast([P, H0, D0]), ALU.mult))
            key_var(4)
            key_split(0, 3)
            link(dve.tensor_tensor(q_sb[:], q_sb[:],
                                   scratch[:, 0:D0].unsqueeze(1).to_broadcast([P, H0, D0]), ALU.mult))
            key_var(5)
            key_split(0, 4)
            twice = q_sb[:].unsqueeze(2).to_broadcast([P, H0, 2, D0])
            then(dve, dve.tensor_copy(qdup0[0][:], twice), "q_split0", 1)
            split_ctx(3)
            key_var(6)
            key_split(0, 5)
            then(dve, dve.tensor_tensor(qdup0[1][:], twice, qdup0[0][:].bitcast(F32), ALU.subtract),
                 "q_split0", 2)
            for i in range(7, NCTX):
                key_var(i)
                key_split(0, i - 1)
            key_split(0, NCTX - 1)
            split_wkv(1)

            attention(0)

            residual(bank_a[:, 0:D], "out0_mm")
            layer_norm("lnB", xs[:])
            rms("rmB", zn[:], normed, row("inw")).then_inc(sem("turn_in"), 1)
            PAD = T // 2
            then(dve, dve.memset(scan[:].rearrange("p i k b t -> p (i k b) t")[:, :, 0:PAD], 0.0), "scan_zero")
            dve.wait_ge(sem("decay"), 2)
            pw = s_("pow", 12)
            for s in range(1, 6):
                link(dve.tensor_tensor(pw[:, 2 * s:2 * s + 2], pw[:, 2 * s - 2:2 * s],
                                       pw[:, 2 * s - 2:2 * s], ALU.mult))
            dve.wait_ge(sem("turned"), nth(TURNS, "normed"))
            for k in range(KT):
                src = bank_c[:, k * P:(k + 1) * P].rearrange("p (b t) -> p b t", b=B)
                dve.tensor_copy(scan[:, 0, k, :, PAD:], src).then_inc(sem("scan"), 1)
                dve.tensor_scalar(skip[:, k], src, col("dskip", k), None, ALU.mult).then_inc(sem("skip"), 1)
            for s in range(6):
                for k in range(KT):
                    dve.wait_ge(sem("scan"), 2 * s + k + 1)
                    now, at = scan[:, s % 2, k], PAD - 2 ** s
                    dve.scalar_tensor_tensor(scan[:, (s + 1) % 2, k, :, PAD:], now[:, :, at:at + T],
                                             pw[:, 2 * s + k:2 * s + k + 1], now[:, :, PAD:],
                                             ALU.mult, ALU.add).then_inc(sem("scan"), 1)
            dve.wait_ge(sem("skip"), 2)
            for k in range(KT):
                dve.wait_ge(sem("scan"), 2 * 6 + k + 1)
                ins = dve.scalar_tensor_tensor(
                    scan_out[:, k * P:(k + 1) * P].rearrange("p (b t) -> p b t", b=B), scan[:, 0, k, :, PAD:],
                    col("cout", k), skip[:, k], ALU.mult, ALU.add)
            ins.then_inc(sem("turn_in"), 1)
            key_split(1, 0)
            dve.wait_ge(sem("turned"), nth(TURNS, "scan_out"))
            link(dve.tensor_tensor(x1[:], zn[:], bank_a[:, 0:D], ALU.add))
            rms("rmC", x1[:], normed, row("ffw")).then_inc(sem("turn_in"), 1)
            key_split(1, 1)
            keep_turned("n2", bank_c)
            key_split(1, 2)
            dve.wait_ge(sem("ff_tanh"), 1)
            dve.scalar_tensor_tensor(wide[:, 0:FF], wide[:, 0:FF], 1.0, bank_b, ALU.add,
                                     ALU.mult).then_inc(sem("ff_act"), 1)
            link(dve.tensor_tensor(acc[:], xs[:], x1[:], ALU.add))
            key_split(1, 3)
            dve.wait_ge(sem("ff_out"), 1)
            link(dve.scalar_tensor_tensor(xs[:], bank_d[:, 0:D], 0.5, acc[:], ALU.mult, ALU.add))
            layer_norm("lnC", xs[:])
            key_split(1, 4)
            keep_turned("lnC", bank_a)
            key_split(1, 5)
            dve.wait_ge(sem("router_mm"), 1)
            link(dve.tensor_tensor(s_("r_logit", E0), bank_b[:, 0:E0], row("rb"), ALU.add))
            link(dve.max(s_("r_top", 8), s_("r_logit", E0)))
            dve.tensor_scalar(s_("r_nmax"), s_("r_top", 8)[:, 0:1], -1.0, None, ALU.mult).then_inc(sem("r_nmax"), 1)
            key_split(1, 6)
            dve.wait_ge(sem("r_exp"), 1)
            link(dve.reciprocal(s_("r_rsum"), s_("r_sum")))
            link(dve.tensor_scalar(s_("r_p", E0), s_("r_exp", E0), s_("r_rsum"), None, ALU.mult))
            route("route0", s_("r_p", E0), E0, 1.0)
            key_split(1, 7)
            dve.wait_ge(sem("route_turn"), 1)
            dve.tensor_copy(routeT[0:E0, :], bank_a[0:E0, 0:P]).then_inc(sem("routeT"), 1)
            key_split(1, 8)
            dve.wait_ge(sem("moe_b2"), 1)
            then(dve, dve.tensor_tensor(acc[:], xs[:], bank_b[:, 0:D], ALU.add), "moe_acc")
            r0 = s_("route0", E0)
            for n in range(E0 // 2):
                dve.wait_ge(sem("moe_out"), n + 1)
                for j in range(2):
                    e = 2 * n + j
                    last = e == E0 - 1
                    link(dve.scalar_tensor_tensor(
                        (xs if last else acc)[:], (bank_a, bank_b, bank_c, bank_d)[n][:, j * D:(j + 1) * D],
                        r0[:, e:e + 1], acc[:], ALU.mult, ALU.add))
                if n < 3:
                    key_split(1, 9 + n)
            layer_norm("lnD", xs[:])
            key_split(1, 12)
            keep_turned("lnD", bank_a)
            key_split(1, 13)
            dve.wait_ge(sem("q1_mm"), 1)
            link(dve.tensor_tensor(acc[:], bank_b[:, 0:D], row("bq1"), ALU.add))
            twice = acc[:].rearrange("p (g d) -> p g d", g=4).unsqueeze(2).to_broadcast([P, 4, 2, 64])
            then(dve, dve.tensor_copy(qdup1[0][:], twice), "q_split1", 1)
            dve.tensor_tensor(qdup1[1][:], twice, qdup1[0][:].bitcast(F32), ALU.subtract).then_inc(sem("q_split1"), 1)
            key_split(1, 14)
            key_split(1, 15)
            for part in range(2):
                dve.wait_ge(sem("q_turn1"), part + 1)
                for n in range(4):
                    ps = (bank_a, bank_b)[part][:, n * P:(n + 1) * P].rearrange("p (b t) -> p b t", b=B)
                    for b in range(B):
                        ins = dve.tensor_tensor(
                            qstack[part][:, b, 4 * n:4 * n + 4, :],
                            ps[:, b].unsqueeze(1).to_broadcast([P, 4, T]),
                            const("headmask").unsqueeze(2).to_broadcast([P, 4, T]), ALU.mult)
                ins.then_inc(sem("q_stacked1"), 1)

            attention(1)

            residual(bank_a[:, 0:D], "out1_mm", row("bo1"))
            layer_norm("lnE", xs[:])
            keep_turned("lnE", bank_c)
            dve.wait_ge(sem("att_qk"), 1)
            for j in range(2 * KT):
                dve.tensor_scalar(wide[:, j * P:(j + 1) * P], bank_b[:, j * P:(j + 1) * P],
                                  col(("abq", "abk")[j // KT], j % KT), None,
                                  ALU.add).then_inc(sem("att_qk_sb"), 1)
            dve.wait_ge(sem("att_v"), 1)
            link(dve.tensor_tensor(att_v, bank_d[:, 0:D], row("abv"), ALU.add))
            dve.wait_ge(sem("att_parts"), 3)
            link(dve.scalar_tensor_tensor(att_theta, att_parts[:, 0, :], 0.1, const("theta0"), ALU.mult, ALU.add))
            link(dve.scalar_tensor_tensor(att_theta, att_parts[:, 1, :], 0.15, att_theta, ALU.mult, ALU.add))
            link(dve.scalar_tensor_tensor(att_theta, att_parts[:, 2, :], 0.1, att_theta, ALU.mult, ALU.add))
            link(dve.tensor_reduce(s_("att_max"), att_theta, AX.X, ALU.max))
            dve.tensor_scalar(s_("att_nmax"), s_("att_max"), -1.0, None, ALU.mult).then_inc(sem("att_nmax"), 1)
            dve.wait_ge(sem("att_exp"), 1)
            link(dve.reciprocal(s_("att_rsum"), s_("att_sum")))
            dve.tensor_scalar(att_p, att_e, s_("att_rsum"), None, ALU.mult).then_inc(sem("att_p"), 1)
            dve.wait_ge(sem("att_p_turn"), 1)
            dve.tensor_copy(att_pT, bank_c[:, 0:P]).then_inc(sem("att_pT"), 1)
            dve.wait_ge(sem("att_o"), 1)
            dve.tensor_copy(zT[:].rearrange("p k n -> p (k n)"), bank_b[:, 0:D]).then_inc(sem("att_oT"), 1)
            residual(bank_d[:, 0:D], "att_out", row("abo"))
            layer_norm("lnF", xs[:])
            keep_turned("lnF", bank_a)
            link(dve.tensor_tensor(acc[:], xs[:], zn[:], ALU.add))
            dve.wait_ge(sem("gate_mm"), 1)
            dve.tensor_tensor(s_("g_logit", E1), bank_b[:, 0:E1], row("gb"), ALU.add).then_inc(sem("g_logit"), 1)
            dve.wait_ge(sem("g_tanh"), 1)
            link(dve.tensor_scalar(s_("g_sig", E1), s_("g_tanh", E1), 1.0, 0.5, ALU.add, ALU.mult))
            route("route1", s_("g_sig", E1), E1, 0.5)
            r1 = s_("route1", E1)
            for n in range(E1 + 3):
                if n <= E1:
                    dve.wait_ge(sem("exp_tanh"), n + 1)
                    link(dve.scalar_tensor_tensor(hid[:, n % 2, 0, :], hid[:, n % 2, 0, :], 1.0,
                                                  banks[n % 2][:, 0:P], ALU.add, ALU.mult))
                    if n >= 2:
                        dve.wait_ge(sem("exp_dn"), n - 1)
                    dve.tensor_tensor(hid[:, n % 2, 1, :], hid[:, n % 2, 0, :], banks[n % 2][:, P:2 * P],
                                      ALU.mult).then_inc(sem("exp_h"), 1)
                if n >= 2:
                    m = n - 2
                    dve.wait_ge(sem("exp_dn"), m + 1)
                    w = 0.5 if m == 0 else r1[:, m - 1:m]
                    then(dve, dve.scalar_tensor_tensor(acc[:], banks[2 + m % 2][:, 0:D], w, acc[:],
                                                       ALU.mult, ALU.add), "exp_sum", m + 1)
            dve.tensor_copy(xs[:], acc[:]).then_inc(sem("x_final"), 1)


SCALE = (1.0, 0.25)


def kernel(**inputs):
    import concourse.bacc as _bacc
    from concourse.bass_utils import run_bass_kernel_spmd as _run

    a = {k: np.asarray(v) for k, v in inputs.items()}

    def by_rows(w):
        return w.reshape(-1, P, w.shape[-1]).transpose(1, 0, 2)

    L0, L1, A = "L0_xattn_", "L1_xattn_", "L1_attn_"
    ctxT = a["ctx_1024"].reshape(B * S, D).T.reshape(KT, P, 4, CHUNK).transpose(2, 1, 0, 3)
    wo0 = a[L0 + "wo"].T.reshape(2, 2, G0, D0, D).transpose(0, 2, 1, 3, 4).reshape(H0 * D0, D)
    eye = np.eye(P, dtype=np.float32)
    p = np.arange(P)
    consts = {
        "ident": eye,
        "headmask": ((p % 64) // D1)[:, None] == np.arange(GRP1)[None, :],
        "pairmask": ((p % 32) // D1)[:, None] == np.arange(2)[None, :],
        "theta0": np.where((p // T)[:, None] == (p // T)[None, :], 0.6, FAR),
        "iota": np.tile(np.arange(E1), (P, 1)),
    }
    f = "L1_ffn_"
    gu = np.concatenate([np.concatenate([a[f + "shared_wg"][None], a[f + "experts_wg"]]),
                         np.concatenate([a[f + "shared_wu"][None], a[f + "experts_wu"]])], axis=2)
    rows = {"qn": a[L0 + "q_norm_w"], "kn": a[L0 + "k_norm_w"], "inw": a["L0_attn_input_norm_w"],
            "ffw": a["L0_attn_ff_norm_w"], "rb": a["L0_ffn_router_b"],
            "kv1b": np.concatenate([a[L1 + "bk"], a[L1 + "bv"]]), "bq1": a[L1 + "bq"],
            "bo1": a[L1 + "bo"], "abv": a[A + "bv"], "abo": a[A + "bo"], "gb": a[f + "gate_b"]}
    on_p = lambda v: v.reshape(-1, P).T
    cols = {"alog": on_p(a["L0_attn_a_log"]), "cout": on_p(a["L0_attn_c_out"]),
            "dskip": on_p(a["L0_attn_d_skip"]), "b1": a["L0_ffn_b1"].T, "abq": on_p(a[A + "bq"]),
            "abk": on_p(a[A + "bk"])}
    arrays = {
        "x": a["x"].reshape(B * T, D),
        "ctxT": ctxT,
        "wkv0": by_rows(np.concatenate([a[L0 + "wk"], a[L0 + "wv"]]).T),
        "wkv1": by_rows(np.concatenate([a[L1 + "Wk"], a[L1 + "Wv"]]).T),
        "wq0": by_rows(a[L0 + "wq"].T),
        "wo0": by_rows(wo0),
        "fc": by_rows(a["L0_attn_ff_fc_w"].T),
        "proj": by_rows(a["L0_attn_ff_proj_w"].T),
        "rw0": by_rows(a["L0_ffn_router_w"]),
        "w1": by_rows(a["L0_ffn_W1"].transpose(1, 0, 2).reshape(D, E0 * F0)),
        "w2": a["L0_ffn_W2"].transpose(1, 0, 2),
        "b2": a["L0_ffn_b2"],
        "wq1": by_rows(a[L1 + "Wq"].T),
        "wo1": by_rows(a[L1 + "Wo"].T),
        "watt": np.stack([by_rows(a[A + n].T) for n in ("Wq", "Wk", "Wv", "Wo")], axis=1),
        "gw1": by_rows(a[f + "gate_w"]),
        "wgu": gu.reshape(E1 + 1, KT, P, 2 * F1).transpose(2, 0, 1, 3),
        "wdn": np.concatenate([a[f + "shared_wd"][None], a[f + "experts_wd"]]).transpose(1, 0, 2),
        "rows": np.concatenate([rows[n] for n, _ in ROWS]),
        "cols": np.concatenate([cols[n] for n, _ in COLS], axis=1),
        "consts": np.concatenate([consts[n].astype(np.float32) for n, _ in CONSTS], axis=1),
    }
    nc = _bacc.Bacc("TRN2", target_bir_lowering=False, num_devices=1)
    fed, t = {}, {}
    for name, v in arrays.items():
        fed["in_" + name] = np.ascontiguousarray(v)
        t[name] = nc.dram_tensor("in_" + name, fed["in_" + name].shape, F32, kind="ExternalInput").ap()
    t["out"] = nc.dram_tensor("out", (B * T, D), F32, kind="ExternalOutput").ap()
    build(nc, t)
    r = _run(nc, [fed], core_ids=[0])
    return r.results[0]["out"].reshape(B, T, D)
```

```python
from contextlib import ExitStack

import numpy as np

import concourse.bass as bass
from concourse import mybir

ALU = mybir.AluOpType
ACT = mybir.ActivationFunctionType
AX = mybir.AxisListType
F32 = mybir.dt.float32
F32R = mybir.dt.float32r
U32 = mybir.dt.uint32

P = 128
B, T, D = 2, 64, 256
KT = D // P
S = 1024
NKEY = S // P
NCTX = B * NKEY
CHUNK = 512
H0, HK0, D0 = 16, 4, 64
G0 = H0 // HK0
H1, D1 = 16, 16
GRP1 = P // (2 * D1)
TILES = B * H0 // 2
FF = 512
E0, F0 = 8, 128
E1, F1 = 16, 128
LN_EPS, RMS_EPS = 1e-5, 1e-6
FAR = -1e30

ROWS = [("inw", D), ("ffw", D), ("rb", E0),
        ("bo1", D), ("abv", D), ("abo", D), ("gb", E1)]
COLS = [("alog", KT), ("cout", KT), ("dskip", KT), ("b1", E0), ("abq", KT), ("abk", KT),
        ("bk1", KT), ("bv1", KT), ("bq1", H1 * D1 // 64)]
CONSTS = [("ident", P), ("headmask", GRP1), ("pairmask", 2 * D1), ("theta0", P), ("iota", E1)]


ROOTS = ["lnA", "lnB", "rmB", "rmC", "lnC", "lnD", "lnE", "lnF"]
KEPT = ["lnA", "n2", "lnC", "lnD", "lnE", "lnF"]
TURNS = ["lnA", "normed", "scan_out", "n2", "lnC", "lnD", "lnE", "lnF"]


def nth(order, name):
    return order.index(name) + 1


def offsets(fields):
    at, out = 0, {}
    for name, n in fields:
        out[name] = (at, n)
        at += n
    return out, at


ROW_AT, NROW = offsets(ROWS)
COL_AT, NCOL = offsets(COLS)
CONST_AT, NCONST = offsets(CONSTS)


def build(nc, t):
    with ExitStack() as ctx:
        known = {}

        def sem(name):
            if name not in known:
                known[name] = nc.alloc_semaphore(name=name)
            return known[name]

        base = -(-nc.sbuf_base // 64) * 64
        top = [base]

        def region(nbytes):
            at = top[0]
            top[0] += -(-nbytes // 32) * 32
            return at

        def place(name, shape, dt, at):
            return nc.alloc_sbuf_tensor_at(name, shape, dt, offset=at)

        def new(name, shape, dt=F32):
            return place(name, shape, dt, region(4 * int(np.prod(shape[1:]))))

        r_ctx = region(4 * 2 * KT * B * S + 4 * 4 * KT * 512)
        ctx_hi = place("ctx_hi", [P, KT, B * S], F32R, r_ctx)
        ctx_lo = place("ctx_lo", [P, KT, B * S], F32R, r_ctx + 4 * KT * B * S)
        r_w = r_ctx + 8 * KT * B * S
        wkv_hi = [place(f"wkv_hi{l}", [P, KT, 512], F32R, r_w + l * 8 * KT * 512) for l in range(2)]
        wkv_lo = [place(f"wkv_lo{l}", [P, KT, 512], F32R, r_w + (2 * l + 1) * 4 * KT * 512) for l in range(2)]
        wgu = place("wgu", [P, E1 + 1, KT, 2 * F1], F32, r_ctx)
        watt = place("watt", [P, 4, KT, D], F32, r_ctx + 4 * (E1 + 1) * KT * 2 * F1)
        assert ((E1 + 1) * KT * 2 * F1 + 4 * KT * D) * 4 <= 8 * KT * B * S + 16 * KT * 512

        wo0 = new("wo0", [P, 8, D])
        r_k = region(4 * 4 * B * S)
        kstack = place("kstack", [P, 4, B * S], F32R, r_k)
        wdn = place("wdn", [P, E1 + 1, D], F32, r_k)
        vals = new("vals", [P, NCTX, D])
        r_pt = region(4 * 4 * NKEY * 256)
        pt = place("pt", [P, 4, NKEY, 256], F32, r_pt)
        ctx_raw = place("ctx_raw", [P, 4, KT, CHUNK], F32, r_pt)
        wkv_raw = [place(f"wkv_raw{l}", [P, KT, 512], F32, r_pt + 4 * 4 * KT * CHUNK + l * 4 * KT * 512)
                   for l in range(2)]
        w1 = place("w1", [P, KT, E0 * F0], F32, r_pt)
        w2 = place("w2", [P, E0, D], F32, r_pt + 4 * KT * E0 * F0)
        fc = place("fc", [P, KT, FF], F32, r_pt + 4 * (KT * E0 * F0 + E0 * D))
        proj = place("proj", [P, FF // P, D], F32, r_pt + 4 * (KT * E0 * F0 + E0 * D + KT * FF))
        r_p = region(4 * 3 * S)
        prob = place("prob", [P, 3, S], F32, r_p)
        wq0 = place("wq0", [P, KT, H0 * D0], F32, r_p)
        qstack = [new(f"qstack_{x}", [P, B, H0, T], F32R) for x in ("hi", "lo")]
        rw0 = new("rw0", [P, KT, E0])
        b2 = new("b2", [P, D])
        wq1 = new("wq1", [P, KT, 2 * D])
        wo1 = new("wo1", [P, KT, D])
        gw1 = new("gw1", [P, KT, E1])
        rows = new("rows", [P, NROW])
        qk_w = new("qk_w", [P, 3, D0])
        cols = new("cols", [P, NCOL])
        consts = new("consts", [P, NCONST])
        ksp = new("ksp", [P, 3, 4, 2, 64], F32R)
        kn = new("kn", [P, 3, D])
        ksq = new("ksq", [P, 2, D])
        kss = new("kss", [P, 2, 4])
        kvar = new("kvar", [P, 2, 4])
        krs = new("krs", [P, 2, 4])
        nmx = new("nmx", [P, 2, TILES])
        sums = new("sums", [P, 2, TILES])
        rsum = new("rsum", [P, 4])
        xs = new("xs", [P, D])
        zn = new("zn", [P, D])
        zT = new("zT", [P, KT, P])
        wide = new("wide", [P, 1024])
        q_sb = place("q_sb", [P, H0, D0], F32, r_p + 4 * KT * H0 * D0)
        qdup0 = [place("qdup0_hi", [P, H0, 2, D0], F32R, r_p),
                 place("qdup0_lo", [P, H0, 2, D0], F32R, r_pt + 4 * 4 * KT * CHUNK + 2 * 4 * KT * 512)]
        oT = new("oT", [P, 8, B, T])
        acc = new("acc", [P, D])
        x1 = new("x1", [P, D])
        normed_t = new("normed_sb", [P, D])
        normed = normed_t[:]
        scratch = new("scratch", [P, D])
        inv_all = x1
        routeT = new("routeT_sb", [P, P])
        scan = place("scan_sb", [P, 2, KT, B, T + T // 2], F32, r_p)
        skip = place("skip_sb", [P, KT, B, T], F32, r_p + 4 * 2 * KT * B * 96)
        scan_out_t = place("scan_out_sb", [P, D], F32, r_p + 4 * (2 * KT * B * 96 + D))
        scan_out = scan_out_t[:]
        att = place("att", [P, 6, P], F32, r_p + 4 * 4 * P)
        att_parts, att_theta, att_e, att_p = att[:, 0:3], att[:, 3], att[:, 4], att[:, 5]
        att_pT_t = place("att_pT_sb", [P, P], F32, r_p + 4 * 10 * P)
        att_pT = att_pT_t[:]
        att_v_t = place("att_v_sb", [P, D], F32, r_p + 4 * 11 * P)
        att_v = att_v_t[:]
        sm = new("sm", [P, 400])
        half = new("half", [P, 16])
        hid = place("hid", [P, 2, 2, P], F32, r_p)
        assert top[0] <= nc.sbuf_usable_end, (top[0], nc.sbuf_usable_end)

        banks = [ctx.enter_context(nc.psum_tensor(f"bank{i}", [P, 512], F32)) for i in range(4)]
        wide_ps = [ctx.enter_context(nc.psum_tensor(f"wide{i}", [P, 1024], F32)) for i in range(2)]
        tr_ps = banks[2:4]
        pv_ps = banks[0:2]
        W0, W1_ = wide_ps[0], wide_ps[1]
        bank_a, bank_b, bank_c, bank_d = W0[:, 0:512], W0[:, 512:1024], W1_[:, 0:512], W1_[:, 512:1024]

        def kv_bank(i):
            return banks[i % 4]

        def turn_bank(i):
            return (bank_a, bank_b)[i % 2]

        def k1_piece(n):
            return n % 2, slice((n // 2) * 512, (n // 2 + 1) * 512), banks[n % 2]

        def row(name):
            at, n = ROW_AT[name]
            return rows[:, at:at + n]

        def col(name, i, n=1):
            at = COL_AT[name][0] + i
            return cols[:, at:at + n]

        def const(name):
            at, n = CONST_AT[name]
            return consts[:, at:at + n]

        ident = const("ident")
        q1_sb = wide[:, 0:512].rearrange("p (b g t) -> p (b g) t", g=4, b=B)

        def q1_stack(part, x):
            return qstack[part][:].rearrange("p b (g x) t -> p (b g) x t", x=GRP1)[:, :, x]

        small = {}

        def s_(name, n=1):
            if name not in small:
                small[name] = (sum(k for _, k in small.values()), n)
                assert sum(k for _, k in small.values()) <= 400
            at, n = small[name]
            return sm[:, at:at + n]

        def then(eng, ins, name, n=1):
            ins.then_inc(sem(name), 1)
            eng.wait_ge(sem(name), n)

        block = ctx.enter_context(nc.Block())

        def loaded(eng, name):
            eng.wait_ge(sem("dma_" + name), 16)

        @block.sync
        def _(sp):
            def load(name, dst, src):
                sp.dma_start(dst, src).then_inc(sem("dma_" + name), 16)

            load("x", xs[:], t["x"])
            load("wkv0", wkv_raw[0][:], t["wkv0"])
            load("ctx0", ctx_raw[:, 0], t["ctxT"][0])
            load("consts", consts[:], t["consts"])
            load("ctx1", ctx_raw[:, 1], t["ctxT"][1])
            load("wq0", wq0[:], t["wq0"])
            load("qk_w", qk_w[:, 0:2], t["qk_rows"].partition_broadcast(P))
            load("ctx2", ctx_raw[:, 2], t["ctxT"][2])
            load("ctx3", ctx_raw[:, 3], t["ctxT"][3])
            load("wkv1", wkv_raw[1][:], t["wkv1"])
            load("cols", cols[:], t["cols"])
            load("rows", rows[:], t["rows"].partition_broadcast(P))
            load("wo0", wo0[:], t["wo0"])
            load("rw0", rw0[:], t["rw0"])
            load("b2", b2[0:E0, :], t["b2"])
            load("wq1", wq1[:], t["wq1"])
            load("wo1", wo1[:], t["wo1"])
            load("gw1", gw1[:], t["gw1"])
            sp.wait_ge(sem("pv0"), 4)
            load("fc", fc[:], t["fc"])
            load("proj", proj[:], t["proj"])
            load("w1", w1[:], t["w1"])
            load("w2", w2[:], t["w2"])
            sp.wait_ge(sem("k1_mm"), 8)
            sp.wait_ge(sem("v1_mm"), 8)
            load("watt", watt[:], t["watt"])
            load("wgu0", wgu[:, 0:8], t["wgu"][:, 0:8])
            load("wgu1", wgu[:, 8:17], t["wgu"][:, 8:17])
            sp.wait_ge(sem("score1"), TILES)
            load("wdn", wdn[:], t["wdn"])
            sp.wait_ge(sem("x_final"), 1)
            sp.dma_start(t["out"], xs[:]).then_inc(sem("stored"), 16)
            sp.wait_ge(sem("stored"), 16)

        @block.gpsimd
        def _(pool):
            then(pool, pool.memset(half[:], -0.5), "half_set")

            def rsqrt(name, n=1):
                pool.wait_ge(sem("var"), nth(ROOTS, name))
                pool.tensor_tensor(s_(name + "_rs", n), s_(name + "_ve", n), half[:, 0:n],
                                   ALU.pow).then_inc(sem("root"), 1)

            def key_rsqrt(i):
                pool.wait_ge(sem("kvar"), i + 1)
                if i >= 2:
                    pool.wait_ge(sem("kn0"), i - 1)
                pool.tensor_tensor(krs[:, i % 2], kvar[:, i % 2], half[:, 0:4],
                                   ALU.pow).then_inc(sem("krs"), 1)

            def ctx_lo_part(c):
                c, hf = divmod(c, 2)
                pool.wait_ge(sem("ctx_hi"), c + 1)
                n = CHUNK // 2
                sl = slice(c * CHUNK + hf * n, c * CHUNK + (hf + 1) * n)
                pool.tensor_tensor(ctx_lo[:, :, sl], ctx_raw[:, c, :, hf * n:(hf + 1) * n],
                                   ctx_hi[:, :, sl].bitcast(F32), ALU.subtract).then_inc(sem("ctx_lo_pool"), 1)

            rsqrt("lnA")
            key_rsqrt(0)
            key_rsqrt(1)
            ctx_lo_part(4)
            key_rsqrt(2)
            key_rsqrt(3)
            ctx_lo_part(5)
            key_rsqrt(4)
            pool.wait_ge(sem("q_var"), 1)
            for n in range(4):
                pool.tensor_tensor(s_("q0_rs", 16)[:, 4 * n:4 * n + 4], s_("q0_ve", 16)[:, 4 * n:4 * n + 4],
                                   half[:, 0:4], ALU.pow).then_inc(sem("q_root"), 1)
                key_rsqrt(5 + n)
            ctx_lo_part(6)
            key_rsqrt(9)
            ctx_lo_part(7)
            for i in range(10, NCTX):
                key_rsqrt(i)
            pool.wait_ge(sem("wkv_split1"), 1)
            pool.tensor_tensor(wkv_lo[1][:], wkv_raw[1][:], wkv_hi[1][:].bitcast(F32),
                               ALU.subtract).then_inc(sem("wkv_split1"), 1)

            for name in ("lnB", "rmB", "rmC", "lnC", "lnD"):
                rsqrt(name)
            rsqrt("lnE")
            rsqrt("lnF")

        @block.tensor
        def _(pe):
            def kv_mm(i):
                c = i // 4
                if i % 4 == 0 and c < 2:
                    pe.wait_ge(sem("ctx_lo_dve"), c + 1)
                if i % 2 == 0 and c >= 2:
                    pe.wait_ge(sem("ctx_lo_pool"), i // 2 - 3)
                if i == 0:
                    pe.wait_ge(sem("wkv_split0"), 2)
                if i >= 4:
                    pe.wait_ge(sem("kn0"), i - 3)
                    pe.wait_ge(sem("v0"), i - 3)
                sl = slice(i * P, (i + 1) * P)
                parts = [(ctx_hi, wkv_hi[0]), (ctx_lo, wkv_hi[0]), (ctx_hi, wkv_lo[0])]
                for n, (a, w) in enumerate(parts):
                    for k in range(KT):
                        mm = pe.matmul(kv_bank(i)[:], a[:, k, sl], w[:, k, :],
                                       start=(n == 0 and k == 0), stop=(n == 2 and k == KT - 1))
                mm.then_inc(sem("kv_mm0"), 1)

            def k1_mm(n):
                ft, keys, bank = k1_piece(n)
                if n == 0:
                    pe.wait_ge(sem("wkv_split1"), 2)
                if n >= 2:
                    pe.wait_ge(sem("klo1"), 2 * (n - 1))
                else:
                    pe.wait_ge(sem("pv_read0"), 4)
                fs = slice(ft * P, (ft + 1) * P)
                parts = [(wkv_hi[1], ctx_hi), (wkv_lo[1], ctx_hi), (wkv_hi[1], ctx_lo)]
                for m, (w, x) in enumerate(parts):
                    for k in range(KT):
                        mm = pe.matmul(bank[:], w[:, k, fs], x[:, k, keys],
                                       start=(m == 0 and k == 0), stop=(m == 2 and k == KT - 1))
                mm.then_inc(sem("k1_mm"), 1)

            def v1_mm(n):
                if n == 0:
                    pe.wait_ge(sem("wkv_split1"), 2)
                if n >= 2:
                    pe.wait_ge(sem("v1"), n - 1)
                else:
                    pe.wait_ge(sem("pt_even0"), TILES)
                    pe.wait_ge(sem("pt_odd0"), TILES)
                parts = [(ctx_hi, wkv_hi[1]), (ctx_lo, wkv_hi[1]), (ctx_hi, wkv_lo[1])]
                for j in range(2):
                    i = 2 * n + j
                    for m, (x, w) in enumerate(parts):
                        for k in range(KT):
                            mm = pe.matmul(banks[2 + n % 2][:, j * D:(j + 1) * D], x[:, k, i * P:(i + 1) * P],
                                           w[:, k, D:2 * D], start=(m == 0 and k == 0),
                                           stop=(m == 2 and k == KT - 1))
                mm.then_inc(sem("v1_mm"), 1)

            def k_turn(i):
                pe.wait_ge(sem("ksplit0"), i + 1)
                if i >= 2:
                    pe.wait_ge(sem("kstack0"), i - 1)
                elif i == 0:
                    pe.wait_ge(sem("kept"), nth(KEPT, "lnA"))
                for h in range(4):
                    mm = pe.transpose(turn_bank(i)[:, h * P:(h + 1) * P],
                                      ksp[:, i % 3, h].bitcast(F32), ident)
                mm.then_inc(sem("k_turn0"), 1)

            def turn(name, src, dst_ps):
                pe.wait_ge(sem("turn_in"), nth(TURNS, name))
                for k in range(KT):
                    mm = pe.transpose(dst_ps[:, k * P:(k + 1) * P], src[:, k * P:(k + 1) * P], ident)
                mm.then_inc(sem("turned"), 1)

            def q_turn(part, n):
                slot = 4 * part + n
                pe.wait_ge(sem("q_split0"), part + 1)
                if slot >= 2:
                    pe.wait_ge(sem("q_stacked0"), slot - 1)
                for j in range(4):
                    mm = pe.transpose((bank_c, bank_d)[slot % 2][:, j * P:(j + 1) * P],
                                      qdup0[part][:, 4 * n + j].bitcast(F32).rearrange("p x d -> p (x d)"),
                                      ident)
                mm.then_inc(sem("q_turn0"), 1)

            def score(l, i):
                b, r = divmod(i, TILES // B)
                if i == 0 and l == 0:
                    pe.wait_ge(sem("kstack0"), NCTX)
                    pe.wait_ge(sem("q_stacked0"), 8)
                if i == 0 and l == 1:
                    pe.wait_ge(sem("klo1"), 16)
                if i < 2 and l == 1:
                    pe.wait_ge(sem("q1_lo"), 2 * i + 2)
                if i >= 2:
                    pe.wait_ge(sem(f"exp{l}"), i - 1)
                h = 2 * r
                grp = h // 4
                for part in range(2):
                    for c in range(S // 512):
                        mm = pe.matmul(wide_ps[i % 2][:, c * 512:(c + 1) * 512],
                                       qstack[part][:, b, h:h + 2, :],
                                       kstack[:, grp, b * S + c * 512:b * S + (c + 1) * 512],
                                       start=(part == 0), stop=(part == 1))
                mm.then_inc(sem(f"score{l}"), 1)

            def p_turn(l, i):
                pe.wait_ge(sem(f"exp{l}"), i + 1)
                for hf in range(2):
                    if i >= 1:
                        pe.wait_ge(sem(f"pt_{('even', 'odd')[hf]}{l}"), i)
                    else:
                        pe.wait_ge(sem(("kstack0", "v1")[l]), (NCTX, 8)[l])
                    for j in range(4):
                        kt = 4 * hf + j
                        mm = pe.transpose(tr_ps[hf][:, j * P:(j + 1) * P],
                                          prob[:, i % 3, kt * P:(kt + 1) * P], ident)
                    mm.then_inc(sem(f"p_turn{l}"), 1)

            def inv_spread(l, g):
                pe.wait_ge(sem(f"inv_sum{l}"), g + 1)
                if g >= 2:
                    pe.wait_ge(sem(f"pv_read{l}"), g - 1)
                elif g == 0 and l == 0:
                    pe.wait_ge(sem("v0"), NCTX)
                    pe.wait_ge(sem("kn0"), NCTX)
                for j in range(4):
                    if l == 0:
                        half = slice(D0 * (j // 2), D0 * (j // 2 + 1))
                        out = pv_ps[g % 2][half, 256 + (j % 2) * P:256 + (j % 2 + 1) * P]
                        inv = acc[:, D0 * j:D0 * (j + 1)]
                    else:
                        out = pv_ps[g % 2][32 * j:32 * j + 32, 256:256 + P]
                        inv = acc[:, 32 * j:32 * j + 32]
                    mm = pe.matmul(out, inv, ident, start=True, stop=True)
                mm.then_inc(sem(f"inv_spread{l}"), 1)

            def pv(l, g, part):
                pe.wait_ge(sem(f"pt_even{l}"), 4 * g + 4)
                pe.wait_ge(sem(f"pt_odd{l}"), 4 * g + 4)
                b, hf = divmod(g, 2)
                for kt in range(2 * part, 2 * part + 2):
                    v = vals[:, b * NKEY + kt, :]
                    if l == 0:
                        for j in range(2):
                            mm = pe.matmul(pv_ps[g % 2][64 * j:64 * j + 64, 0:256],
                                           v[:, (2 * hf + j) * D0:(2 * hf + j + 1) * D0],
                                           pt[:, (2 * g + j) % 4, kt, :],
                                           start=(kt == 0), stop=(kt == NKEY - 1))
                    else:
                        for j in range(4):
                            f = P * hf + 32 * j
                            mm = pe.matmul(pv_ps[g % 2][32 * j:32 * j + 32, 0:P], v[:, f:f + 32],
                                           pt[:, (2 * g + j // 2) % 4, kt, (j % 2) * P:(j % 2 + 1) * P],
                                           start=(kt == 0), stop=(kt == NKEY - 1))
                if part == 3:
                    mm.then_inc(sem(f"pv{l}"), 1)

            def attention(l):
                for i in range(TILES + 6):
                    if i < TILES:
                        score(l, i)
                    if 2 <= i < TILES + 2:
                        p_turn(l, i - 2)
                    if i >= 6:
                        g, part = divmod(i - 6, 4)
                        if part == 0:
                            inv_spread(l, g)
                        pv(l, g, part)

            def linear(out, lhs, rhs, n):
                for k in range(n):
                    mm = pe.matmul(out, lhs(k), rhs(k), start=(k == 0), stop=(k == n - 1))
                return mm

            loaded(pe, "consts")
            turn("lnA", zn, bank_a)
            for i in range(2):
                kv_mm(i)
            pe.wait_ge(sem("kept"), nth(KEPT, "lnA"))
            loaded(pe, "wq0")
            for n in range(2):
                mm = linear(W1_[:, n * 512:(n + 1) * 512], lambda k: zT[:, k, :],
                            lambda k: wq0[:, k, n * 512:(n + 1) * 512], KT)
            mm.then_inc(sem("q0_mm"), 1)
            for i in range(2, NCTX + 3):
                if i < NCTX:
                    kv_mm(i)
                if i >= 3:
                    k_turn(i - 3)
                if i >= 12 and i < 16:
                    q_turn((i - 12) // 2, 2 * (i % 2))
                    q_turn((i - 12) // 2, 2 * (i % 2) + 1)

            attention(0)

            v1_mm(0)
            pe.wait_ge(sem("pv_read0"), 4)
            loaded(pe, "wo0")
            linear(bank_a[:, 0:D], lambda k: oT[:, k].rearrange("p b t -> p (b t)"),
                   lambda k: wo0[:, k, :], 8).then_inc(sem("out0_mm"), 1)
            v1_mm(1)
            k1_mm(0)
            k1_mm(1)
            turn("normed", normed, bank_c)
            for n in range(2, 6):
                v1_mm(n)
            turn("scan_out", scan_out, bank_a)
            k1_mm(2)
            turn("n2", normed, bank_c)
            pe.wait_ge(sem("kept"), nth(KEPT, "n2"))
            loaded(pe, "fc")
            for j in range(FF // P):
                mm = linear(bank_b[:, j * P:(j + 1) * P], lambda k: fc[:, k, j * P:(j + 1) * P],
                            lambda k: zT[:, k, :], KT)
            mm.then_inc(sem("ff_h"), 1)
            k1_mm(3)
            pe.wait_ge(sem("ff_act"), 1)
            loaded(pe, "proj")
            linear(bank_d[:, 0:D], lambda k: wide[:, k * P:(k + 1) * P], lambda k: proj[:, k, :],
                   FF // P).then_inc(sem("ff_out"), 1)
            k1_mm(4)
            turn("lnC", zn, bank_a)
            pe.wait_ge(sem("kept"), nth(KEPT, "lnC"))
            loaded(pe, "rw0")
            linear(bank_b[:, 0:E0], lambda k: zT[:, k, :], lambda k: rw0[:, k, :],
                   KT).then_inc(sem("router_mm"), 1)
            loaded(pe, "w1")
            for e in range(E0):
                mm = linear((bank_c, bank_d)[e // 4][:, (e % 4) * P:(e % 4 + 1) * P],
                            lambda k: w1[:, k, e * F0:(e + 1) * F0], lambda k: zT[:, k, :], KT)
                if e % 4 == 3:
                    mm.then_inc(sem("moe_h"), 1)
            k1_mm(5)
            pe.wait_ge(sem("route0"), 1)
            pe.transpose(bank_a[0:E0, 0:P], s_("route0", E0), ident).then_inc(sem("route_turn"), 1)
            pe.wait_ge(sem("routeT"), 1)
            loaded(pe, "b2")
            pe.matmul(bank_b[:, 0:D], routeT[0:E0, :], b2[0:E0, :], start=True,
                      stop=True).then_inc(sem("moe_b2"), 1)
            loaded(pe, "w2")
            for n in range(E0 // 2):
                if n == 1:
                    pe.wait_ge(sem("moe_acc"), 1)
                pe.wait_ge(sem("moe_act"), E0 if n >= 2 else 2 * n + 2)
                for j in range(2):
                    e = 2 * n + j
                    mm = pe.matmul((bank_a, bank_b, bank_c, bank_d)[n][:, j * D:(j + 1) * D],
                                   wide[:, e * P:(e + 1) * P], w2[:, e, :], start=True, stop=True)
                mm.then_inc(sem("moe_out"), 1)
            v1_mm(6)
            v1_mm(7)
            k1_mm(6)
            k1_mm(7)
            turn("lnD", zn, bank_a)
            pe.wait_ge(sem("kept"), nth(KEPT, "lnD"))
            loaded(pe, "wq1")
            for g in range(4):
                mm = linear(bank_b[:, g * P:(g + 1) * P], lambda k: wq1[:, k, g * P:(g + 1) * P],
                            lambda k: zT[:, k, :], KT)
            mm.then_inc(sem("q1_mm"), 1)

            attention(1)

            pe.wait_ge(sem("pv_read1"), 4)
            loaded(pe, "wo1")
            linear(bank_a[:, 0:D], lambda k: oT[:, k].rearrange("p b t -> p (b t)"),
                   lambda k: wo1[:, k, :], KT).then_inc(sem("out1_mm"), 1)

            turn("lnE", zn, bank_c)
            pe.wait_ge(sem("kept"), nth(KEPT, "lnE"))
            loaded(pe, "watt")
            for j in range(2 * KT):
                mm = linear(bank_b[:, j * P:(j + 1) * P],
                            lambda k: watt[:, j // KT, k, (j % KT) * P:(j % KT + 1) * P],
                            lambda k: zT[:, k, :], KT)
            mm.then_inc(sem("att_qk"), 1)
            linear(bank_d[:, 0:D], lambda k: zT[:, k, :], lambda k: watt[:, 2, k, :],
                   KT).then_inc(sem("att_v"), 1)
            pe.wait_ge(sem("att_qk_sb"), 4)
            linear(bank_a[:, 0:P], lambda k: wide[:, k * P:(k + 1) * P],
                   lambda k: wide[:, (2 + k) * P:(3 + k) * P], KT).then_inc(sem("att_s"), 1)
            pe.wait_ge(sem("att_p"), 1)
            pe.transpose(bank_c[:, 0:P], att_p, ident).then_inc(sem("att_p_turn"), 1)
            pe.wait_ge(sem("att_pT"), 1)
            for m in range(KT):
                mm = pe.matmul(bank_b[:, m * P:(m + 1) * P], att_v[:, m * P:(m + 1) * P],
                               att_pT, start=True, stop=True)
            mm.then_inc(sem("att_o"), 1)
            pe.wait_ge(sem("att_oT"), 1)
            linear(bank_d[:, 0:D], lambda k: zT[:, k, :], lambda k: watt[:, 3, k, :],
                   KT).then_inc(sem("att_out"), 1)

            turn("lnF", zn, bank_a)
            pe.wait_ge(sem("kept"), nth(KEPT, "lnF"))
            loaded(pe, "gw1")
            linear(bank_b[:, 0:E1], lambda k: zT[:, k, :], lambda k: gw1[:, k, :],
                   KT).then_inc(sem("gate_mm"), 1)
            for n in range(E1 + 3):
                if n <= E1:
                    loaded(pe, "wgu0" if n < 8 else "wgu1")
                    if n >= 2:
                        pe.wait_ge(sem("exp_h"), n - 1)
                    for gu in range(2):
                        mm = linear(banks[n % 2][:, gu * P:(gu + 1) * P],
                                    lambda k: wgu[:, n, k, gu * F1:(gu + 1) * F1],
                                    lambda k: zT[:, k, :], KT)
                    mm.then_inc(sem("exp_gu"), 1)
                if n >= 2:
                    m = n - 2
                    if m == 0:
                        loaded(pe, "wdn")
                    pe.wait_ge(sem("exp_h"), m + 1)
                    if m >= 2:
                        pe.wait_ge(sem("exp_sum"), m - 1)
                    pe.matmul(banks[2 + m % 2][:, 0:D], hid[:, m % 2, 1, :], wdn[:, m, :],
                              start=True, stop=True).then_inc(sem("exp_dn"), 1)

        @block.scalar
        def _(act):
            def v_copy(i):
                act.wait_ge(sem("kv_mm0"), i + 1)
                if i >= 2:
                    act.wait_ge(sem("kss"), i - 1)
                act.activation(ksq[:, i % 2], kv_bank(i)[:, 0:D], ACT.Square).then_inc(sem("ksq"), 1)
                act.activation(vals[:, i], kv_bank(i)[:, D:2 * D], ACT.Copy).then_inc(sem("v0"), 1)

            def k_hi(i):
                act.wait_ge(sem("kn0"), i + 1)
                if i >= 3:
                    act.wait_ge(sem("k_turn0"), i - 2)
                act.activation(ksp[:, i % 3, :, 0, :], kn[:, i % 3].rearrange("p (h d) -> p h d", h=4),
                               ACT.Copy).then_inc(sem("khi0"), 1)

            def k_stack(i):
                act.wait_ge(sem("k_turn0"), i + 1)
                act.activation(kstack[:, :, i * P:(i + 1) * P],
                               turn_bank(i).rearrange("p (h k) -> p h k", h=4),
                               ACT.Copy).then_inc(sem("kstack0"), 1)

            def k1_hi(n):
                ft, keys, bank = k1_piece(n)
                act.wait_ge(sem("k1_mm"), n + 1)
                for half in range(2):
                    rows_ = slice(64 * half, 64 * half + 64)
                    act.activation(kstack[rows_, 2 * ft + half, keys], bank[rows_, :], ACT.Identity,
                                   bias=cols[rows_, COL_AT["bk1"][0] + ft:COL_AT["bk1"][0] + ft + 1]
                                   ).then_inc(sem("khi1"), 1)

            def v1_copy(n):
                act.wait_ge(sem("v1_mm"), n + 1)
                if n == 0:
                    act.wait_ge(sem("pv0"), 4)
                act.activation(vals[:, 2 * n:2 * n + 2, :],
                               banks[2 + n % 2][:].rearrange("p (j d) -> p j d", j=2),
                               ACT.Copy).then_inc(sem("v1"), 1)

            def q_stack(slot):
                part, n = divmod(slot, 4)
                act.wait_ge(sem("q_turn0"), slot + 1)
                act.activation(qstack[part][:, :, 4 * n:4 * n + 4, :],
                               (bank_c, bank_d)[slot % 2].rearrange("p (h b t) -> p b h t", h=4, b=B),
                               ACT.Copy).then_inc(sem("q_stacked0"), 1)

            def ctx_hi_part(c):
                loaded(act, f"ctx{c}")
                act.activation(ctx_hi[:, :, c * CHUNK:(c + 1) * CHUNK], ctx_raw[:, c],
                               ACT.Copy).then_inc(sem("ctx_hi"), 1)

            def exp(l, i):
                act.wait_ge(sem(f"nmx{l}"), i + 1)
                if i >= 3:
                    act.wait_ge(sem(f"p_turn{l}"), 2 * (i - 2))
                act.activation(prob[:, i % 3], wide_ps[i % 2][:], ACT.Exp, bias=nmx[:, l, i:i + 1],
                               accum_out=sums[:, l, i:i + 1]).then_inc(sem(f"exp{l}"), 1)

            def pt_even(l, i):
                act.wait_ge(sem(f"p_turn{l}"), 2 * i + 1)
                if l == 0 and i == 4:
                    act.wait_ge(sem("wkv_split1"), 2)
                if i >= 8 and i % 4 == 0:
                    act.wait_ge(sem(f"pv{l}"), i // 4 - 1)
                act.activation(pt[:, (i // 2) % 4, 0:4, (i % 2) * P:(i % 2 + 1) * P],
                               tr_ps[0][:].rearrange("p (k q) -> p k q", k=4),
                               ACT.Copy).then_inc(sem(f"pt_even{l}"), 1)

            def attention(l):
                for i in range(TILES + 2):
                    if i >= 2:
                        pt_even(l, i - 2)
                    if i < TILES:
                        exp(l, i)

            loaded(act, "wkv0")
            act.activation(wkv_hi[0][:], wkv_raw[0][:], ACT.Copy).then_inc(sem("wkv_split0"), 1)
            ctx_hi_part(0)
            ctx_hi_part(1)
            for i in range(NCTX + 3):
                if i < NCTX:
                    v_copy(i)
                if 1 <= i <= NCTX:
                    k_hi(i - 1)
                if i >= 3:
                    k_stack(i - 3)
                if i == 1:
                    act.wait_ge(sem("q0_mm"), 1)
                    act.activation(wide[:], W1_[:], ACT.Square).then_inc(sem("q_sq"), 1)
                if i == 2:
                    ctx_hi_part(2)
                if i == 5:
                    ctx_hi_part(3)
                if i == 11:
                    act.wait_ge(sem("q_ready"), 1)
                    act.activation(qdup0[0][:], q_sb[:].unsqueeze(2).to_broadcast([P, H0, 2, D0]),
                                   ACT.Copy).then_inc(sem("q_split0"), 1)
                if 12 <= i < 16:
                    q_stack(2 * (i - 12))
                    q_stack(2 * (i - 12) + 1)
            loaded(act, "wkv1")
            act.activation(wkv_hi[1][:], wkv_raw[1][:], ACT.Copy).then_inc(sem("wkv_split1"), 1)
            loaded(act, "cols")
            then(act, act.activation(s_("ea", KT), cols[:, 0:KT], ACT.Exp), "decay")
            act.activation(s_("pow", 12)[:, 0:KT], s_("ea", KT), ACT.Exp, scale=-1.0).then_inc(sem("decay"), 1)

            attention(0)

            v1_copy(0)
            v1_copy(1)
            k1_hi(0)
            k1_hi(1)
            for n in range(2, 6):
                v1_copy(n)
            k1_hi(2)
            act.wait_ge(sem("ff_h"), 1)
            act.activation(wide[:, 0:FF], bank_b, ACT.Tanh, scale=0.5).then_inc(sem("ff_tanh"), 1)
            k1_hi(3)
            k1_hi(4)
            act.wait_ge(sem("r_nmax"), 1)
            act.activation(s_("r_exp", E0), s_("r_logit", E0), ACT.Exp, bias=s_("r_nmax"),
                           accum_out=s_("r_sum")).then_inc(sem("r_exp"), 1)
            for e in range(E0):
                act.wait_ge(sem("moe_h"), e // 4 + 1)
                act.activation(wide[:, e * P:(e + 1) * P], (bank_c, bank_d)[e // 4][:, (e % 4) * P:(e % 4 + 1) * P],
                               ACT.Gelu, bias=col("b1", e)).then_inc(sem("moe_act"), 1)
            k1_hi(5)
            v1_copy(6)
            v1_copy(7)
            k1_hi(6)
            k1_hi(7)
            act.wait_ge(sem("q1_sb"), 1)
            for x in range(GRP1):
                act.activation(q1_stack(0, x), q1_sb, ACT.Copy,
                               scale=const("headmask")[:, x:x + 1]).then_inc(sem("q1_hi"), 1)

            attention(1)

            act.wait_ge(sem("att_s"), 1)
            for n, (func, scale) in enumerate(((ACT.Tanh, 0.5), (ACT.Tanh, 1.0), (ACT.Relu, 1.0))):
                act.activation(att_parts[:, n, :], bank_a[:, 0:P], func,
                               scale=scale).then_inc(sem("att_parts"), 1)
            act.wait_ge(sem("att_nmax"), 1)
            act.activation(att_e, att_theta, ACT.Exp, bias=s_("att_nmax"),
                           accum_out=s_("att_sum")).then_inc(sem("att_exp"), 1)
            act.wait_ge(sem("g_logit"), 1)
            act.activation(s_("g_tanh", E1), s_("g_logit", E1), ACT.Tanh, scale=0.5).then_inc(sem("g_tanh"), 1)
            for n in range(E1 + 1):
                act.wait_ge(sem("exp_gu"), n + 1)
                if n >= 2:
                    act.wait_ge(sem("exp_h"), n - 1)
                act.activation(hid[:, n % 2, 0, :], banks[n % 2][:, 0:P], ACT.Tanh,
                               scale=0.5).then_inc(sem("exp_tanh"), 1)

        @block.vector
        def _(dve):
            count = [0]

            def link(ins):
                count[0] += 1
                ins.then_inc(sem("dve_link"), 1)
                dve.wait_ge(sem("dve_link"), count[0])

            def layer_norm(name, src):
                link(dve.bn_stats(s_("bn", 6), src))
                link(dve.bn_aggr(s_(name + "_mv", 2), s_("bn", 6)))
                dve.tensor_scalar(s_(name + "_ve"), s_(name + "_mv", 2)[:, 1:2], LN_EPS, None,
                                  ALU.add).then_inc(sem("var"), 1)
                dve.wait_ge(sem("root"), nth(ROOTS, name))
                ins = dve.tensor_scalar(zn[:], src, s_(name + "_mv", 2)[:, 0:1], s_(name + "_rs"),
                                        ALU.subtract, ALU.mult)
                if name == "lnB":
                    link(ins)
                else:
                    then(dve, ins, "turn_in", nth(TURNS, name))

            def rms(name, src, out, weight, meanwhile=None):
                link(dve.tensor_tensor_reduce(scratch[:], src, src, 1.0, 0.0, ALU.mult, ALU.add,
                                              s_(name + "_ss")))
                dve.tensor_scalar(s_(name + "_ve"), s_(name + "_ss"), 1.0 / D, RMS_EPS, ALU.mult,
                                  ALU.add).then_inc(sem("var"), 1)
                if meanwhile is not None:
                    meanwhile()
                dve.wait_ge(sem("root"), nth(ROOTS, name))
                return dve.scalar_tensor_tensor(out, src, s_(name + "_rs"), weight, ALU.mult, ALU.mult)

            def keep_turned(name, ps):
                dve.wait_ge(sem("turned"), nth(TURNS, name))
                dve.tensor_copy(zT[:].rearrange("p k n -> p (k n)"), ps[:, 0:2 * P]
                                ).then_inc(sem("kept"), 1)

            def low(lo, src, hi, name):
                dve.tensor_tensor(lo, src, hi.bitcast(F32), ALU.subtract).then_inc(sem(name), 1)

            def key_var(i):
                dve.wait_ge(sem("ksq"), i + 1)
                then(dve, dve.tensor_reduce(kss[:, i % 2], ksq[:, i % 2].rearrange("p (h d) -> p h d", h=4),
                                            AX.X, ALU.add), "kss", i + 1)
                if i >= 2:
                    dve.wait_ge(sem("krs"), i - 1)
                dve.tensor_scalar(kvar[:, i % 2], kss[:, i % 2], 1.0 / D0, RMS_EPS, ALU.mult,
                                  ALU.add).then_inc(sem("kvar"), 1)

            def key_scale(i):
                dve.wait_ge(sem("krs"), i + 1)
                dve.wait_ge(sem("v0"), i + 1)
                dve.tensor_tensor(kn[:, i % 3].rearrange("p (h d) -> p h d", h=4),
                                  kv_bank(i)[:, 0:D].rearrange("p (h d) -> p h d", h=4),
                                  krs[:, i % 2].unsqueeze(2).to_broadcast([P, 4, D0]),
                                  ALU.mult).then_inc(sem("kn0"), 1)

            def key_lo(i):
                dve.wait_ge(sem("khi0"), i + 1)
                low(ksp[:, i % 3, :, 1, :], kn[:, i % 3].rearrange("p (h d) -> p h d", h=4),
                    ksp[:, i % 3, :, 0, :], "ksplit0")

            def k1_lo(n):
                n, half = divmod(n, 2)
                ft, keys, bank = k1_piece(n)
                dve.wait_ge(sem("khi1"), 2 * n + 1 + half)
                if half == 0:
                    dve.wait_ge(sem("khi1"), 2 * n + 2)
                rows_, other = slice(64 * half, 64 * half + 64), slice(64 - 64 * half, 128 - 64 * half)
                dve.scalar_tensor_tensor(kstack[other, 2 * ft + half, keys], bank[rows_, :],
                                         cols[rows_, COL_AT["bk1"][0] + ft:COL_AT["bk1"][0] + ft + 1],
                                         kstack[rows_, 2 * ft + half, keys].bitcast(F32),
                                         ALU.add, ALU.subtract).then_inc(sem("klo1"), 1)

            def row_max(l, i):
                dve.wait_ge(sem(f"score{l}"), i + 1)
                dve.tensor_reduce(nmx[:, l, i:i + 1], wide_ps[i % 2][:], AX.X, ALU.max,
                                  negate=True).then_inc(sem(f"nmx{l}"), 1)

            def inv_sum(l, g):
                dve.wait_ge(sem(f"exp{l}"), 4 * g + 4)
                if g >= 1:
                    dve.wait_ge(sem(f"inv_spread{l}"), g)
                link(dve.reciprocal(rsum[:], sums[:, l, 4 * g:4 * g + 4]))
                if l == 0:
                    ins = dve.tensor_copy(acc[:].rearrange("p (j d) -> p j d", j=4),
                                          rsum[:].unsqueeze(2).to_broadcast([P, 4, D0]))
                else:
                    ins = dve.tensor_tensor(acc[:, 0:P].rearrange("p (j d) -> p j d", j=4),
                                            rsum[:].unsqueeze(2).to_broadcast([P, 4, 2 * D1]),
                                            const("pairmask").unsqueeze(1).to_broadcast([P, 4, 2 * D1]),
                                            ALU.mult)
                ins.then_inc(sem(f"inv_sum{l}"), 1)

            def pt_odd(l, i):
                dve.wait_ge(sem(f"p_turn{l}"), 2 * i + 2)
                if l == 0 and i == 4:
                    dve.wait_ge(sem("wkv_split1"), 2)
                if i >= 8 and i % 4 == 0:
                    dve.wait_ge(sem(f"pv{l}"), i // 4 - 1)
                dve.tensor_copy(pt[:, (i // 2) % 4, 4:8, (i % 2) * P:(i % 2 + 1) * P],
                                tr_ps[1][:].rearrange("p (k q) -> p k q", k=4)
                                ).then_inc(sem(f"pt_odd{l}"), 1)

            def pv_read(l, g):
                dve.wait_ge(sem(f"pv{l}"), g + 1)
                b, hf = divmod(g, 2)
                if g >= 1:
                    dve.wait_ge(sem(f"pv_read{l}"), g)
                then(dve, dve.tensor_copy(inv_all[:, 0:(256, P)[l]], pv_ps[g % 2][:, 256:256 + (256, P)[l]]),
                     "inv_all", 4 * l + g + 1)
                if l == 0:
                    dve.tensor_tensor(oT[:, 4 * hf:4 * hf + 4, b, :],
                                      pv_ps[g % 2][:, 0:256].rearrange("p (g t) -> p g t", g=4),
                                      inv_all[:].rearrange("p (g t) -> p g t", g=4),
                                      ALU.mult).then_inc(sem("pv_read0"), 1)
                else:
                    link(dve.tensor_tensor(scratch[:, 0:P], pv_ps[g % 2][:, 0:P], inv_all[:, 0:P], ALU.mult))
                    then(dve, dve.scalar_tensor_tensor(oT[:, hf, b, :], scratch[:, 0:T], col("bv1", hf),
                                                       scratch[:, T:2 * T], ALU.add, ALU.add),
                         "pv_read1", g + 1)

            def attention(l):
                for i in range(TILES + 7):
                    if i < TILES:
                        row_max(l, i)
                    if 2 <= i < TILES + 2:
                        pt_odd(l, i - 2)
                    if i >= 5 and i % 4 == 1 and i < TILES + 4:
                        inv_sum(l, (i - 5) // 4)
                    if i >= 10 and i % 4 == 2:
                        pv_read(l, (i - 10) // 4)

            def residual(ps, name, bias=None):
                dve.wait_ge(sem(name), 1)
                if bias is not None:
                    link(dve.tensor_tensor(acc[:], ps, bias, ALU.add))
                    link(dve.tensor_tensor(xs[:], xs[:], acc[:], ALU.add))
                else:
                    link(dve.tensor_tensor(xs[:], xs[:], ps, ALU.add))

            def route(name, values, n, factor):
                top, idx, w = s_(name + "_top", 8), s_(name + "_idx", 8), s_(name + "_w", 2)
                link(dve.max(top, values))
                link(dve.max_index(idx.bitcast(U32), top, values))
                link(dve.tensor_copy(s_(name + "_at", 2), idx[:, 0:2].bitcast(U32)))
                link(dve.tensor_tensor(s_(name + "_s"), top[:, 0:1], top[:, 1:2], ALU.add))
                link(dve.reciprocal(s_(name + "_r"), s_(name + "_s")))
                link(dve.tensor_scalar(w, top[:, 0:2], s_(name + "_r"), factor, ALU.mult, ALU.mult))
                at = s_(name + "_at", 2)
                link(dve.tensor_scalar(s_(name + "_a", n), const("iota")[:, 0:n], at[:, 0:1], w[:, 0:1],
                                       ALU.is_equal, ALU.mult))
                link(dve.tensor_scalar(s_(name + "_b", n), const("iota")[:, 0:n], at[:, 1:2], w[:, 1:2],
                                       ALU.is_equal, ALU.mult))
                then(dve, dve.tensor_tensor(s_(name, n), s_(name + "_a", n), s_(name + "_b", n), ALU.add), name)

            loaded(dve, "x")
            layer_norm("lnA", xs[:])
            dve.wait_ge(sem("wkv_split0"), 1)
            low(wkv_lo[0][:], wkv_raw[0][:], wkv_hi[0][:], "wkv_split0")
            for c in range(2):
                dve.wait_ge(sem("ctx_hi"), c + 1)
                sl = slice(c * CHUNK, (c + 1) * CHUNK)
                low(ctx_lo[:, :, sl], ctx_raw[:, c], ctx_hi[:, :, sl], "ctx_lo_dve")
                if c == 0:
                    keep_turned("lnA", bank_a)
            for i in range(NCTX + 2):
                if i < NCTX:
                    key_var(i)
                if 1 <= i <= NCTX:
                    key_scale(i - 1)
                if i >= 2:
                    key_lo(i - 2)
                if i == 3:
                    dve.wait_ge(sem("q_sq"), 1)
                    link(dve.tensor_reduce(s_("q0_ss", 16), wide[:].rearrange("p (h d) -> p h d", h=H0),
                                           AX.X, ALU.add))
                    dve.tensor_scalar(s_("q0_ve", 16), s_("q0_ss", 16), 1.0 / D0, RMS_EPS, ALU.mult,
                                      ALU.add).then_inc(sem("q_var"), 1)
                if i == 5:
                    loaded(dve, "qk_w")
                    link(dve.tensor_tensor(qk_w[:, 2], qk_w[:, 0], qk_w[:, 1], ALU.mult))
                if i == 9:
                    dve.wait_ge(sem("q_root"), 4)
                    link(dve.tensor_tensor(q_sb[:], W1_[:].rearrange("p (h d) -> p h d", h=H0),
                                           s_("q0_rs", 16).unsqueeze(2).to_broadcast([P, H0, D0]), ALU.mult))
                if i == 10:
                    dve.tensor_tensor(q_sb[:], q_sb[:], qk_w[:, 2].unsqueeze(1).to_broadcast([P, H0, D0]),
                                      ALU.mult).then_inc(sem("q_ready"), 1)
                if i == 12:
                    dve.wait_ge(sem("q_split0"), 1)
                    low(qdup0[1][:], q_sb[:].unsqueeze(2).to_broadcast([P, H0, 2, D0]), qdup0[0][:], "q_split0")

            attention(0)

            residual(bank_a[:, 0:D], "out0_mm")
            layer_norm("lnB", xs[:])
            rms("rmB", zn[:], normed, row("inw")).then_inc(sem("turn_in"), 1)
            PAD = T // 2
            then(dve, dve.memset(scan[:].rearrange("p i k b t -> p (i k b) t")[:, :, 0:PAD], 0.0), "scan_zero")
            dve.wait_ge(sem("decay"), 2)
            pw = s_("pow", 12)
            for s in range(1, 6):
                link(dve.tensor_tensor(pw[:, 2 * s:2 * s + 2], pw[:, 2 * s - 2:2 * s],
                                       pw[:, 2 * s - 2:2 * s], ALU.mult))
            dve.wait_ge(sem("turned"), nth(TURNS, "normed"))
            for k in range(KT):
                src = bank_c[:, k * P:(k + 1) * P].rearrange("p (b t) -> p b t", b=B)
                dve.tensor_copy(scan[:, 0, k, :, PAD:], src).then_inc(sem("scan"), 1)
                dve.tensor_scalar(skip[:, k], src, col("dskip", k), None, ALU.mult).then_inc(sem("skip"), 1)
            for s in range(6):
                for k in range(KT):
                    dve.wait_ge(sem("scan"), 2 * s + k + 1)
                    now, at = scan[:, s % 2, k], PAD - 2 ** s
                    dve.scalar_tensor_tensor(scan[:, (s + 1) % 2, k, :, PAD:], now[:, :, at:at + T],
                                             pw[:, 2 * s + k:2 * s + k + 1], now[:, :, PAD:],
                                             ALU.mult, ALU.add).then_inc(sem("scan"), 1)
            dve.wait_ge(sem("skip"), 2)
            for k in range(KT):
                dve.wait_ge(sem("scan"), 2 * 6 + k + 1)
                ins = dve.scalar_tensor_tensor(
                    scan_out[:, k * P:(k + 1) * P].rearrange("p (b t) -> p b t", b=B), scan[:, 0, k, :, PAD:],
                    col("cout", k), skip[:, k], ALU.mult, ALU.add)
            ins.then_inc(sem("turn_in"), 1)
            k1_lo(0)
            dve.wait_ge(sem("turned"), nth(TURNS, "scan_out"))
            link(dve.tensor_tensor(x1[:], zn[:], bank_a[:, 0:D], ALU.add))
            rms("rmC", x1[:], normed, row("ffw"), lambda: k1_lo(1)).then_inc(sem("turn_in"), 1)
            k1_lo(2)
            keep_turned("n2", bank_c)
            link(dve.tensor_tensor(acc[:], xs[:], x1[:], ALU.add))
            k1_lo(3)
            k1_lo(4)
            dve.wait_ge(sem("ff_tanh"), 1)
            dve.scalar_tensor_tensor(wide[:, 0:FF], wide[:, 0:FF], 1.0, bank_b, ALU.add,
                                     ALU.mult).then_inc(sem("ff_act"), 1)
            k1_lo(5)
            k1_lo(6)
            dve.wait_ge(sem("ff_out"), 1)
            link(dve.scalar_tensor_tensor(xs[:], bank_d[:, 0:D], 0.5, acc[:], ALU.mult, ALU.add))
            layer_norm("lnC", xs[:])
            k1_lo(7)
            keep_turned("lnC", bank_a)
            dve.wait_ge(sem("router_mm"), 1)
            link(dve.tensor_tensor(s_("r_logit", E0), bank_b[:, 0:E0], row("rb"), ALU.add))
            link(dve.max(s_("r_top", 8), s_("r_logit", E0)))
            dve.tensor_scalar(s_("r_nmax"), s_("r_top", 8)[:, 0:1], -1.0, None, ALU.mult).then_inc(sem("r_nmax"), 1)
            k1_lo(8)
            dve.wait_ge(sem("r_exp"), 1)
            link(dve.reciprocal(s_("r_rsum"), s_("r_sum")))
            link(dve.tensor_scalar(s_("r_p", E0), s_("r_exp", E0), s_("r_rsum"), None, ALU.mult))
            route("route0", s_("r_p", E0), E0, 1.0)
            k1_lo(9)
            dve.wait_ge(sem("route_turn"), 1)
            dve.tensor_copy(routeT[0:E0, :], bank_a[0:E0, 0:P]).then_inc(sem("routeT"), 1)
            k1_lo(10)
            k1_lo(11)
            dve.wait_ge(sem("moe_b2"), 1)
            then(dve, dve.tensor_tensor(acc[:], xs[:], bank_b[:, 0:D], ALU.add), "moe_acc")
            r0 = s_("route0", E0)
            for n in range(E0 // 2):
                dve.wait_ge(sem("moe_out"), n + 1)
                for j in range(2):
                    e = 2 * n + j
                    last = e == E0 - 1
                    link(dve.scalar_tensor_tensor(
                        (xs if last else acc)[:], (bank_a, bank_b, bank_c, bank_d)[n][:, j * D:(j + 1) * D],
                        r0[:, e:e + 1], acc[:], ALU.mult, ALU.add))
            layer_norm("lnD", xs[:])
            k1_lo(12)
            keep_turned("lnD", bank_a)
            k1_lo(13)
            k1_lo(14)
            dve.wait_ge(sem("q1_mm"), 1)
            dve.tensor_tensor(wide[:, 0:512].rearrange("p (b g t) -> p g b t", g=4, b=B),
                              bank_b.rearrange("p (g b t) -> p g b t", g=4, b=B),
                              col("bq1", 0, 4).unsqueeze(2).unsqueeze(3).to_broadcast([P, 4, B, T]),
                              ALU.add).then_inc(sem("q1_sb"), 1)
            k1_lo(15)
            for x in range(GRP1):
                dve.wait_ge(sem("q1_hi"), x + 1)
                dve.scalar_tensor_tensor(q1_stack(1, x), q1_sb, const("headmask")[:, x:x + 1],
                                         q1_stack(0, x).bitcast(F32), ALU.mult,
                                         ALU.subtract).then_inc(sem("q1_lo"), 1)

            attention(1)

            residual(bank_a[:, 0:D], "out1_mm", row("bo1"))
            layer_norm("lnE", xs[:])
            keep_turned("lnE", bank_c)
            dve.wait_ge(sem("att_qk"), 1)
            for j in range(2 * KT):
                dve.tensor_scalar(wide[:, j * P:(j + 1) * P], bank_b[:, j * P:(j + 1) * P],
                                  col(("abq", "abk")[j // KT], j % KT), None,
                                  ALU.add).then_inc(sem("att_qk_sb"), 1)
            dve.wait_ge(sem("att_v"), 1)
            link(dve.tensor_tensor(att_v, bank_d[:, 0:D], row("abv"), ALU.add))
            dve.wait_ge(sem("att_parts"), 3)
            link(dve.scalar_tensor_tensor(att_theta, att_parts[:, 0, :], 0.1, const("theta0"), ALU.mult, ALU.add))
            link(dve.scalar_tensor_tensor(att_theta, att_parts[:, 1, :], 0.15, att_theta, ALU.mult, ALU.add))
            link(dve.scalar_tensor_tensor(att_theta, att_parts[:, 2, :], 0.1, att_theta, ALU.mult, ALU.add))
            link(dve.tensor_reduce(s_("att_max"), att_theta, AX.X, ALU.max))
            dve.tensor_scalar(s_("att_nmax"), s_("att_max"), -1.0, None, ALU.mult).then_inc(sem("att_nmax"), 1)
            dve.wait_ge(sem("att_exp"), 1)
            link(dve.reciprocal(s_("att_rsum"), s_("att_sum")))
            dve.tensor_scalar(att_p, att_e, s_("att_rsum"), None, ALU.mult).then_inc(sem("att_p"), 1)
            dve.wait_ge(sem("att_p_turn"), 1)
            dve.tensor_copy(att_pT, bank_c[:, 0:P]).then_inc(sem("att_pT"), 1)
            dve.wait_ge(sem("att_o"), 1)
            dve.tensor_copy(zT[:].rearrange("p k n -> p (k n)"), bank_b[:, 0:D]).then_inc(sem("att_oT"), 1)
            residual(bank_d[:, 0:D], "att_out", row("abo"))
            layer_norm("lnF", xs[:])
            keep_turned("lnF", bank_a)
            link(dve.tensor_tensor(acc[:], xs[:], zn[:], ALU.add))
            dve.wait_ge(sem("gate_mm"), 1)
            dve.tensor_tensor(s_("g_logit", E1), bank_b[:, 0:E1], row("gb"), ALU.add).then_inc(sem("g_logit"), 1)
            dve.wait_ge(sem("g_tanh"), 1)
            link(dve.tensor_scalar(s_("g_sig", E1), s_("g_tanh", E1), 1.0, 0.5, ALU.add, ALU.mult))
            route("route1", s_("g_sig", E1), E1, 0.5)
            r1 = s_("route1", E1)
            for n in range(E1 + 3):
                if n <= E1:
                    dve.wait_ge(sem("exp_tanh"), n + 1)
                    link(dve.scalar_tensor_tensor(hid[:, n % 2, 0, :], hid[:, n % 2, 0, :], 1.0,
                                                  banks[n % 2][:, 0:P], ALU.add, ALU.mult))
                    if n >= 2:
                        dve.wait_ge(sem("exp_dn"), n - 1)
                    dve.tensor_tensor(hid[:, n % 2, 1, :], hid[:, n % 2, 0, :], banks[n % 2][:, P:2 * P],
                                      ALU.mult).then_inc(sem("exp_h"), 1)
                if n >= 2:
                    m = n - 2
                    dve.wait_ge(sem("exp_dn"), m + 1)
                    w = 0.5 if m == 0 else r1[:, m - 1:m]
                    then(dve, dve.scalar_tensor_tensor(acc[:], banks[2 + m % 2][:, 0:D], w, acc[:],
                                                       ALU.mult, ALU.add), "exp_sum", m + 1)
            dve.tensor_copy(xs[:], acc[:]).then_inc(sem("x_final"), 1)




def kernel(**inputs):
    import concourse.bacc as _bacc
    from concourse.bass_utils import run_bass_kernel_spmd as _run

    a = {k: np.asarray(v) for k, v in inputs.items()}

    def by_rows(w):
        return w.reshape(-1, P, w.shape[-1]).transpose(1, 0, 2)

    L0, L1, A = "L0_xattn_", "L1_xattn_", "L1_attn_"
    ctxT = a["ctx_1024"].reshape(B * S, D).T.reshape(KT, P, 4, CHUNK).transpose(2, 1, 0, 3)
    wo0 = a[L0 + "wo"].T.reshape(2, 2, G0, D0, D).transpose(0, 2, 1, 3, 4).reshape(H0 * D0, D)
    eye = np.eye(P, dtype=np.float32)
    p = np.arange(P)
    consts = {
        "ident": eye,
        "headmask": (((p % 64) // D1)[:, None] == np.arange(GRP1)[None, :]) / 4.0,
        "pairmask": (p // T)[:, None] == (np.arange(2 * D1) // D1)[None, :],
        "theta0": np.where((p // T)[:, None] == (p // T)[None, :], 0.6, FAR),
        "iota": np.tile(np.arange(E1), (P, 1)),
    }
    f = "L1_ffn_"
    gu = np.concatenate([np.concatenate([a[f + "shared_wg"][None], a[f + "experts_wg"]]),
                         np.concatenate([a[f + "shared_wu"][None], a[f + "experts_wu"]])], axis=2)
    rows = {"inw": a["L0_attn_input_norm_w"],
            "ffw": a["L0_attn_ff_norm_w"], "rb": a["L0_ffn_router_b"],
            "bo1": a[L1 + "bo"], "abv": a[A + "bv"], "abo": a[A + "bo"], "gb": a[f + "gate_b"]}
    on_p = lambda v: v.reshape(-1, P).T
    cols = {"alog": on_p(a["L0_attn_a_log"]), "cout": on_p(a["L0_attn_c_out"]),
            "dskip": on_p(a["L0_attn_d_skip"]), "b1": a["L0_ffn_b1"].T, "abq": on_p(a[A + "bq"]),
            "abk": on_p(a[A + "bk"]), "bk1": on_p(a[L1 + "bk"]), "bv1": on_p(a[L1 + "bv"]),
            "bq1": np.tile(a[L1 + "bq"].reshape(-1, 64).T, (2, 1))}
    arrays = {
        "x": a["x"].reshape(B * T, D),
        "ctxT": ctxT,
        "wkv0": by_rows(np.concatenate([a[L0 + "wk"], a[L0 + "wv"]]).T),
        "wkv1": by_rows(np.concatenate([a[L1 + "Wk"], a[L1 + "Wv"]]).T),
        "wq0": by_rows(a[L0 + "wq"].T),
        "wo0": by_rows(wo0),
        "fc": by_rows(a["L0_attn_ff_fc_w"].T),
        "proj": by_rows(a["L0_attn_ff_proj_w"].T),
        "rw0": by_rows(a["L0_ffn_router_w"]),
        "w1": by_rows(a["L0_ffn_W1"].transpose(1, 0, 2).reshape(D, E0 * F0)),
        "w2": a["L0_ffn_W2"].transpose(1, 0, 2),
        "b2": a["L0_ffn_b2"],
        "wq1": by_rows(np.tile(a[L1 + "Wq"].T.reshape(D, 4, 1, 64), (1, 1, 2, 1)).reshape(D, 2 * D)),
        "wo1": by_rows(a[L1 + "Wo"].T),
        "watt": np.stack([by_rows(a[A + n].T) for n in ("Wq", "Wk", "Wv", "Wo")], axis=1),
        "gw1": by_rows(a[f + "gate_w"]),
        "wgu": gu.reshape(E1 + 1, KT, P, 2 * F1).transpose(2, 0, 1, 3),
        "wdn": np.concatenate([a[f + "shared_wd"][None], a[f + "experts_wd"]]).transpose(1, 0, 2),
        "qk_rows": np.concatenate([a[L0 + "q_norm_w"], a[L0 + "k_norm_w"]]),
        "rows": np.concatenate([rows[n] for n, _ in ROWS]),
        "cols": np.concatenate([cols[n] for n, _ in COLS], axis=1),
        "consts": np.concatenate([consts[n].astype(np.float32) for n, _ in CONSTS], axis=1),
    }
    nc = _bacc.Bacc("TRN2", target_bir_lowering=False, num_devices=1)
    fed, t = {}, {}
    for name, v in arrays.items():
        fed["in_" + name] = np.ascontiguousarray(v)
        t[name] = nc.dram_tensor("in_" + name, fed["in_" + name].shape, F32, kind="ExternalInput").ap()
    t["out"] = nc.dram_tensor("out", (B * T, D), F32, kind="ExternalOutput").ap()
    build(nc, t)
    r = _run(nc, [fed], core_ids=[0])
    return r.results[0]["out"].reshape(B, T, D)
```

```python
from contextlib import ExitStack

import numpy as np

import concourse.bass as bass
from concourse import mybir

ALU = mybir.AluOpType
ACT = mybir.ActivationFunctionType
AX = mybir.AxisListType
F32 = mybir.dt.float32
F32R = mybir.dt.float32r
U32 = mybir.dt.uint32

P = 128
B, T, D = 2, 64, 256
KT = D // P
S = 1024
NKEY = S // P
NCTX = B * NKEY
CHUNK = 512
H0, HK0, D0 = 16, 4, 64
G0 = H0 // HK0
H1, D1 = 16, 16
GRP1 = P // (2 * D1)
TILES = B * H0 // 2
FF = 512
E0, F0 = 8, 128
E1, F1 = 16, 128
LN_EPS, RMS_EPS = 1e-5, 1e-6
FAR = -1e30

ROWS = [("inw", D), ("ffw", D), ("rb", E0),
        ("bo1", D), ("abo", D), ("gb", E1)]
COLS = [("alog", KT), ("cout", KT), ("dskip", KT), ("b1", E0), ("abq", KT), ("abk", KT), ("abv", KT),
        ("bk1", KT), ("bv1", KT), ("bq1", H1 * D1 // 64),
        ("qnw", 1), ("knw", 1)]
CONSTS = [("ident", P), ("headmask", GRP1), ("pairmask", 2 * D1), ("theta0", P), ("iota", E1)]


ROOTS = ["lnA", "lnB", "rmB", "rmC", "lnC", "lnD", "lnE", "lnF"]
KEPT = ["lnA", "n2", "lnC", "lnD", "lnE", "lnF"]
TURNS = ["lnA", "normed", "scan_out", "n2", "lnC", "lnD", "lnE", "lnF"]


def nth(order, name):
    return order.index(name) + 1


def offsets(fields):
    at, out = 0, {}
    for name, n in fields:
        out[name] = (at, n)
        at += n
    return out, at


ROW_AT, NROW = offsets(ROWS)
COL_AT, NCOL = offsets(COLS)
CONST_AT, NCONST = offsets(CONSTS)


def build(nc, t):
    with ExitStack() as ctx:
        known = {}

        def sem(name):
            if name not in known:
                known[name] = nc.alloc_semaphore(name=name)
            return known[name]

        base = -(-nc.sbuf_base // 64) * 64
        top = [base]

        def region(nbytes):
            at = top[0]
            top[0] += -(-nbytes // 32) * 32
            return at

        def place(name, shape, dt, at):
            return nc.alloc_sbuf_tensor_at(name, shape, dt, offset=at)

        def new(name, shape, dt=F32):
            return place(name, shape, dt, region(4 * int(np.prod(shape[1:]))))

        r_ctx = region(4 * 2 * KT * B * S + 4 * 4 * KT * 512)
        ctx_hi = place("ctx_hi", [P, KT, B * S], F32R, r_ctx)
        ctx_lo = place("ctx_lo", [P, KT, B * S], F32R, r_ctx + 4 * KT * B * S)
        r_w = r_ctx + 8 * KT * B * S
        wkv_hi = [place(f"wkv_hi{l}", [P, KT, 512], F32R, r_w + l * 8 * KT * 512) for l in range(2)]
        wkv_lo = [place(f"wkv_lo{l}", [P, KT, 512], F32R, r_w + (2 * l + 1) * 4 * KT * 512) for l in range(2)]
        wgu = place("wgu", [P, E1 + 1, KT, 2 * F1], F32, r_ctx)
        watt = place("watt", [P, 4, KT, D], F32, r_ctx + 4 * (E1 + 1) * KT * 2 * F1)
        assert ((E1 + 1) * KT * 2 * F1 + 4 * KT * D) * 4 <= 8 * KT * B * S + 16 * KT * 512

        wo0 = new("wo0", [P, 8, D])
        r_k = region(4 * 4 * B * S)
        kstack = place("kstack", [P, 4, B * S], F32R, r_k)
        wdn = place("wdn", [P, E1 + 1, D], F32, r_k)
        vals = new("vals", [P, NCTX, D])
        r_pt = region(4 * 4 * NKEY * 256)
        pt = place("pt", [P, 4, NKEY, 256], F32, r_pt)
        ctx_raw = place("ctx_raw", [P, 4, KT, CHUNK], F32, r_pt)
        wkv_raw = [place(f"wkv_raw{l}", [P, KT, 512], F32, r_pt + 4 * 4 * KT * CHUNK + l * 4 * KT * 512)
                   for l in range(2)]
        w1 = place("w1", [P, KT, E0 * F0], F32, r_pt)
        w2 = place("w2", [P, E0, D], F32, r_pt + 4 * KT * E0 * F0)
        fc = place("fc", [P, KT, FF], F32, r_pt + 4 * (KT * E0 * F0 + E0 * D))
        proj = place("proj", [P, FF // P, D], F32, r_pt + 4 * (KT * E0 * F0 + E0 * D + KT * FF))
        r_p = region(4 * 3 * S)
        prob = place("prob", [P, 3, S], F32, r_p)
        wq0 = place("wq0", [P, KT, H0 * D0], F32, r_p)
        qstack = [new(f"qstack_{x}", [P, B, H0, T], F32R) for x in ("hi", "lo")]
        rw0 = new("rw0", [P, KT, E0])
        b2 = new("b2", [P, D])
        wq1 = new("wq1", [P, KT, 2 * D])
        wo1 = new("wo1", [P, KT, D])
        gw1 = new("gw1", [P, KT, E1])
        rows = new("rows", [P, NROW])
        cols = new("cols", [P, NCOL])
        consts = new("consts", [P, NCONST])
        kn = new("kn", [P, 4, D])
        ksq = new("ksq", [P, 2, HK0, D0 + 1])
        kss = new("kss", [P, 2, 4])
        krs = new("krs", [P, 2, 4])
        nmx = new("nmx", [P, 2, TILES])
        sums = new("sums", [P, 2, TILES])
        rsum = new("rsum", [P, 4])
        xs = new("xs", [P, D])
        zn = new("zn", [P, D])
        zT = new("zT", [P, KT, P])
        wide = new("wide", [P, H0 * (D0 + 1)])
        qsq = wide[:].rearrange("p (h d) -> p h d", h=H0)
        q_twice = place("q_twice", [P, H0, 2, D0], F32, r_p)
        oT = new("oT", [P, 8, B, T])
        acc = new("acc", [P, D])
        x1 = new("x1", [P, D])
        normed_t = new("normed_sb", [P, D])
        normed = normed_t[:]
        scratch = new("scratch", [P, D])
        x_bias = new("x_bias", [P, D])
        inv_all = x1
        routeT = new("routeT_sb", [P, P])
        scan = place("scan_sb", [P, D], F32, r_p)
        skip = place("skip_sb", [P, D], F32, r_p + 4 * D)
        scan_out_t = place("scan_out_sb", [P, D], F32, r_p + 4 * 2 * D)
        decays = new("decays", [P, KT, B, T])
        bv_wide = new("bv_wide", [P, KT, P])
        wvo = new("wvo", [P, KT, D])
        scan_out = scan_out_t[:]
        att = place("att", [P, 6, P], F32, r_p + 4 * 4 * P)
        att_parts, att_theta, att_e, att_eT = att[:, 0:3], att[:, 3], att[:, 4], att[:, 5]
        att_v_t = place("att_v_sb", [P, D], F32, r_p + 4 * 11 * P)
        att_v = att_v_t[:]
        sm = new("sm", [P, 400])
        half = new("half", [P, 16])
        hid = place("hid", [P, 2, 2, P], F32, r_p)
        assert top[0] <= nc.sbuf_usable_end, (top[0], nc.sbuf_usable_end)

        banks = [ctx.enter_context(nc.psum_tensor(f"bank{i}", [P, 512], F32)) for i in range(4)]
        wide_ps = [ctx.enter_context(nc.psum_tensor(f"wide{i}", [P, 1024], F32)) for i in range(2)]
        tr_ps = banks[2:4]
        pv_ps = banks[0:2]
        W0, W1_ = wide_ps[0], wide_ps[1]
        bank_a, bank_b, bank_c, bank_d = W0[:, 0:512], W0[:, 512:1024], W1_[:, 0:512], W1_[:, 512:1024]

        def kv_bank(i):
            return banks[i % 4]

        def turn_bank(p):
            return (bank_a, bank_b)[p % 2] if p < NCTX // 2 - 2 else banks[p % 2][:]

        def k1_piece(n):
            return n % 2, slice((n // 2) * 512, (n // 2 + 1) * 512), banks[n % 2]

        def scores(l, i):
            return wide_ps[(i + 1 - l) % 2]

        def moe_bank(n):
            return (bank_a, bank_c, bank_d, bank_b)[n]

        def inv_bank(g):
            return bank_c[:, 0:D] if g == 3 else pv_ps[g % 2][:, D:2 * D]

        def row(name):
            at, n = ROW_AT[name]
            return rows[:, at:at + n]

        def col(name, i, n=1):
            at = COL_AT[name][0] + i
            return cols[:, at:at + n]

        def const(name):
            at, n = CONST_AT[name]
            return consts[:, at:at + n]

        ident = const("ident")
        q1_sb = wide[:, 0:512].rearrange("p (b g t) -> p (b g) t", g=4, b=B)

        def q1_stack(part, x):
            return qstack[part][:].rearrange("p b (g x) t -> p (b g) x t", x=GRP1)[:, :, x]

        small = {}

        def s_(name, n=1):
            if name not in small:
                small[name] = (sum(k for _, k in small.values()), n)
                assert sum(k for _, k in small.values()) <= 400
            at, n = small[name]
            return sm[:, at:at + n]

        def then(eng, ins, name, n=1):
            ins.then_inc(sem(name), 1)
            eng.wait_ge(sem(name), n)

        block = ctx.enter_context(nc.Block())

        def loaded(eng, name):
            eng.wait_ge(sem("dma_" + name), 16)

        @block.sync
        def _(sp):
            def load(name, dst, src):
                sp.dma_start(dst, src).then_inc(sem("dma_" + name), 16)

            load("x", xs[:], t["x"])
            load("wkv0", wkv_raw[0][:], t["wkv0"])
            for hf in range(2):
                half_c = slice(hf * CHUNK // 2, (hf + 1) * CHUNK // 2)
                load(f"ctx0_{hf}", ctx_raw[:, 0, :, half_c], t["ctxT"][0][:, :, half_c])
            load("consts", consts[:], t["consts"])
            load("ctx1", ctx_raw[:, 1], t["ctxT"][1])
            load("wq0", wq0[:], t["wq0"])
            load("ctx2", ctx_raw[:, 2], t["ctxT"][2])
            load("ctx3", ctx_raw[:, 3], t["ctxT"][3])
            load("cols", cols[:], t["cols"])
            load("wkv1", wkv_raw[1][:], t["wkv1"])
            load("rows", rows[:], t["rows"].partition_broadcast(P))
            load("wo0", wo0[:], t["wo0"])
            load("rw0", rw0[:], t["rw0"])
            load("b2", b2[0:E0, :], t["b2"])
            load("wq1", wq1[:], t["wq1"])
            load("wo1", wo1[:], t["wo1"])
            load("gw1", gw1[:], t["gw1"])
            sp.wait_ge(sem("pv0"), 4)
            load("fc", fc[:], t["fc"])
            load("proj", proj[:], t["proj"])
            load("w1", w1[:], t["w1"])
            load("w2", w2[:], t["w2"])
            sp.wait_ge(sem("k1_mm"), 8)
            sp.wait_ge(sem("v1_mm"), NCTX)
            load("watt", watt[:], t["watt"])
            load("wgu0", wgu[:, 0:8], t["wgu"][:, 0:8])
            load("wgu1", wgu[:, 8:17], t["wgu"][:, 8:17])
            sp.wait_ge(sem("score1"), TILES)
            load("wdn", wdn[:], t["wdn"])
            sp.wait_ge(sem("exp_sum"), E1 + 1)
            sp.dma_start(t["out"], xs[:]).then_inc(sem("stored"), 16)
            sp.wait_ge(sem("stored"), 16)

        @block.gpsimd
        def _(pool):
            pool.memset(ksq[:, :, :, D0:D0 + 1], RMS_EPS)
            pool.memset(qsq[:, :, D0:D0 + 1], RMS_EPS).then_inc(sem("eps_set"), 1)
            then(pool, pool.memset(half[:], -0.5), "half_set")

            def rsqrt(name, n=1):
                pool.wait_ge(sem("var"), nth(ROOTS, name))
                pool.tensor_tensor(s_(name + "_rs", n), s_(name + "_ve", n), half[:, 0:n],
                                   ALU.pow).then_inc(sem("root"), 1)

            def key_rsqrt(i):
                pool.wait_ge(sem("kss"), i + 1)
                if i >= 2:
                    pool.wait_ge(sem("kn0"), i - 1)
                pool.tensor_tensor(krs[:, i % 2], kss[:, i % 2], half[:, 0:4],
                                   ALU.pow).then_inc(sem("krs"), 1)

            def ctx_lo_part(c, hf):
                n = CHUNK // 2
                pool.wait_ge(sem("ctx_hi"), 2 if c == 0 else c + 2)
                sl = slice(c * CHUNK + hf * n, c * CHUNK + (hf + 1) * n)
                pool.tensor_tensor(ctx_lo[:, :, sl], ctx_raw[:, c, :, hf * n:(hf + 1) * n],
                                   ctx_hi[:, :, sl].bitcast(F32), ALU.subtract).then_inc(sem("ctx_lo_pool"), 1)

            rsqrt("lnA")
            ctx_lo_part(0, 1)
            for i in range(NCTX):
                key_rsqrt(i)
                if i == 4:
                    pool.wait_ge(sem("q_var"), 1)
                if 4 <= i < 8:
                    n = i - 4
                    pool.tensor_tensor(s_("q0_rs", 16)[:, 4 * n:4 * n + 4], s_("q0_ve", 16)[:, 4 * n:4 * n + 4],
                                       half[:, 0:4], ALU.pow).then_inc(sem("q_root"), 1)
                if i == 3:
                    ctx_lo_part(3, 0)
                    ctx_lo_part(3, 1)
            pool.wait_ge(sem("wkv_split1"), 1)
            pool.tensor_tensor(wkv_lo[1][:], wkv_raw[1][:], wkv_hi[1][:].bitcast(F32),
                               ALU.subtract).then_inc(sem("wkv_split1"), 1)

            for name in ROOTS[1:]:
                rsqrt(name)

        @block.tensor
        def _(pe):
            def kv_mm(i, low=None):
                c = i // 4
                if not low and (i == 2 or i % 4 == 0):
                    pe.wait_ge(sem("ctx_hi"), {0: 1, 2: 2}.get(i, c + 2))
                if i == 0 and not low:
                    pe.wait_ge(sem("wkv_split0"), 1)
                if i >= 4:
                    pe.wait_ge(sem("kn0"), i - 3)
                    pe.wait_ge(sem("v0"), i - 3)
                sl = slice(i * P, (i + 1) * P)
                parts = [(ctx_hi, wkv_hi[0]), (ctx_hi, wkv_lo[0]), (ctx_lo, wkv_hi[0])]
                for n, (a, w) in enumerate(parts):
                    if low is not None and low != (n == 2):
                        continue
                    if n == 1 and i == 0:
                        pe.wait_ge(sem("wkv_split0"), 2)
                    if n == 2 and i % 4 == 0 and c < 3:
                        pe.wait_ge(sem("ctx_lo_dve"), c + 1)
                    if n == 2 and i in (2, 12, 14):
                        pe.wait_ge(sem("ctx_lo_pool"), {2: 1, 12: 2, 14: 3}[i])
                    for k in range(KT):
                        mm = pe.matmul(kv_bank(i)[:], a[:, k, sl], w[:, k, :],
                                       start=(n == 0 and k == 0), stop=(n == 2 and k == KT - 1))
                if low is not False:
                    mm.then_inc(sem("kv_mm0"), 1)

            def k1_mm(n):
                ft, keys, bank = k1_piece(n)
                if n == 0:
                    pe.wait_ge(sem("wkv_split1"), 2)
                if n >= 2:
                    pe.wait_ge(sem("klo1"), 2 * (n - 1))
                else:
                    pe.wait_ge(sem("pv_read0"), 4)
                fs = slice(ft * P, (ft + 1) * P)
                parts = [(wkv_hi[1], ctx_hi), (wkv_lo[1], ctx_hi), (wkv_hi[1], ctx_lo)]
                for m, (w, x) in enumerate(parts):
                    for k in range(KT):
                        mm = pe.matmul(bank[:], w[:, k, fs], x[:, k, keys],
                                       start=(m == 0 and k == 0), stop=(m == 2 and k == KT - 1))
                mm.then_inc(sem("k1_mm"), 1)

            def v1_mm(*tiles):
                for i in tiles:
                    if i == 0:
                        pe.wait_ge(sem("wkv_split1"), 2)
                    if i >= 2:
                        pe.wait_ge(sem("v1"), i - 1)
                    else:
                        pe.wait_ge(sem("pt_even0"), TILES)
                        pe.wait_ge(sem("pt_odd0"), TILES)
                    parts = [(ctx_hi, wkv_hi[1]), (ctx_lo, wkv_hi[1]), (ctx_hi, wkv_lo[1])]
                    for m, (x, w) in enumerate(parts):
                        for k in range(KT):
                            mm = pe.matmul(banks[2 + i % 2][:, 0:D], x[:, k, i * P:(i + 1) * P],
                                           w[:, k, D:2 * D], start=(m == 0 and k == 0),
                                           stop=(m == 2 and k == KT - 1))
                    mm.then_inc(sem("v1_mm"), 1)

            def k_turn(p):
                pe.wait_ge(sem("kn0"), 2 * p + 2)
                if p >= NCTX // 2 - 2:
                    pe.wait_ge(sem("kn0"), NCTX - 2)
                elif p >= 2:
                    pe.wait_ge(sem("klo0"), 2 * (p - 1))
                elif p == 0:
                    pe.wait_ge(sem("kept"), nth(KEPT, "lnA"))
                for ft in range(2):
                    for j in range(2):
                        mm = pe.transpose(turn_bank(p)[:, (2 * ft + j) * P:(2 * ft + j + 1) * P],
                                          kn[:, (2 * p + j) % 4, ft * P:(ft + 1) * P], ident)
                mm.then_inc(sem("k_turn0"), 1)

            def turn(name, src, dst_ps):
                pe.wait_ge(sem("turn_in"), nth(TURNS, name))
                if name == "lnA":
                    loaded(pe, "consts")
                for k in range(KT):
                    mm = pe.transpose(dst_ps[:, k * P:(k + 1) * P], src[:, k * P:(k + 1) * P], ident)
                mm.then_inc(sem("turned"), 1)

            def q_turn(n):
                pe.wait_ge(sem("q_ready"), n + 1)
                if n >= 2:
                    pe.wait_ge(sem("q_lo0"), n - 1)
                dst = (bank_c, bank_d)[n % 2].rearrange("p (b h t) -> p b h t", b=B, h=4)
                for j in range(4):
                    mm = pe.transpose(dst[:, :, j, :],
                                      q_twice[:, 4 * n + j].rearrange("p x d -> p (x d)"), ident)
                mm.then_inc(sem("q_turn0"), 1)

            def score(l, i):
                b, r = divmod(i, TILES // B)
                if i == 0 and l == 0:
                    pe.wait_ge(sem("q_lo0"), 4)
                    pe.wait_ge(sem("klo0"), NKEY)
                if i == 1 and l == 0:
                    pe.wait_ge(sem("klo0"), NCTX - 4)
                if i == 8 and l == 0:
                    pe.wait_ge(sem("klo0"), NCTX)
                if i % 8 == 0 and l == 1:
                    pe.wait_ge(sem("klo1"), i + 8)
                if i < 2 and l == 1:
                    pe.wait_ge(sem("q1_lo"), 2 * i + 2)
                if i >= 2:
                    pe.wait_ge(sem(f"exp{l}"), i - 1)
                h = 2 * r
                grp = h // 4
                for part in range(2):
                    for c in range(S // 512):
                        mm = pe.matmul(scores(l, i)[:, c * 512:(c + 1) * 512],
                                       qstack[part][:, b, h:h + 2, :],
                                       kstack[:, grp, b * S + c * 512:b * S + (c + 1) * 512],
                                       start=(part == 0), stop=(part == 1))
                mm.then_inc(sem(f"score{l}"), 1)

            def p_turn(l, i):
                pe.wait_ge(sem(f"exp{l}"), i + 1)
                for hf in range(2):
                    if i >= 1:
                        pe.wait_ge(sem(f"pt_{('even', 'odd')[hf]}{l}"), i)
                    else:
                        pe.wait_ge(sem(("kn0", "v1")[l]), NCTX)
                    for j in range(4):
                        kt = 4 * hf + j
                        mm = pe.transpose(tr_ps[hf][:, j * P:(j + 1) * P],
                                          prob[:, i % 3, kt * P:(kt + 1) * P], ident)
                    mm.then_inc(sem(f"p_turn{l}"), 1)

            def inv_spread(l, g):
                pe.wait_ge(sem(f"inv_sum{l}"), g + 1)
                if g >= 2:
                    pe.wait_ge(sem(f"pv_read{l}"), g - 1)
                elif g == 0 and l == 0:
                    pe.wait_ge(sem("klo0"), NCTX)
                    pe.wait_ge(sem("v0"), NCTX)
                elif g == 0:
                    pe.wait_ge(sem("klo1"), 16)
                for j in range(4):
                    if l == 0:
                        half = slice(D0 * (j // 2), D0 * (j // 2 + 1))
                        out = inv_bank(g)[half, (j % 2) * P:(j % 2 + 1) * P]
                        inv = acc[:, D0 * j:D0 * (j + 1)]
                    else:
                        out = inv_bank(g)[32 * j:32 * j + 32, 0:P]
                        inv = acc[:, 32 * j:32 * j + 32]
                    mm = pe.matmul(out, inv, ident, start=True, stop=True)
                mm.then_inc(sem(f"inv_spread{l}"), 1)

            def pv(l, g, part):
                pe.wait_ge(sem(f"pt_even{l}"), 4 * g + 4)
                pe.wait_ge(sem(f"pt_odd{l}"), 4 * g + 4)
                b, hf = divmod(g, 2)
                for kt in range(2 * part, 2 * part + 2):
                    v = vals[:, b * NKEY + kt, :]
                    if l == 0:
                        for j in range(2):
                            mm = pe.matmul(pv_ps[g % 2][64 * j:64 * j + 64, 0:256],
                                           v[:, (2 * hf + j) * D0:(2 * hf + j + 1) * D0],
                                           pt[:, (2 * g + j) % 4, kt, :],
                                           start=(kt == 0), stop=(kt == NKEY - 1))
                    else:
                        for j in range(4):
                            f = P * hf + 32 * j
                            mm = pe.matmul(pv_ps[g % 2][32 * j:32 * j + 32, 0:P], v[:, f:f + 32],
                                           pt[:, (2 * g + j // 2) % 4, kt, (j % 2) * P:(j % 2 + 1) * P],
                                           start=(kt == 0), stop=(kt == NKEY - 1))
                if part == 3:
                    mm.then_inc(sem(f"pv{l}"), 1)

            def attention(l):
                for i in range(TILES + 6):
                    if i < TILES and (l == 1 or i >= 2):
                        score(l, i)
                    if l == 1 and i == 1:
                        v1_mm(14, 15)
                    if 2 <= i < TILES + 2:
                        p_turn(l, i - 2)
                    if i >= 6:
                        g, part = divmod(i - 6, 4)
                        if part == 0:
                            inv_spread(l, g)
                        pv(l, g, part)

            oT_flat = oT[:].rearrange("p k b t -> p (k b t)")[:, 0:D]

            def keep_warm(n, src):
                for _ in range(n):
                    pe.matmul(banks[0][:, 0:D], src[:, 0:P], src, start=True, stop=True)

            def linear(out, lhs, rhs, n):
                for k in range(n):
                    mm = pe.matmul(out, lhs(k), rhs(k), start=(k == 0), stop=(k == n - 1))
                return mm

            kv_mm(0, False)
            turn("lnA", zn, bank_a)
            kv_mm(0, True)
            for i in range(1, 4):
                kv_mm(i)
            pe.wait_ge(sem("kept"), nth(KEPT, "lnA"))
            loaded(pe, "wq0")
            for n in range(2):
                mm = linear(W1_[:, n * 512:(n + 1) * 512], lambda k: zT[:, k, :],
                            lambda k: wq0[:, k, n * 512:(n + 1) * 512], KT)
            mm.then_inc(sem("q0_mm"), 1)
            for i in range(4, NCTX):
                kv_mm(i)
                if 12 <= i < 16:
                    q_turn(i - 12)
                if i % 2 == 0 and i >= 4:
                    k_turn((i - 4) // 2)
            k_turn(NCTX // 2 - 2)
            score(0, 0)
            k_turn(NCTX // 2 - 1)
            score(0, 1)

            attention(0)

            loaded(pe, "wo0")
            for k in range(8):
                if k % 4 == 0:
                    pe.wait_ge(sem("pv_read0"), 3 + k // 4)
                mm = pe.matmul(bank_a[:, 0:D], oT[:, k].rearrange("p b t -> p (b t)"), wo0[:, k, :],
                               start=(k == 0), stop=(k == 7))
            mm.then_inc(sem("out0_mm"), 1)
            v1_mm(0, 1)
            k1_mm(0)
            k1_mm(1)
            turn("normed", normed, bank_c)
            v1_mm(2, 3, 4)
            turn("scan_out", scan_out, bank_a)
            v1_mm(5, 6)
            k1_mm(2)
            turn("n2", normed, bank_a)
            v1_mm(7)
            pe.wait_ge(sem("kept"), nth(KEPT, "n2"))
            loaded(pe, "fc")
            for j in range(FF // P):
                mm = linear((bank_b, bank_c)[j // 2][:, (j % 2) * P:(j % 2 + 1) * P],
                            lambda k: fc[:, k, j * P:(j + 1) * P], lambda k: zT[:, k, :], KT)
                if j % 2 == 1:
                    mm.then_inc(sem("ff_h"), 1)
            loaded(pe, "proj")
            for k in range(FF // P):
                if k % 2 == 0:
                    pe.wait_ge(sem("ff_act"), k // 2 + 1)
                mm = pe.matmul(bank_d[:, 0:D], wide[:, k * P:(k + 1) * P], proj[:, k, :],
                               start=(k == 0), stop=(k == FF // P - 1))
            mm.then_inc(sem("ff_out"), 1)
            k1_mm(3)
            k1_mm(4)
            turn("lnC", zn, bank_a)
            v1_mm(8)
            pe.wait_ge(sem("kept"), nth(KEPT, "lnC"))
            loaded(pe, "rw0")
            linear(bank_b[:, 0:E0], lambda k: zT[:, k, :], lambda k: rw0[:, k, :],
                   KT).then_inc(sem("router_mm"), 1)
            loaded(pe, "w1")
            for e in range(E0):
                mm = linear((bank_c, bank_d)[e // 4][:, (e % 4) * P:(e % 4 + 1) * P],
                            lambda k: w1[:, k, e * F0:(e + 1) * F0], lambda k: zT[:, k, :], KT)
                if e % 4 == 3:
                    mm.then_inc(sem("moe_h"), 1)
            pe.wait_ge(sem("route0"), 1)
            pe.transpose(bank_b[0:E0, 0:P], s_("route0", E0), ident).then_inc(sem("route_turn"), 1)
            loaded(pe, "w2")
            for n in range(E0 // 2):
                pe.wait_ge(sem("moe_act"), (2, 4, 8, 8)[n])
                if n == 3:
                    pe.wait_ge(sem("moe_acc"), 1)
                for j in range(2):
                    e = 2 * n + j
                    mm = pe.matmul(moe_bank(n)[:, j * D:(j + 1) * D],
                                   wide[:, e * P:(e + 1) * P], w2[:, e, :], start=True, stop=True)
                mm.then_inc(sem("moe_out"), 1)
                if n == 0:
                    pe.wait_ge(sem("routeT"), 1)
                    loaded(pe, "b2")
                    pe.matmul(bank_b[:, D:2 * D], routeT[0:E0, :], b2[0:E0, :], start=True,
                              stop=True).then_inc(sem("moe_b2"), 1)
            k1_mm(5)
            v1_mm(9, 10)
            k1_mm(6)
            v1_mm(11)
            turn("lnD", zn, bank_a)
            v1_mm(12)
            pe.wait_ge(sem("kept"), nth(KEPT, "lnD"))
            loaded(pe, "wq1")
            for g in range(4):
                mm = linear(bank_b[:, g * P:(g + 1) * P], lambda k: wq1[:, k, g * P:(g + 1) * P],
                            lambda k: zT[:, k, :], KT)
            mm.then_inc(sem("q1_mm"), 1)
            k1_mm(7)
            v1_mm(13)

            attention(1)

            def wvo_mm(k):
                linear(bank_d[:, k * D:(k + 1) * D], lambda m: watt[:, 2, m, k * P:(k + 1) * P],
                       lambda m: watt[:, 3, m, :], KT).then_inc(sem("wvo_mm"), 1)

            loaded(pe, "wo1")
            loaded(pe, "watt")
            for k in range(KT):
                if k == 1:
                    wvo_mm(0)
                pe.wait_ge(sem("pv_read1"), 3 + k)
                mm = pe.matmul(bank_a[:, 0:D], oT[:, k].rearrange("p b t -> p (b t)"), wo1[:, k, :],
                               start=(k == 0), stop=(k == KT - 1))
            mm.then_inc(sem("out1_mm"), 1)
            pe.wait_ge(sem("bv_wide"), 1)
            linear(bank_b[:, 0:D], lambda k: bv_wide[:, k, :], lambda k: watt[:, 3, k, :],
                   KT).then_inc(sem("bvo_mm"), 1)
            wvo_mm(1)

            turn("lnE", zn, bank_c)
            pe.wait_ge(sem("kept"), nth(KEPT, "lnE"))
            pe.wait_ge(sem("bvo_read"), 1)
            for n in range(2):
                for j in range(KT):
                    mm = linear((bank_b, bank_c)[n][:, j * P:(j + 1) * P],
                                lambda k: watt[:, n, k, j * P:(j + 1) * P], lambda k: zT[:, k, :], KT)
                mm.then_inc(sem("att_qk"), 1)
            pe.wait_ge(sem("wvo_sb"), 1)
            linear(bank_d[:, 0:D], lambda k: zT[:, k, :], lambda k: wvo[:, k, :],
                   KT).then_inc(sem("att_v"), 1)
            pe.wait_ge(sem("att_q_sb"), KT)
            pe.wait_ge(sem("att_k_sb"), KT)
            linear(bank_a[:, 0:P], lambda k: wide[:, k * P:(k + 1) * P],
                   lambda k: wide[:, (2 + k) * P:(3 + k) * P], KT).then_inc(sem("att_s"), 1)
            pe.wait_ge(sem("att_exp"), 1)
            pe.transpose(bank_c[:, 0:P], att_e, ident).then_inc(sem("att_e_turn"), 1)
            pe.wait_ge(sem("att_eT"), 1)
            pe.wait_ge(sem("att_v_sb"), 1)
            pe.matmul(bank_b[:, 0:D], att_eT, att_v, start=True, stop=True).then_inc(sem("att_out"), 1)

            keep_warm(5, oT_flat)
            turn("lnF", zn, bank_a)
            pe.wait_ge(sem("kept"), nth(KEPT, "lnF"))
            loaded(pe, "gw1")
            linear(bank_b[:, 0:E1], lambda k: zT[:, k, :], lambda k: gw1[:, k, :],
                   KT).then_inc(sem("gate_mm"), 1)
            for n in range(E1 + 3):
                if n <= E1:
                    loaded(pe, "wgu0" if n < 8 else "wgu1")
                    if n >= 2:
                        pe.wait_ge(sem("exp_h"), n - 1)
                    for gu in range(2):
                        mm = linear(banks[n % 2][:, gu * P:(gu + 1) * P],
                                    lambda k: wgu[:, n, k, gu * F1:(gu + 1) * F1],
                                    lambda k: zT[:, k, :], KT)
                    mm.then_inc(sem("exp_gu"), 1)
                if n >= 2:
                    m = n - 2
                    if m == 0:
                        loaded(pe, "wdn")
                    pe.wait_ge(sem("exp_h"), m + 1)
                    if m >= 2:
                        pe.wait_ge(sem("exp_sum"), m - 1)
                    pe.matmul(banks[2 + m % 2][:, 0:D], hid[:, m % 2, 1, :], wdn[:, m, :],
                              start=True, stop=True).then_inc(sem("exp_dn"), 1)

        @block.scalar
        def _(act):
            def v_copy(i):
                act.wait_ge(sem("kv_mm0"), i + 1)
                if i >= 2:
                    act.wait_ge(sem("kss"), i - 1)
                if i == 0:
                    act.wait_ge(sem("eps_set"), 1)
                act.activation(ksq[:, i % 2, :, 0:D0], kv_bank(i)[:, 0:D].rearrange("p (h d) -> p h d", h=HK0),
                               ACT.Square, scale=D0 ** -0.5).then_inc(sem("ksq"), 1)
                act.activation(vals[:, i], kv_bank(i)[:, D:2 * D], ACT.Copy).then_inc(sem("v0"), 1)

            def k_hi(m):
                p, half = divmod(m, 2)
                act.wait_ge(sem("k_turn0"), p + 1)
                rows_ = slice(64 * half, 64 * half + 64)
                act.activation(kstack[rows_, half::2, 2 * p * P:(2 * p + 2) * P],
                               turn_bank(p)[rows_, :].rearrange("p (h k) -> p h k", h=2),
                               ACT.Copy).then_inc(sem("khi0"), 1)

            def k1_hi(n):
                ft, keys, bank = k1_piece(n)
                act.wait_ge(sem("k1_mm"), n + 1)
                for half in range(2):
                    rows_ = slice(64 * half, 64 * half + 64)
                    act.activation(kstack[rows_, 2 * ft + half, keys], bank[rows_, :], ACT.Identity,
                                   bias=cols[rows_, COL_AT["bk1"][0] + ft:COL_AT["bk1"][0] + ft + 1]
                                   ).then_inc(sem("khi1"), 1)

            def v1_copy(*tiles):
                for i in tiles:
                    act.wait_ge(sem("v1_mm"), i + 1)
                    if i == 0:
                        act.wait_ge(sem("pv0"), 4)
                    act.activation(vals[:, i, :], banks[2 + i % 2][:, 0:D], ACT.Copy).then_inc(sem("v1"), 1)

            def q_hi(n):
                act.wait_ge(sem("q_turn0"), n + 1)
                if n == 0:
                    act.wait_ge(sem("qk_w"), 1)
                act.activation(qstack[0][:, :, 4 * n:4 * n + 4, :],
                               (bank_c, bank_d)[n % 2].rearrange("p (b h t) -> p b h t", b=B, h=4),
                               ACT.Copy, scale=s_("qk_w")).then_inc(sem("q_hi0"), 1)

            def ctx_hi_part(c):
                loaded(act, f"ctx{c}")
                act.activation(ctx_hi[:, :, c * CHUNK:(c + 1) * CHUNK], ctx_raw[:, c],
                               ACT.Copy).then_inc(sem("ctx_hi"), 1)

            def exp(l, i):
                act.wait_ge(sem(f"nmx{l}"), i + 1)
                if i >= 3:
                    act.wait_ge(sem(f"p_turn{l}"), 2 * (i - 2))
                act.activation(prob[:, i % 3], scores(l, i)[:], ACT.Exp, bias=nmx[:, l, i:i + 1],
                               accum_out=sums[:, l, i:i + 1]).then_inc(sem(f"exp{l}"), 1)

            def pt_even(l, i):
                act.wait_ge(sem(f"p_turn{l}"), 2 * i + 1)
                if l == 0 and i == 4:
                    act.wait_ge(sem("wkv_split1"), 2)
                if i >= 8 and i % 4 == 0:
                    act.wait_ge(sem(f"pv{l}"), i // 4 - 1)
                act.activation(pt[:, (i // 2) % 4, 0:4, (i % 2) * P:(i % 2 + 1) * P],
                               tr_ps[0][:].rearrange("p (k q) -> p k q", k=4),
                               ACT.Copy).then_inc(sem(f"pt_even{l}"), 1)

            def attention(l):
                for i in range(TILES + 2):
                    if i >= 2:
                        pt_even(l, i - 2)
                    if i < TILES:
                        exp(l, i)
                    if l == 1 and i < 2:
                        v1_copy(14 + i)

            loaded(act, "wkv0")
            act.activation(wkv_hi[0][:], wkv_raw[0][:], ACT.Copy).then_inc(sem("wkv_split0"), 1)
            for hf in range(2):
                half_c = slice(hf * CHUNK // 2, (hf + 1) * CHUNK // 2)
                loaded(act, f"ctx0_{hf}")
                act.activation(ctx_hi[:, :, half_c], ctx_raw[:, 0, :, half_c],
                               ACT.Copy).then_inc(sem("ctx_hi"), 1)
            ctx_hi_part(1)
            for i in range(NCTX):
                v_copy(i)
                if i >= 5:
                    k_hi(i - 5)
                if i == 1:
                    ctx_hi_part(2)
                if i == 3:
                    ctx_hi_part(3)
                    act.wait_ge(sem("q0_mm"), 1)
                    act.activation(qsq[:, :, 0:D0], W1_[:].rearrange("p (h d) -> p h d", h=H0), ACT.Square,
                                   scale=D0 ** -0.5).then_inc(sem("q_sq"), 1)
                if i == 7:
                    loaded(act, "wkv1")
                    act.activation(wkv_hi[1][:], wkv_raw[1][:], ACT.Copy).then_inc(sem("wkv_split1"), 1)
                if i == 9:
                    loaded(act, "cols")
                    then(act, act.activation(s_("ea", KT), cols[:, 0:KT], ACT.Exp), "decay")
                    act.activation(s_("decay", KT), s_("ea", KT), ACT.Exp,
                                   scale=-1.0).then_inc(sem("decay"), 1)
                if 12 <= i < 16:
                    q_hi(i - 12)
            for m in range(NCTX - 5, NCTX):
                k_hi(m)

            attention(0)

            v1_copy(0, 1)
            k1_hi(0)
            k1_hi(1)
            v1_copy(2, 3, 4, 5, 6)
            k1_hi(2)
            v1_copy(7)
            for n in range(2):
                act.wait_ge(sem("ff_h"), n + 1)
                act.activation(wide[:, n * D:(n + 1) * D], (bank_b, bank_c)[n][:, 0:D], ACT.Tanh,
                               scale=0.5).then_inc(sem("ff_tanh"), 1)
            k1_hi(3)
            k1_hi(4)
            v1_copy(8)
            act.wait_ge(sem("r_nmax"), 1)
            act.activation(s_("r_exp", E0), s_("r_logit", E0), ACT.Exp, bias=s_("r_nmax"),
                           accum_out=s_("r_sum")).then_inc(sem("r_exp"), 1)
            for e in range(E0):
                act.wait_ge(sem("moe_h"), e // 4 + 1)
                act.activation(wide[:, e * P:(e + 1) * P],
                               (bank_c, bank_d)[e // 4][:, (e % 4) * P:(e % 4 + 1) * P],
                               ACT.Gelu, bias=col("b1", e)).then_inc(sem("moe_act"), 1)
            k1_hi(5)
            v1_copy(9, 10)
            k1_hi(6)
            v1_copy(11, 12)
            act.activation(s_("ea", KT), s_("decay", KT), ACT.Exp).then_inc(sem("exp_table"), 1)
            act.wait_ge(sem("q1_sb"), 1)
            for x in range(GRP1):
                act.activation(q1_stack(0, x), q1_sb, ACT.Copy,
                               scale=const("headmask")[:, x:x + 1]).then_inc(sem("q1_hi"), 1)
            v1_copy(13)
            k1_hi(7)

            attention(1)

            act.wait_ge(sem("wvo_mm"), 2)
            act.activation(wvo[:].rearrange("p k n -> p (k n)"), bank_d, ACT.Copy).then_inc(sem("wvo_sb"), 1)
            act.wait_ge(sem("att_qk"), 1)
            for j in range(KT):
                act.activation(wide[:, j * P:(j + 1) * P], bank_b[:, j * P:(j + 1) * P], ACT.Identity,
                               bias=col("abq", j)).then_inc(sem("att_q_sb"), 1)
            act.wait_ge(sem("att_v"), 1)
            act.activation(att_v, bank_d[:, 0:D], ACT.Copy).then_inc(sem("att_v_sb"), 1)
            act.wait_ge(sem("att_s"), 1)
            for n, (func, scale) in enumerate(((ACT.Relu, 1.0), (ACT.Tanh, 0.5), (ACT.Tanh, 1.0))):
                act.activation(att_parts[:, n, :], bank_a[:, 0:P], func,
                               scale=scale).then_inc(sem("att_parts"), 1)
            act.wait_ge(sem("att_nmax"), 1)
            act.activation(att_e, att_theta, ACT.Exp, bias=s_("att_nmax"),
                           accum_out=s_("att_sum")).then_inc(sem("att_exp"), 1)
            act.wait_ge(sem("g_logit"), 1)
            act.activation(s_("g_tanh", E1), s_("g_logit", E1), ACT.Tanh, scale=0.5).then_inc(sem("g_tanh"), 1)
            for n in range(E1 + 1):
                act.wait_ge(sem("exp_gu"), n + 1)
                if n >= 2:
                    act.wait_ge(sem("exp_h"), n - 1)
                act.activation(hid[:, n % 2, 0, :], banks[n % 2][:, 0:P], ACT.Tanh,
                               scale=0.5).then_inc(sem("exp_tanh"), 1)

        @block.vector
        def _(dve):
            count = [0]

            def link(ins):
                count[0] += 1
                ins.then_inc(sem("dve_link"), 1)
                dve.wait_ge(sem("dve_link"), count[0])

            def layer_norm(name, src, meanwhile=None):
                link(dve.bn_stats(s_("bn", 6), src))
                link(dve.bn_aggr(s_(name + "_mv", 2), s_("bn", 6)))
                dve.tensor_scalar(s_(name + "_ve"), s_(name + "_mv", 2)[:, 1:2], LN_EPS, None,
                                  ALU.add).then_inc(sem("var"), 1)
                if meanwhile is not None:
                    meanwhile()
                dve.wait_ge(sem("root"), nth(ROOTS, name))
                ins = dve.tensor_scalar(zn[:], src, s_(name + "_mv", 2)[:, 0:1], s_(name + "_rs"),
                                        ALU.subtract, ALU.mult)
                if name == "lnB":
                    link(ins)
                else:
                    then(dve, ins, "turn_in", nth(TURNS, name))

            def rms(name, src, out, weight, meanwhile=None):
                dve.tensor_tensor_reduce(scratch[:], src, src, 1.0 / D, RMS_EPS, ALU.mult, ALU.add,
                                         s_(name + "_ve")).then_inc(sem("var"), 1)
                if meanwhile is not None:
                    meanwhile()
                dve.wait_ge(sem("root"), nth(ROOTS, name))
                return dve.scalar_tensor_tensor(out, src, s_(name + "_rs"), weight, ALU.mult, ALU.mult)

            def keep_turned(name, ps):
                dve.wait_ge(sem("turned"), nth(TURNS, name))
                dve.tensor_copy(zT[:].rearrange("p k n -> p (k n)"), ps[:, 0:2 * P]
                                ).then_inc(sem("kept"), 1)

            def low(lo, src, hi, name):
                dve.tensor_tensor(lo, src, hi.bitcast(F32), ALU.subtract).then_inc(sem(name), 1)

            def key_squares(i):
                dve.wait_ge(sem("ksq"), i + 1)
                if i >= 2:
                    dve.wait_ge(sem("krs"), i - 1)
                dve.tensor_reduce(kss[:, i % 2], ksq[:, i % 2], AX.X, ALU.add).then_inc(sem("kss"), 1)

            def key_scale(i):
                dve.wait_ge(sem("krs"), i + 1)
                dve.wait_ge(sem("v0"), i + 1)
                if i >= 4:
                    dve.wait_ge(sem("k_turn0"), (i - 2) // 2)
                dve.tensor_tensor(kn[:, i % 4].rearrange("p (h d) -> p h d", h=4),
                                  kv_bank(i)[:, 0:D].rearrange("p (h d) -> p h d", h=4),
                                  krs[:, i % 2].unsqueeze(2).to_broadcast([P, 4, D0]),
                                  ALU.mult).then_inc(sem("kn0"), 1)

            def k_lo(m):
                p, half = divmod(m, 2)
                dve.wait_ge(sem("khi0"), 2 * p + 2)
                rows_, other = slice(64 * half, 64 * half + 64), slice(64 - 64 * half, 128 - 64 * half)
                keys = slice(2 * p * P, (2 * p + 2) * P)
                dve.tensor_tensor(kstack[other, half::2, keys],
                                  turn_bank(p)[rows_, :].rearrange("p (h k) -> p h k", h=2),
                                  kstack[rows_, half::2, keys].bitcast(F32),
                                  ALU.subtract).then_inc(sem("klo0"), 1)

            def q_lo(n):
                dve.wait_ge(sem("q_hi0"), n + 1)
                out = qstack[1][:, :, 4 * n:4 * n + 4, :].rearrange("p b h t -> p b (h t)")
                dve.scalar_tensor_tensor(out, (bank_c, bank_d)[n % 2].rearrange("p (b n) -> p b n", b=B),
                                         s_("qk_w"),
                                         qstack[0][:, :, 4 * n:4 * n + 4, :].bitcast(F32).rearrange(
                                             "p b h t -> p b (h t)"),
                                         ALU.mult, ALU.subtract).then_inc(sem("q_lo0"), 1)

            def k1_lo(n):
                n, half = divmod(n, 2)
                ft, keys, bank = k1_piece(n)
                dve.wait_ge(sem("khi1"), 2 * n + 1 + half)
                if half == 0:
                    dve.wait_ge(sem("khi1"), 2 * n + 2)
                rows_, other = slice(64 * half, 64 * half + 64), slice(64 - 64 * half, 128 - 64 * half)
                dve.scalar_tensor_tensor(kstack[other, 2 * ft + half, keys], bank[rows_, :],
                                         cols[rows_, COL_AT["bk1"][0] + ft:COL_AT["bk1"][0] + ft + 1],
                                         kstack[rows_, 2 * ft + half, keys].bitcast(F32),
                                         ALU.add, ALU.subtract).then_inc(sem("klo1"), 1)

            def row_max(l, i):
                dve.wait_ge(sem(f"score{l}"), i + 1)
                dve.tensor_reduce(nmx[:, l, i:i + 1], scores(l, i)[:], AX.X, ALU.max,
                                  negate=True).then_inc(sem(f"nmx{l}"), 1)

            def inv_sum(l, g):
                dve.wait_ge(sem(f"exp{l}"), 4 * g + 4)
                if g >= 1:
                    dve.wait_ge(sem(f"inv_spread{l}"), g)
                link(dve.reciprocal(rsum[:], sums[:, l, 4 * g:4 * g + 4]))
                if l == 0:
                    ins = dve.tensor_copy(acc[:].rearrange("p (j d) -> p j d", j=4),
                                          rsum[:].unsqueeze(2).to_broadcast([P, 4, D0]))
                else:
                    ins = dve.tensor_tensor(acc[:, 0:P].rearrange("p (j d) -> p j d", j=4),
                                            rsum[:].unsqueeze(2).to_broadcast([P, 4, 2 * D1]),
                                            const("pairmask").unsqueeze(1).to_broadcast([P, 4, 2 * D1]),
                                            ALU.mult)
                ins.then_inc(sem(f"inv_sum{l}"), 1)

            def pt_odd(l, i):
                dve.wait_ge(sem(f"p_turn{l}"), 2 * i + 2)
                if l == 0 and i == 4:
                    dve.wait_ge(sem("wkv_split1"), 2)
                if i >= 8 and i % 4 == 0:
                    dve.wait_ge(sem(f"pv{l}"), i // 4 - 1)
                dve.tensor_copy(pt[:, (i // 2) % 4, 4:8, (i % 2) * P:(i % 2 + 1) * P],
                                tr_ps[1][:].rearrange("p (k q) -> p k q", k=4)
                                ).then_inc(sem(f"pt_odd{l}"), 1)

            def inv_read(l, g):
                dve.wait_ge(sem("inv_spread%d" % l if g == 3 else "pv%d" % l), g + 1)
                if g >= 1:
                    dve.wait_ge(sem(f"pv_read{l}"), g)
                n = (D, P)[l]
                then(dve, dve.tensor_copy(inv_all[:, 0:n], inv_bank(g)[:, 0:n]), "inv_all", 4 * l + g + 1)

            def pv_read(l, g):
                if g != 3:
                    inv_read(l, g)
                dve.wait_ge(sem(f"pv{l}"), g + 1)
                b, hf = divmod(g, 2)
                if l == 0:
                    dve.tensor_tensor(oT[:, 4 * hf:4 * hf + 4, b, :],
                                      pv_ps[g % 2][:, 0:256].rearrange("p (g t) -> p g t", g=4),
                                      inv_all[:].rearrange("p (g t) -> p g t", g=4),
                                      ALU.mult).then_inc(sem("pv_read0"), 1)
                else:
                    link(dve.tensor_tensor(scratch[:, 0:P], pv_ps[g % 2][:, 0:P], inv_all[:, 0:P], ALU.mult))
                    then(dve, dve.scalar_tensor_tensor(oT[:, hf, b, :], scratch[:, 0:T], col("bv1", hf),
                                                       scratch[:, T:2 * T], ALU.add, ALU.add),
                         "pv_read1", g + 1)

            def attention(l):
                for i in range(TILES + 7):
                    if i < TILES and (l == 1 or i >= 2):
                        row_max(l, i)
                    if l == 1 and i == 1:
                        k1_lo(14)
                        k1_lo(15)
                        dve.tensor_tensor(x_bias[:], xs[:], row("bo1"), ALU.add).then_inc(sem("x_bias0"), 1)
                    if 2 <= i < TILES + 2:
                        pt_odd(l, i - 2)
                    if i >= 5 and i % 4 == 1 and i < TILES + 4:
                        inv_sum(l, (i - 5) // 4)
                    if i >= 10 and i % 4 == 2:
                        pv_read(l, (i - 10) // 4)
                    if i == TILES + 3:
                        inv_read(l, 3)

            def route(name, values, n, factor, meanwhile=None):
                top, idx, w = s_(name + "_top", 8), s_(name + "_idx", 8), s_(name + "_w", 2)
                link(dve.max(top, values))
                link(dve.max_index(idx.bitcast(U32), top, values))
                link(dve.tensor_copy(s_(name + "_at", 2), idx[:, 0:2].bitcast(U32)))
                link(dve.tensor_tensor(s_(name + "_s"), top[:, 0:1], top[:, 1:2], ALU.add))
                link(dve.reciprocal(s_(name + "_r"), s_(name + "_s")))
                if meanwhile is not None:
                    meanwhile()
                link(dve.tensor_scalar(w, top[:, 0:2], s_(name + "_r"), factor, ALU.mult, ALU.mult))
                at = s_(name + "_at", 2)
                link(dve.tensor_scalar(s_(name + "_a", n), const("iota")[:, 0:n], at[:, 0:1], w[:, 0:1],
                                       ALU.is_equal, ALU.mult))
                link(dve.tensor_scalar(s_(name + "_b", n), const("iota")[:, 0:n], at[:, 1:2], w[:, 1:2],
                                       ALU.is_equal, ALU.mult))
                then(dve, dve.tensor_tensor(s_(name, n), s_(name + "_a", n), s_(name + "_b", n), ALU.add), name)

            def ctx_lo_chunk(c):
                n = CHUNK // 2 if c == 0 else CHUNK
                dve.wait_ge(sem("ctx_hi"), 1 if c == 0 else c + 2)
                sl = slice(c * CHUNK, c * CHUNK + n)
                low(ctx_lo[:, :, sl], ctx_raw[:, c, :, 0:n], ctx_hi[:, :, sl], "ctx_lo_dve")

            loaded(dve, "x")
            layer_norm("lnA", xs[:])
            dve.wait_ge(sem("wkv_split0"), 1)
            low(wkv_lo[0][:], wkv_raw[0][:], wkv_hi[0][:], "wkv_split0")
            ctx_lo_chunk(0)
            keep_turned("lnA", bank_a)
            ctx_lo_chunk(1)
            for i in range(NCTX + 6):
                if 2 <= i < NCTX + 2:
                    key_scale(i - 2)
                if i < NCTX:
                    key_squares(i)
                if i == 1:
                    ctx_lo_chunk(2)
                if i == 4:
                    dve.wait_ge(sem("q_sq"), 1)
                    dve.tensor_reduce(s_("q0_ve", 16), qsq, AX.X, ALU.add).then_inc(sem("q_var"), 1)
                if i == 6:
                    loaded(dve, "cols")
                    dve.tensor_tensor(s_("qk_w"), col("qnw", 0), col("knw", 0), ALU.mult).then_inc(sem("qk_w"), 1)
                if 8 <= i < 12:
                    n = i - 8
                    hs = slice(4 * n, 4 * n + 4)
                    dve.wait_ge(sem("q_root"), n + 1)
                    dve.tensor_tensor(q_twice[:, hs],
                                      W1_[:, 256 * n:256 * (n + 1)].rearrange(
                                          "p (h d) -> p h d", h=4).unsqueeze(2).to_broadcast([P, 4, 2, D0]),
                                      s_("q0_rs", 16)[:, hs].unsqueeze(2).unsqueeze(3).to_broadcast(
                                          [P, 4, 2, D0]), ALU.mult).then_inc(sem("q_ready"), 1)
                if i in (NCTX + 2, NCTX + 4):
                    row_max(0, (i - NCTX - 2) // 2)
                if 13 <= i < 17:
                    q_lo(i - 13)
                if i >= 6:
                    k_lo(i - 6)

            attention(0)

            dve.wait_ge(sem("decay"), 2)
            link(dve.tensor_copy(decays[:].rearrange("p k b t -> p k (b t)"),
                                 s_("decay", KT).unsqueeze(2).to_broadcast([P, KT, B * T])))
            dve.memset(decays[:].rearrange("p k b t -> p (k b) t")[:, :, 0:1], 0.0).then_inc(sem("decays"), 1)
            dve.tensor_copy(bv_wide[:], col("abv", 0, KT).unsqueeze(2).to_broadcast([P, KT, P])
                            ).then_inc(sem("bv_wide"), 1)
            dve.wait_ge(sem("out0_mm"), 1)
            link(dve.tensor_tensor(xs[:], xs[:], bank_a[:, 0:D], ALU.add))
            layer_norm("lnB", xs[:])
            rms("rmB", zn[:], normed, row("inw")).then_inc(sem("turn_in"), 1)
            k1_lo(0)
            dve.wait_ge(sem("turned"), nth(TURNS, "normed"))
            dve.wait_ge(sem("decays"), 1)
            dve.tensor_tensor_scan(scan[:], decays[:].rearrange("p k b t -> p (k b t)"), bank_c[:, 0:D],
                                   0.0, ALU.mult, ALU.add).then_inc(sem("scan"), 1)
            for k in range(KT):
                ks = slice(k * P, (k + 1) * P)
                dve.tensor_scalar(skip[:, ks], bank_c[:, ks], col("dskip", k), None,
                                  ALU.mult).then_inc(sem("skip"), 1)
            dve.wait_ge(sem("scan"), 1)
            dve.wait_ge(sem("skip"), 2)
            for k in range(KT):
                ks = slice(k * P, (k + 1) * P)
                ins = dve.scalar_tensor_tensor(scan_out[:, ks], scan[:, ks], col("cout", k), skip[:, ks],
                                               ALU.mult, ALU.add)
            ins.then_inc(sem("turn_in"), 1)
            k1_lo(1)
            dve.wait_ge(sem("turned"), nth(TURNS, "scan_out"))
            link(dve.tensor_tensor(x1[:], zn[:], bank_a[:, 0:D], ALU.add))
            rms("rmC", x1[:], normed, row("ffw"), lambda: k1_lo(2)).then_inc(sem("turn_in"), 1)
            k1_lo(3)
            keep_turned("n2", bank_a)
            link(dve.tensor_tensor(acc[:], xs[:], x1[:], ALU.add))
            k1_lo(4)
            for n in range(2):
                dve.wait_ge(sem("ff_tanh"), n + 1)
                dve.scalar_tensor_tensor(wide[:, n * D:(n + 1) * D], wide[:, n * D:(n + 1) * D], 1.0,
                                         (bank_b, bank_c)[n][:, 0:D], ALU.add,
                                         ALU.mult).then_inc(sem("ff_act"), 1)
            k1_lo(5)
            dve.wait_ge(sem("ff_out"), 1)
            link(dve.scalar_tensor_tensor(xs[:], bank_d[:, 0:D], 0.5, acc[:], ALU.mult, ALU.add))
            layer_norm("lnC", xs[:])
            k1_lo(6)
            keep_turned("lnC", bank_a)
            dve.wait_ge(sem("router_mm"), 1)
            link(dve.tensor_tensor(s_("r_logit", E0), bank_b[:, 0:E0], row("rb"), ALU.add))
            link(dve.max(s_("r_top", 8), s_("r_logit", E0)))
            dve.tensor_scalar(s_("r_nmax"), s_("r_top", 8)[:, 0:1], -1.0, None,
                              ALU.mult).then_inc(sem("r_nmax"), 1)
            k1_lo(7)
            dve.wait_ge(sem("r_exp"), 1)
            link(dve.reciprocal(s_("r_rsum"), s_("r_sum")))
            link(dve.tensor_scalar(s_("r_p", E0), s_("r_exp", E0), s_("r_rsum"), None, ALU.mult))
            route("route0", s_("r_p", E0), E0, 1.0)
            k1_lo(8)
            dve.wait_ge(sem("route_turn"), 1)
            dve.tensor_copy(routeT[0:E0, :], bank_b[0:E0, 0:P]).then_inc(sem("routeT"), 1)
            k1_lo(9)
            dve.wait_ge(sem("moe_b2"), 1)
            dve.tensor_tensor(acc[:], xs[:], bank_b[:, D:2 * D], ALU.add).then_inc(sem("moe_acc"), 1)
            r0 = s_("route0", E0)
            for n in range(E0 // 2):
                dve.wait_ge(sem("moe_out"), n + 1)
                dve.wait_ge(sem("moe_acc"), 2 * n + 1)
                dve.scalar_tensor_tensor(acc[:], moe_bank(n)[:, 0:D], r0[:, 2 * n:2 * n + 1], acc[:],
                                         ALU.mult, ALU.add).then_inc(sem("moe_acc"), 1)
                out, w = moe_bank(n)[:, D:2 * D], r0[:, 2 * n + 1:2 * n + 2]
                if n == 0:
                    ins = dve.tensor_scalar(scratch[:], out, w, None, ALU.mult)
                else:
                    ins = dve.scalar_tensor_tensor(scratch[:], out, w, scratch[:], ALU.mult, ALU.add)
                ins.then_inc(sem("moe_acc"), 1)
            dve.wait_ge(sem("moe_acc"), E0 + 1)
            link(dve.tensor_tensor(xs[:], acc[:], scratch[:], ALU.add))
            layer_norm("lnD", xs[:], lambda: k1_lo(10))
            k1_lo(11)
            keep_turned("lnD", bank_a)
            k1_lo(12)
            k1_lo(13)
            dve.wait_ge(sem("q1_mm"), 1)
            dve.tensor_tensor(wide[:, 0:512].rearrange("p (b g t) -> p g b t", g=4, b=B),
                              bank_b.rearrange("p (g b t) -> p g b t", g=4, b=B),
                              col("bq1", 0, 4).unsqueeze(2).unsqueeze(3).to_broadcast([P, 4, B, T]),
                              ALU.add).then_inc(sem("q1_sb"), 1)
            for x in range(GRP1):
                dve.wait_ge(sem("q1_hi"), x + 1)
                dve.scalar_tensor_tensor(q1_stack(1, x), q1_sb, const("headmask")[:, x:x + 1],
                                         q1_stack(0, x).bitcast(F32), ALU.mult,
                                         ALU.subtract).then_inc(sem("q1_lo"), 1)

            attention(1)

            dve.wait_ge(sem("x_bias0"), 1)
            dve.wait_ge(sem("out1_mm"), 1)
            link(dve.tensor_tensor(xs[:], x_bias[:], bank_a[:, 0:D], ALU.add))
            layer_norm("lnE", xs[:], lambda: (
                dve.wait_ge(sem("bvo_mm"), 1),
                dve.tensor_tensor(acc[:], bank_b[:, 0:D], row("abo"), ALU.add).then_inc(sem("bvo_read"), 1)))
            keep_turned("lnE", bank_c)
            dve.wait_ge(sem("bvo_read"), 1)
            dve.tensor_tensor(x_bias[:], acc[:], xs[:], ALU.add).then_inc(sem("x_bias"), 1)
            dve.wait_ge(sem("att_qk"), 2)
            for j in range(KT):
                dve.tensor_scalar(wide[:, (KT + j) * P:(KT + j + 1) * P], bank_c[:, j * P:(j + 1) * P],
                                  col("abk", j), None, ALU.add).then_inc(sem("att_k_sb"), 1)
            for n, w in enumerate((0.1, 0.1, 0.15)):
                dve.wait_ge(sem("att_parts"), n + 1)
                link(dve.scalar_tensor_tensor(att_theta, att_parts[:, n, :], w,
                                              const("theta0") if n == 0 else att_theta, ALU.mult, ALU.add))
            dve.tensor_reduce(s_("att_nmax"), att_theta, AX.X, ALU.max,
                              negate=True).then_inc(sem("att_nmax"), 1)
            dve.wait_ge(sem("att_e_turn"), 1)
            dve.tensor_copy(att_eT, bank_c[:, 0:P]).then_inc(sem("att_eT"), 1)
            link(dve.reciprocal(s_("att_rsum"), s_("att_sum")))
            dve.wait_ge(sem("x_bias"), 1)
            dve.wait_ge(sem("att_out"), 1)
            link(dve.scalar_tensor_tensor(xs[:], bank_b[:, 0:D], s_("att_rsum"), x_bias[:],
                                          ALU.mult, ALU.add))
            layer_norm("lnF", xs[:])
            keep_turned("lnF", bank_a)
            link(dve.tensor_tensor(acc[:], xs[:], zn[:], ALU.add))
            dve.wait_ge(sem("gate_mm"), 1)
            dve.tensor_tensor(s_("g_logit", E1), bank_b[:, 0:E1], row("gb"), ALU.add).then_inc(sem("g_logit"), 1)
            dve.wait_ge(sem("g_tanh"), 1)
            link(dve.tensor_scalar(s_("g_sig", E1), s_("g_tanh", E1), 1.0, 0.5, ALU.add, ALU.mult))

            def hidden(n):
                dve.wait_ge(sem("exp_tanh"), n + 1)
                link(dve.scalar_tensor_tensor(hid[:, n % 2, 0, :], hid[:, n % 2, 0, :], 1.0,
                                              banks[n % 2][:, 0:P], ALU.add, ALU.mult))
                if n >= 2:
                    dve.wait_ge(sem("exp_dn"), n - 1)
                dve.tensor_tensor(hid[:, n % 2, 1, :], hid[:, n % 2, 0, :], banks[n % 2][:, P:2 * P],
                                  ALU.mult).then_inc(sem("exp_h"), 1)

            route("route1", s_("g_sig", E1), E1, 0.5, lambda: hidden(0))
            r1 = s_("route1", E1)
            for n in range(1, E1 + 3):
                if n <= E1:
                    hidden(n)
                if n >= 2:
                    m = n - 2
                    dve.wait_ge(sem("exp_dn"), m + 1)
                    w = 0.5 if m == 0 else r1[:, m - 1:m]
                    then(dve, dve.scalar_tensor_tensor((xs if m == E1 else acc)[:], banks[2 + m % 2][:, 0:D],
                                                       w, acc[:], ALU.mult, ALU.add), "exp_sum", m + 1)


def kernel(**inputs):
    import concourse.bacc as _bacc
    from concourse.bass_utils import run_bass_kernel_spmd as _run

    a = {k: np.asarray(v) for k, v in inputs.items()}

    def by_rows(w):
        return w.reshape(-1, P, w.shape[-1]).transpose(1, 0, 2)

    L0, L1, A = "L0_xattn_", "L1_xattn_", "L1_attn_"
    ctxT = a["ctx_1024"].reshape(B * S, D).T.reshape(KT, P, 4, CHUNK).transpose(2, 1, 0, 3)
    wo0 = a[L0 + "wo"].T.reshape(2, 2, G0, D0, D).transpose(0, 2, 1, 3, 4).reshape(H0 * D0, D)
    eye = np.eye(P, dtype=np.float32)
    p = np.arange(P)
    consts = {
        "ident": eye,
        "headmask": (((p % 64) // D1)[:, None] == np.arange(GRP1)[None, :]) / 4.0,
        "pairmask": (p // T)[:, None] == (np.arange(2 * D1) // D1)[None, :],
        "theta0": np.where((p // T)[:, None] == (p // T)[None, :], 0.6, FAR),
        "iota": np.tile(np.arange(E1), (P, 1)),
    }
    f = "L1_ffn_"
    gu = np.concatenate([np.concatenate([a[f + "shared_wg"][None], a[f + "experts_wg"]]),
                         np.concatenate([a[f + "shared_wu"][None], a[f + "experts_wu"]])], axis=2)
    rows = {"inw": a["L0_attn_input_norm_w"],
            "ffw": a["L0_attn_ff_norm_w"], "rb": a["L0_ffn_router_b"],
            "bo1": a[L1 + "bo"], "abo": a[A + "bo"], "gb": a[f + "gate_b"]}
    on_p = lambda v: v.reshape(-1, P).T
    cols = {"alog": on_p(a["L0_attn_a_log"]), "cout": on_p(a["L0_attn_c_out"]),
            "dskip": on_p(a["L0_attn_d_skip"]), "b1": a["L0_ffn_b1"].T, "abq": on_p(a[A + "bq"]),
            "abk": on_p(a[A + "bk"]), "abv": on_p(a[A + "bv"]),
            "bk1": on_p(a[L1 + "bk"]), "bv1": on_p(a[L1 + "bv"]),
            "bq1": np.tile(a[L1 + "bq"].reshape(-1, 64).T, (2, 1)),
            "qnw": np.tile(a[L0 + "q_norm_w"], 2)[:, None], "knw": np.tile(a[L0 + "k_norm_w"], 2)[:, None]}
    arrays = {
        "x": a["x"].reshape(B * T, D),
        "ctxT": ctxT,
        "wkv0": by_rows(np.concatenate([a[L0 + "wk"], a[L0 + "wv"]]).T),
        "wkv1": by_rows(np.concatenate([a[L1 + "Wk"], a[L1 + "Wv"]]).T),
        "wq0": by_rows(a[L0 + "wq"].T),
        "wo0": by_rows(wo0),
        "fc": by_rows(a["L0_attn_ff_fc_w"].T),
        "proj": by_rows(a["L0_attn_ff_proj_w"].T),
        "rw0": by_rows(a["L0_ffn_router_w"]),
        "w1": by_rows(a["L0_ffn_W1"].transpose(1, 0, 2).reshape(D, E0 * F0)),
        "w2": a["L0_ffn_W2"].transpose(1, 0, 2),
        "b2": a["L0_ffn_b2"],
        "wq1": by_rows(np.tile(a[L1 + "Wq"].T.reshape(D, 4, 1, 64), (1, 1, 2, 1)).reshape(D, 2 * D)),
        "wo1": by_rows(a[L1 + "Wo"].T),
        "watt": np.stack([by_rows(w) for w in (a[A + "Wq"].T, a[A + "Wk"].T, a[A + "Wv"], a[A + "Wo"].T)],
                         axis=1),
        "gw1": by_rows(a[f + "gate_w"]),
        "wgu": gu.reshape(E1 + 1, KT, P, 2 * F1).transpose(2, 0, 1, 3),
        "wdn": np.concatenate([a[f + "shared_wd"][None], a[f + "experts_wd"]]).transpose(1, 0, 2),
        "rows": np.concatenate([rows[n] for n, _ in ROWS]),
        "cols": np.concatenate([cols[n] for n, _ in COLS], axis=1),
        "consts": np.concatenate([consts[n].astype(np.float32) for n, _ in CONSTS], axis=1),
    }
    nc = _bacc.Bacc("TRN2", target_bir_lowering=False, num_devices=1)
    fed, t = {}, {}
    for name, v in arrays.items():
        fed["in_" + name] = np.ascontiguousarray(v)
        t[name] = nc.dram_tensor("in_" + name, fed["in_" + name].shape, F32, kind="ExternalInput").ap()
    t["out"] = nc.dram_tensor("out", (B * T, D), F32, kind="ExternalOutput").ap()
    build(nc, t)
    r = _run(nc, [fed], core_ids=[0])
    return r.results[0]["out"].reshape(B, T, D)
```
